# Optimizing a Trainium2 kernel written in Bass

```python
import numpy as np
import jax
import jax.numpy as jnp

def _softmax(x, axis=-1):
    return jax.nn.softmax(x, axis=axis)

def _gelu(x):
    return jax.nn.gelu(x, approximate=True)

def _silu(x):
    return jax.nn.silu(x)

def _sigmoid(x):
    return jax.nn.sigmoid(x)

def _layernorm(x, axis=-1, eps=1e-05):
    m = jnp.mean(x, axis=axis, keepdims=True)
    v = jnp.var(x, axis=axis, keepdims=True)
    return (x - m) / jnp.sqrt(v + eps)

def _scatter_add(tgt, idx, src, axis=0):
    return tgt.at[idx].add(src)

def _segment_sum(src, seg, n):
    return jax.ops.segment_sum(src, seg, n)
kernel_name = 'mk_xattn_ffn_d4_seqx_r4_6cd65e'

def setup_inputs(seed: int=0):
    np.random.seed(seed)
    _w = jnp.asarray

    def _rec_inputs():
        import jax
        import jax.numpy as jnp
        _rk = jax.random.key(seed)
        x = 7.22e-05 + 1 * jax.random.normal(jax.random.fold_in(_rk, 1), (8, 100, 256), jnp.float32)
        _lenS = 100 - jax.random.randint(jax.random.fold_in(_rk, 7), (8,), 0, max(1, 100 // 4) + 1, jnp.int32)
        _lenS2 = 361 - jax.random.randint(jax.random.fold_in(_rk, 8), (8,), 0, max(1, 361 // 4) + 1, jnp.int32)
        _ctx_1024P = jax.random.normal(jax.random.fold_in(_rk, 11), (8, 16, 256), jnp.float32)
        _ctx_1024c = jax.random.dirichlet(jax.random.fold_in(_rk, 511), 0.3 * jnp.ones((16,), jnp.float32), (8, 361))
        _ctx_1024t = jnp.einsum('bsk,bkd->bsd', _ctx_1024c, _ctx_1024P)
        _ctx_1024t = _ctx_1024t * jax.lax.rsqrt(jnp.mean(jnp.square(_ctx_1024t)) + 1e-12) * 0.953939
        ctx_1024 = -0.000514642 + 1.00011 * (_ctx_1024t + 0.3 * jax.random.normal(jax.random.fold_in(_rk, 611), (8, 361, 256), jnp.float32))
        _validS = jnp.arange(100)[None, :] < _lenS[:, None]
        _validS2 = jnp.arange(361)[None, :] < _lenS2[:, None]
        _causal = jnp.tril(jnp.ones((100, 100), dtype=bool))
        mask_Bx1xSxS2_ik1 = jnp.where(jnp.broadcast_to(_validS2[:, None, None, :], (8, 1, 100, 361)), 1, 0).astype(jnp.int32)
        return (x, ctx_1024, mask_Bx1xSxS2_ik1)
    x, ctx_1024, mask_Bx1xSxS2_ik1 = _rec_inputs()

    def _L0_xattn_setup():
        import jax, jax.numpy as jnp
        import numpy as np
        B, L_ENC, L_DEC, D = (16, 128, 128, 256)
        key = jax.random.key(seed)
        k1, k2, k3, k4, k5, k6 = jax.random.split(key, 6)
        encoder_hc = jax.random.normal(k1, (B, L_ENC, D), dtype=jnp.float32)
        decoder_hq = jax.random.normal(k2, (B, L_DEC, D), dtype=jnp.float32)
        w_sim = jax.random.normal(k3, (3 * D,), dtype=jnp.float32) * 0.02
        b_sim = jax.random.normal(k4, (1,), dtype=jnp.float32) * 0.02
        W_qv = jax.random.normal(k5, (4 * D, D), dtype=jnp.float32) * 0.02
        b_qv = jax.random.normal(k6, (D,), dtype=jnp.float32) * 0.02
        return {'encoder_hc': encoder_hc, 'decoder_hq': decoder_hq, 'w_sim': w_sim, 'b_sim': b_sim, 'W_qv': W_qv, 'b_qv': b_qv}
    _L0_xattn_all = _L0_xattn_setup()
    _L0_xattn_in = {k: v for k, v in _L0_xattn_all.items() if k in ('w_sim', 'b_sim', 'W_qv', 'b_qv')}
    del _L0_xattn_all

    def _L0_ffn_setup():
        import jax, jax.numpy as jnp
        import numpy as np
        B, S, D_IN, D_OUT, E, GATE_K, TOP_K = (4, 2048, 256, 256, 8, 64, 2)

        def _gate(x, Vg):
            T = x.shape[0]
            xe = jnp.einsum('ti,eir->ter', x, Vg)
            proj = jnp.einsum('ter,eir->tei', xe, Vg)
            residuals = jnp.linalg.norm(x[:, None, :] - proj, axis=-1)
            rw = jax.nn.softmax(-residuals, axis=1)
            thr = 1.0 / E
            mask = rw > thr
            rows = jnp.arange(T)[:, None]
            top1_idx = jnp.argmax(rw, axis=1, keepdims=True)
            top1_mask = jnp.zeros_like(mask).at[rows, top1_idx].set(True)
            mask = jnp.where(jnp.any(mask), mask, top1_mask)
            if TOP_K < E:
                _, topi = jax.lax.top_k(rw, TOP_K)
                topk_mask = jnp.zeros_like(mask).at[rows, topi].set(True)
                mask = mask & topk_mask
            fw = rw * mask.astype(rw.dtype)
            sw = fw.sum(axis=1, keepdims=True)
            sw = jnp.where(sw == 0, jnp.ones_like(sw), sw)
            return fw / sw
        key = jax.random.key(seed)
        ks = jax.random.split(key, 6)
        return {'hidden_states': jax.random.normal(ks[0], (B, S, D_IN), dtype=jnp.float32), 'Wp': jax.random.normal(ks[1], (D_OUT, D_IN), dtype=jnp.float32) * 0.02, 'bp': jax.random.normal(ks[2], (D_OUT,), dtype=jnp.float32) * 0.02, 'We': jax.random.normal(ks[3], (E, D_OUT, D_IN), dtype=jnp.float32) * 0.02, 'be': jax.random.normal(ks[4], (E, D_OUT), dtype=jnp.float32) * 0.02, 'Vg': jax.random.normal(ks[5], (E, D_IN, GATE_K), dtype=jnp.float32) * 0.05}
    _L0_ffn_all = _L0_ffn_setup()
    _L0_ffn_in = {k: v for k, v in _L0_ffn_all.items() if k in ('Wp', 'bp', 'We', 'be', 'Vg')}
    del _L0_ffn_all

    def _L1_xattn_setup():
        import jax, jax.numpy as jnp
        import numpy as np
        N_HEAD, MODEL_DIM, KEY_DIM, VALUE_DIM = (16, 256, 64, 64)
        B, S = (4, 512)
        EPS = 1e-05
        TEMP = float(np.sqrt(KEY_DIM))
        key = jax.random.key(seed)
        ks = jax.random.split(key, 12)
        d = {'query': jax.random.normal(ks[0], (B, S, MODEL_DIM), jnp.float32), 'key': jax.random.normal(ks[1], (B, S, MODEL_DIM), jnp.float32), 'value': jax.random.normal(ks[2], (B, S, MODEL_DIM), jnp.float32), 'Wq': jax.random.normal(ks[3], (MODEL_DIM, N_HEAD * KEY_DIM), jnp.float32) * np.sqrt(2.0 / (MODEL_DIM + KEY_DIM)), 'bq': jnp.zeros((N_HEAD * KEY_DIM,), jnp.float32), 'Wk': jax.random.normal(ks[4], (MODEL_DIM, N_HEAD * KEY_DIM), jnp.float32) * np.sqrt(2.0 / (MODEL_DIM + KEY_DIM)), 'bk': jnp.zeros((N_HEAD * KEY_DIM,), jnp.float32), 'Wv': jax.random.normal(ks[5], (MODEL_DIM, N_HEAD * VALUE_DIM), jnp.float32) * np.sqrt(2.0 / (MODEL_DIM + VALUE_DIM)), 'bv': jnp.zeros((N_HEAD * VALUE_DIM,), jnp.float32), 'Wo': jax.random.normal(ks[6], (N_HEAD * VALUE_DIM, MODEL_DIM), jnp.float32) * np.sqrt(2.0 / (N_HEAD * VALUE_DIM + MODEL_DIM)), 'bo': jnp.zeros((MODEL_DIM,), jnp.float32), 'ln_gamma': jnp.ones((MODEL_DIM,), jnp.float32), 'ln_beta': jnp.zeros((MODEL_DIM,), jnp.float32)}
        return d
    _L1_xattn_all = _L1_xattn_setup()
    _L1_xattn_in = {k: v for k, v in _L1_xattn_all.items() if k in ('Wq', 'bq', 'Wk', 'bk', 'Wv', 'bv', 'Wo', 'bo', 'ln_gamma', 'ln_beta')}
    del _L1_xattn_all

    def _L1_ffn_setup():
        import jax, jax.numpy as jnp
        import numpy as np
        B, S, D_MODEL, D_HIDDEN = (4, 512, 256, 1024)

        def act_quant(x):
            scale = 127.0 / jnp.clip(jnp.max(jnp.abs(x), axis=-1, keepdims=True), 1e-05)
            return jnp.clip(jnp.round(x * scale), -128, 127) / scale

        def weight_quant(w):
            scale = 1.0 / jnp.clip(jnp.mean(jnp.abs(w)), 1e-05)
            return jnp.clip(jnp.round(w * scale), -1, 1) / scale

        def bit_linear(x, w):
            xq = x + jax.lax.stop_gradient(act_quant(x) - x)
            wq = w + jax.lax.stop_gradient(weight_quant(w) - w)
            return jnp.einsum('bsd,hd->bsh', xq, wq)

        def depthwise_conv1d(x_bcl, w, b):
            y = jax.lax.conv_general_dilated(x_bcl, w, window_strides=(1,), padding=[(1, 1)], dimension_numbers=('NCH', 'OIH', 'NCH'), feature_group_count=x_bcl.shape[1])
            return y + b[None, :, None]
        key = jax.random.key(seed)
        ks = jax.random.split(key, 5)
        lim1 = 1.0 / np.sqrt(D_MODEL)
        lim2 = 1.0 / np.sqrt(D_HIDDEN)
        limc = 1.0 / np.sqrt(3.0)
        return {'x': jax.random.normal(ks[0], (B, S, D_MODEL), dtype=jnp.float32), 'w1': jax.random.uniform(ks[1], (D_HIDDEN, D_MODEL), jnp.float32, -lim1, lim1), 'conv_w': jax.random.uniform(ks[2], (D_HIDDEN, 1, 3), jnp.float32, -limc, limc), 'conv_b': jax.random.uniform(ks[3], (D_HIDDEN,), jnp.float32, -limc, limc), 'w2': jax.random.uniform(ks[4], (D_MODEL, D_HIDDEN), jnp.float32, -lim2, lim2)}
    _L1_ffn_all = _L1_ffn_setup()
    _L1_ffn_in = {k: v for k, v in _L1_ffn_all.items() if k in ('w1', 'conv_w', 'conv_b', 'w2')}
    del _L1_ffn_all

    def _L2_xattn_setup():
        import jax, jax.numpy as jnp
        import numpy as np
        NUM_HEADS = 16
        INPUT_SIZE = 256
        HEAD_SIZE = INPUT_SIZE // NUM_HEADS
        B, L = (4, 512)
        key = jax.random.key(seed)
        ks = jax.random.split(key, 6)
        keys = jax.random.normal(ks[0], (B, L, INPUT_SIZE), dtype=jnp.float32)
        values = jax.random.normal(ks[1], (B, L, INPUT_SIZE), dtype=jnp.float32)
        queries = jax.random.normal(ks[2], (B, L, INPUT_SIZE), dtype=jnp.float32)
        mask = jax.random.randint(ks[3], (B, 1, L, L), 0, 2, dtype=jnp.int32)
        W_v = jax.random.normal(ks[4], (HEAD_SIZE, HEAD_SIZE), dtype=jnp.float32) / np.sqrt(HEAD_SIZE)
        W_o = jax.random.normal(ks[5], (INPUT_SIZE, INPUT_SIZE), dtype=jnp.float32) / np.sqrt(INPUT_SIZE)
        return {'keys': keys, 'values': values, 'queries': queries, 'mask': mask, 'W_v': W_v, 'W_o': W_o}
    _L2_xattn_all = _L2_xattn_setup()
    _L2_xattn_in = {k: v for k, v in _L2_xattn_all.items() if k in ('W_v', 'W_o')}
    del _L2_xattn_all

    def _L2_ffn_setup():
        import jax, jax.numpy as jnp
        import numpy as np
        NUM_EXPERTS_TOTAL = 9
        TOP_K = 2
        key = jax.random.key(seed)
        k0, k1, k2, k3, k4 = jax.random.split(key, 5)
        B, S, H, I = (2, 512, 256, 704)
        E = NUM_EXPERTS_TOTAL
        x = jax.random.normal(k0, (B, S, H), dtype=jnp.float32)
        Wr = jax.random.normal(k1, (H, E), dtype=jnp.float32) * 0.02
        Wg = jax.random.normal(k2, (E, H, I), dtype=jnp.float32) * 0.02
        Wu = jax.random.normal(k3, (E, H, I), dtype=jnp.float32) * 0.02
        Wd = jax.random.normal(k4, (E, I, H), dtype=jnp.float32) * 0.02
        return {'x': x, 'Wr': Wr, 'Wg': Wg, 'Wu': Wu, 'Wd': Wd}
    _L2_ffn_all = _L2_ffn_setup()
    _L2_ffn_in = {k: v for k, v in _L2_ffn_all.items() if k in ('Wr', 'Wg', 'Wu', 'Wd')}
    del _L2_ffn_all

    def _L3_xattn_setup():
        import jax, jax.numpy as jnp
        import numpy as np
        D_MODEL = 256
        N_HEAD = 16
        D_K = D_MODEL // N_HEAD
        key = jax.random.key(seed)
        ks = jax.random.split(key, 11)
        B, S = (2, 512)
        scale = 1.0 / np.sqrt(D_MODEL)
        inp = {'q': jax.random.normal(ks[0], (B, S, D_MODEL), jnp.float32), 'k': jax.random.normal(ks[1], (B, S, D_MODEL), jnp.float32), 'v': jax.random.normal(ks[2], (B, S, D_MODEL), jnp.float32), 'Wq': jax.random.normal(ks[3], (D_MODEL, D_MODEL), jnp.float32) * scale, 'bq': jnp.zeros((D_MODEL,), jnp.float32), 'Wk': jax.random.normal(ks[4], (D_MODEL, D_MODEL), jnp.float32) * scale, 'bk': jnp.zeros((D_MODEL,), jnp.float32), 'Wv': jax.random.normal(ks[5], (D_MODEL, D_MODEL), jnp.float32) * scale, 'bv': jnp.zeros((D_MODEL,), jnp.float32), 'Wo': jax.random.normal(ks[6], (D_MODEL, D_MODEL), jnp.float32) * scale, 'bo': jnp.zeros((D_MODEL,), jnp.float32)}
        return inp
    _L3_xattn_all = _L3_xattn_setup()
    _L3_xattn_in = {k: v for k, v in _L3_xattn_all.items() if k in ('Wq', 'bq', 'Wk', 'bk', 'Wv', 'bv', 'Wo', 'bo')}
    del _L3_xattn_all

    def _L3_ffn_setup():
        import jax, jax.numpy as jnp
        import numpy as np
        S, B, H, I, E = (128, 2, 256, 704, 8)
        key = jax.random.key(seed)
        ks = jax.random.split(key, 5)
        return {'hidden_states': jax.random.normal(ks[0], (S, B, H), dtype=jnp.float32), 'router_w': jax.random.normal(ks[1], (E, H), dtype=jnp.float32) * 0.02, 'gate_w': jax.random.normal(ks[2], (E, I, H), dtype=jnp.float32) * 0.02, 'up_w': jax.random.normal(ks[3], (E, I, H), dtype=jnp.float32) * 0.02, 'down_w': jax.random.normal(ks[4], (E, H, I), dtype=jnp.float32) * 0.02}
    _L3_ffn_all = _L3_ffn_setup()
    _L3_ffn_in = {k: v for k, v in _L3_ffn_all.items() if k in ('router_w', 'gate_w', 'up_w', 'down_w')}
    del _L3_ffn_all
    return {'x': x, 'ctx_1024': ctx_1024, 'mask_Bx1xSxS2_ik1': mask_Bx1xSxS2_ik1, 'L0_xattn_w_sim': _L0_xattn_in['w_sim'], 'L0_xattn_b_sim': _L0_xattn_in['b_sim'], 'L0_xattn_W_qv': _L0_xattn_in['W_qv'], 'L0_xattn_b_qv': _L0_xattn_in['b_qv'], 'L0_ffn_Wp': _L0_ffn_in['Wp'], 'L0_ffn_bp': _L0_ffn_in['bp'], 'L0_ffn_We': _L0_ffn_in['We'], 'L0_ffn_be': _L0_ffn_in['be'], 'L0_ffn_Vg': _L0_ffn_in['Vg'], 'L1_xattn_Wq': _L1_xattn_in['Wq'], 'L1_xattn_bq': _L1_xattn_in['bq'], 'L1_xattn_Wk': _L1_xattn_in['Wk'], 'L1_xattn_bk': _L1_xattn_in['bk'], 'L1_xattn_Wv': _L1_xattn_in['Wv'], 'L1_xattn_bv': _L1_xattn_in['bv'], 'L1_xattn_Wo': _L1_xattn_in['Wo'], 'L1_xattn_bo': _L1_xattn_in['bo'], 'L1_xattn_ln_gamma': _L1_xattn_in['ln_gamma'], 'L1_xattn_ln_beta': _L1_xattn_in['ln_beta'], 'L1_ffn_w1': _L1_ffn_in['w1'], 'L1_ffn_conv_w': _L1_ffn_in['conv_w'], 'L1_ffn_conv_b': _L1_ffn_in['conv_b'], 'L1_ffn_w2': _L1_ffn_in['w2'], 'L2_xattn_W_v': _L2_xattn_in['W_v'], 'L2_xattn_W_o': _L2_xattn_in['W_o'], 'L2_ffn_Wr': _L2_ffn_in['Wr'], 'L2_ffn_Wg': _L2_ffn_in['Wg'], 'L2_ffn_Wu': _L2_ffn_in['Wu'], 'L2_ffn_Wd': _L2_ffn_in['Wd'], 'L3_xattn_Wq': _L3_xattn_in['Wq'], 'L3_xattn_bq': _L3_xattn_in['bq'], 'L3_xattn_Wk': _L3_xattn_in['Wk'], 'L3_xattn_bk': _L3_xattn_in['bk'], 'L3_xattn_Wv': _L3_xattn_in['Wv'], 'L3_xattn_bv': _L3_xattn_in['bv'], 'L3_xattn_Wo': _L3_xattn_in['Wo'], 'L3_xattn_bo': _L3_xattn_in['bo'], 'L3_ffn_router_w': _L3_ffn_in['router_w'], 'L3_ffn_gate_w': _L3_ffn_in['gate_w'], 'L3_ffn_up_w': _L3_ffn_in['up_w'], 'L3_ffn_down_w': _L3_ffn_in['down_w']}

def reference(x, ctx_1024, mask_Bx1xSxS2_ik1, L0_xattn_w_sim, L0_xattn_b_sim, L0_xattn_W_qv, L0_xattn_b_qv, L0_ffn_Wp, L0_ffn_bp, L0_ffn_We, L0_ffn_be, L0_ffn_Vg, L1_xattn_Wq, L1_xattn_bq, L1_xattn_Wk, L1_xattn_bk, L1_xattn_Wv, L1_xattn_bv, L1_xattn_Wo, L1_xattn_bo, L1_xattn_ln_gamma, L1_xattn_ln_beta, L1_ffn_w1, L1_ffn_conv_w, L1_ffn_conv_b, L1_ffn_w2, L2_xattn_W_v, L2_xattn_W_o, L2_ffn_Wr, L2_ffn_Wg, L2_ffn_Wu, L2_ffn_Wd, L3_xattn_Wq, L3_xattn_bq, L3_xattn_Wk, L3_xattn_bk, L3_xattn_Wv, L3_xattn_bv, L3_xattn_Wo, L3_xattn_bo, L3_ffn_router_w, L3_ffn_gate_w, L3_ffn_up_w, L3_ffn_down_w):
    import jax
    import jax.numpy as jnp

    def _L0_xattn_ref(encoder_hc, decoder_hq, w_sim, b_sim, W_qv, b_qv):
        import jax, jax.numpy as jnp
        import numpy as np
        B, L_ENC, L_DEC, D = (16, 128, 128, 256)
        d = encoder_hc.shape[-1]
        w1, w2, w3 = (w_sim[:d], w_sim[d:2 * d], w_sim[2 * d:])
        Sim = (encoder_hc @ w1)[:, :, None] + (decoder_hq @ w2)[:, None, :] + jnp.einsum('bid,bjd->bij', encoder_hc * w3, decoder_hq) + b_sim[0]
        A = jax.nn.softmax(Sim, axis=2)
        hq_hat = jnp.einsum('bij,bjd->bid', A, decoder_hq)
        Batt = jax.nn.softmax(jnp.max(Sim, axis=2), axis=1)
        hc_bar = jnp.einsum('bi,bid->bd', Batt, encoder_hc)[:, None, :]
        hc_hat = jnp.broadcast_to(hc_bar, encoder_hc.shape)
        feats = jnp.concatenate([encoder_hc, hq_hat, encoder_hc * hq_hat, encoder_hc * hc_hat], axis=-1)
        hcq = feats @ W_qv + b_qv
        return hcq

    def _L0_ffn_ref(hidden_states, Wp, bp, We, be, Vg):
        import jax, jax.numpy as jnp
        import numpy as np
        B, S, D_IN, D_OUT, E, GATE_K, TOP_K = (4, 2048, 256, 256, 8, 64, 2)

        def _gate(x, Vg):
            T = x.shape[0]
            xe = jnp.einsum('ti,eir->ter', x, Vg)
            proj = jnp.einsum('ter,eir->tei', xe, Vg)
            residuals = jnp.linalg.norm(x[:, None, :] - proj, axis=-1)
            rw = jax.nn.softmax(-residuals, axis=1)
            thr = 1.0 / E
            mask = rw > thr
            rows = jnp.arange(T)[:, None]
            top1_idx = jnp.argmax(rw, axis=1, keepdims=True)
            top1_mask = jnp.zeros_like(mask).at[rows, top1_idx].set(True)
            mask = jnp.where(jnp.any(mask), mask, top1_mask)
            if TOP_K < E:
                _, topi = jax.lax.top_k(rw, TOP_K)
                topk_mask = jnp.zeros_like(mask).at[rows, topi].set(True)
                mask = mask & topk_mask
            fw = rw * mask.astype(rw.dtype)
            sw = fw.sum(axis=1, keepdims=True)
            sw = jnp.where(sw == 0, jnp.ones_like(sw), sw)
            return fw / sw
        in_shape = hidden_states.shape
        pretrained_out = jnp.einsum('bsi,oi->bso', hidden_states, Wp) + bp
        x = hidden_states.reshape(-1, in_shape[-1])
        w = _gate(x, Vg)
        expert_out = jnp.einsum('ti,eoi->teo', x, We) + be[None]
        final = jnp.einsum('te,teo->to', w, expert_out)
        final = final.reshape(*in_shape[:-1], We.shape[1])
        return pretrained_out + final

    def _L1_xattn_ref(query, key, value, Wq, bq, Wk, bk, Wv, bv, Wo, bo, ln_gamma, ln_beta):
        import jax, jax.numpy as jnp
        import numpy as np
        N_HEAD, MODEL_DIM, KEY_DIM, VALUE_DIM = (16, 256, 64, 64)
        B, S = (4, 512)
        EPS = 1e-05
        TEMP = float(np.sqrt(KEY_DIM))
        b, sq, _ = query.shape
        residual = query
        q = (query @ Wq + bq).reshape(b, sq, N_HEAD, KEY_DIM)
        k = (key @ Wk + bk).reshape(b, key.shape[1], N_HEAD, KEY_DIM)
        v = (value @ Wv + bv).reshape(b, value.shape[1], N_HEAD, VALUE_DIM)
        scores = jnp.einsum('bqhd,bkhd->bhqk', q, k) / TEMP
        attn = jax.nn.softmax(scores, axis=-1)
        out = jnp.einsum('bhqk,bkhd->bqhd', attn, v).reshape(b, sq, N_HEAD * VALUE_DIM)
        out = out @ Wo + bo + residual
        mu = jnp.mean(out, axis=-1, keepdims=True)
        var = jnp.var(out, axis=-1, keepdims=True)
        return (out - mu) * jax.lax.rsqrt(var + EPS) * ln_gamma + ln_beta

    def _L1_ffn_ref(x, w1, conv_w, conv_b, w2):
        import jax, jax.numpy as jnp
        import numpy as np
        B, S, D_MODEL, D_HIDDEN = (4, 512, 256, 1024)

        def act_quant(x):
            scale = 127.0 / jnp.clip(jnp.max(jnp.abs(x), axis=-1, keepdims=True), 1e-05)
            return jnp.clip(jnp.round(x * scale), -128, 127) / scale

        def weight_quant(w):
            scale = 1.0 / jnp.clip(jnp.mean(jnp.abs(w)), 1e-05)
            return jnp.clip(jnp.round(w * scale), -1, 1) / scale

        def bit_linear(x, w):
            xq = x + jax.lax.stop_gradient(act_quant(x) - x)
            wq = w + jax.lax.stop_gradient(weight_quant(w) - w)
            return jnp.einsum('bsd,hd->bsh', xq, wq)

        def depthwise_conv1d(x_bcl, w, b):
            y = jax.lax.conv_general_dilated(x_bcl, w, window_strides=(1,), padding=[(1, 1)], dimension_numbers=('NCH', 'OIH', 'NCH'), feature_group_count=x_bcl.shape[1])
            return y + b[None, :, None]
        h = bit_linear(x, w1)
        h = depthwise_conv1d(h.transpose(0, 2, 1), conv_w, conv_b)
        h = h.transpose(0, 2, 1)
        h = jax.nn.silu(h)
        return bit_linear(h, w2)

    def _L2_xattn_ref(keys, values, queries, mask, W_v, W_o):
        import jax, jax.numpy as jnp
        import numpy as np
        NUM_HEADS = 16
        INPUT_SIZE = 256
        HEAD_SIZE = INPUT_SIZE // NUM_HEADS
        B, L = (4, 512)
        b, q_len, d = queries.shape
        k_len = keys.shape[1]
        n, h = (NUM_HEADS, HEAD_SIZE)
        k = jnp.einsum('bknh,oh->bkno', keys.reshape(b, k_len, n, h), W_v)
        v = jnp.einsum('bknh,oh->bkno', values.reshape(b, k_len, n, h), W_v)
        q = jnp.einsum('bqnh,oh->bqno', queries.reshape(b, q_len, n, h), W_v)
        z = jnp.einsum('bqnh,bknh->bnqk', q, k)
        z = jnp.where(mask == 0, jnp.float32(-1e-20), z)
        attention = jax.nn.softmax(z / jnp.sqrt(jnp.float32(d)), axis=3)
        out = jnp.einsum('bnqk,bknh->bqnh', attention, v).reshape(b, q_len, n * h)
        out = jnp.einsum('bqd,od->bqo', out, W_o)
        return out

    def _L2_ffn_ref(x, Wr, Wg, Wu, Wd):
        import jax, jax.numpy as jnp
        import numpy as np
        NUM_EXPERTS_TOTAL = 9
        TOP_K = 2
        B, S, H = x.shape
        E = NUM_EXPERTS_TOTAL
        T = B * S
        logits = jnp.einsum('bsh,he->bse', x, Wr)
        probs = jax.nn.softmax(logits, axis=-1)
        topk_w, topk_idx = jax.lax.top_k(probs, TOP_K)
        topk_w = topk_w / jnp.sum(topk_w, axis=-1, keepdims=True)
        xf = x.reshape(T, H)
        wf = topk_w.reshape(T, TOP_K)
        idxf = topk_idx.reshape(T, TOP_K)
        cw = jnp.zeros((T, E), dtype=x.dtype).at[jnp.arange(T)[:, None], idxf].add(wf)
        gate = jax.nn.silu(jnp.einsum('th,ehi->tei', xf, Wg))
        hidden = gate * jnp.einsum('th,ehi->tei', xf, Wu)
        out = jnp.einsum('tei,eih,te->th', hidden, Wd, cw)
        return out.reshape(B, S, H)

    def _L3_xattn_ref(q, k, v, Wq, bq, Wk, bk, Wv, bv, Wo, bo):
        import jax, jax.numpy as jnp
        import numpy as np
        D_MODEL = 256
        N_HEAD = 16
        D_K = D_MODEL // N_HEAD
        B, S, _ = q.shape

        def proj(x, W, b):
            y = x @ W + b
            return y.reshape(B, -1, N_HEAD, D_K).transpose(0, 2, 1, 3)
        qh = proj(q, Wq, bq)
        kh = proj(k, Wk, bk)
        vh = proj(v, Wv, bv)
        scores = jnp.einsum('bhsd,bhtd->bhst', qh, kh) / jnp.sqrt(jnp.float32(D_K))
        attn = jax.nn.sigmoid(scores)
        ctx = jnp.einsum('bhst,bhtd->bhsd', attn, vh)
        ctx = ctx.transpose(0, 2, 1, 3).reshape(B, S, D_MODEL)
        return ctx @ Wo + bo

    def _L3_ffn_ref(hidden_states, router_w, gate_w, up_w, down_w):
        import jax, jax.numpy as jnp
        import numpy as np
        S, B, H, I, E = (128, 2, 256, 704, 8)
        router_logits = jnp.einsum('sbh,eh->sbe', hidden_states, router_w)
        routing_indices = jnp.argmax(router_logits, axis=-1)
        out = jnp.zeros_like(hidden_states)
        for e in range(E):
            mask = (routing_indices == e)[..., None]
            xe = jnp.where(mask, hidden_states, 0.0)
            g = jnp.einsum('sbh,ih->sbi', xe, gate_w[e])
            u = jnp.einsum('sbh,ih->sbi', xe, up_w[e])
            ye = jnp.einsum('sbi,hi->sbh', jax.nn.silu(g) * u, down_w[e])
            out = out + jnp.where(mask, ye, 0.0)
        return out
    x = x + _L0_xattn_ref(_layernorm(x, axis=-1), ctx_1024, L0_xattn_w_sim, L0_xattn_b_sim, L0_xattn_W_qv, L0_xattn_b_qv)
    x = x + _L0_ffn_ref(_layernorm(x, axis=-1), L0_ffn_Wp, L0_ffn_bp, L0_ffn_We, L0_ffn_be, L0_ffn_Vg)
    x = x + _L1_xattn_ref(_layernorm(x, axis=-1), ctx_1024, ctx_1024, L1_xattn_Wq, L1_xattn_bq, L1_xattn_Wk, L1_xattn_bk, L1_xattn_Wv, L1_xattn_bv, L1_xattn_Wo, L1_xattn_bo, L1_xattn_ln_gamma, L1_xattn_ln_beta)
    x = x + _L1_ffn_ref(_layernorm(x, axis=-1), L1_ffn_w1, L1_ffn_conv_w, L1_ffn_conv_b, L1_ffn_w2)
    x = x + _L2_xattn_ref(ctx_1024, ctx_1024, _layernorm(x, axis=-1), mask_Bx1xSxS2_ik1, L2_xattn_W_v, L2_xattn_W_o)
    x = x + _L2_ffn_ref(_layernorm(x, axis=-1), L2_ffn_Wr, L2_ffn_Wg, L2_ffn_Wu, L2_ffn_Wd)
    x = x + _L3_xattn_ref(_layernorm(x, axis=-1), ctx_1024, ctx_1024, L3_xattn_Wq, L3_xattn_bq, L3_xattn_Wk, L3_xattn_bk, L3_xattn_Wv, L3_xattn_bv, L3_xattn_Wo, L3_xattn_bo)
    x = x + _L3_ffn_ref(_layernorm(x, axis=-1), L3_ffn_router_w, L3_ffn_gate_w, L3_ffn_up_w, L3_ffn_down_w)
    return x

_drawn_inputs = setup_inputs


def setup_inputs(seed=0):
    import zlib

    import numpy as np

    out = dict(_drawn_inputs(seed))
    spreads = {'L1_xattn_bq': (0.0, 0.8),
     'L1_xattn_bk': (0.0, 2.0),
     'L1_xattn_bv': (0.0, 0.734),
     'L1_xattn_bo': (0.0, 0.8),
     'L1_xattn_ln_gamma': (1.0, 0.6),
     'L1_xattn_ln_beta': (0.0, 0.689),
     'L3_xattn_bq': (0.0, 0.332),
     'L3_xattn_bk': (0.0, 0.1),
     'L3_xattn_bv': (0.0, 0.1),
     'L3_xattn_bo': (0.0, 2.0)}
    factors = {'L0_xattn_w_sim': 4.192,
     'L0_xattn_b_qv': 7.158,
     'L0_ffn_bp': 8.0,
     'L0_ffn_be': 8.0,
     'L1_ffn_w1': 7.844,
     'L1_ffn_conv_w': 7.579,
     'L1_ffn_conv_b': 7.397,
     'L1_ffn_w2': 4.811,
     'L2_ffn_Wr': 8.0,
     'L2_ffn_Wg': 8.0,
     'L2_ffn_Wu': 8.0,
     'L2_ffn_Wd': 8.0,
     'L3_ffn_router_w': 8.0,
     'L3_ffn_gate_w': 8.0,
     'L3_ffn_up_w': 8.0,
     'L3_ffn_down_w': 8.0}
    for name, (base, spread) in spreads.items():
        noise = np.random.default_rng([zlib.crc32(name.encode()), seed]).standard_normal(out[name].shape)
        drawn = base * np.exp(spread * noise) if base else spread * noise
        out[name] = jnp.asarray(drawn.astype(out[name].dtype))
    for name, factor in factors.items():
        out[name] = (out[name] * factor).astype(out[name].dtype)
    return out
```

```python
from contextlib import ExitStack

import concourse.bass as bass
from concourse import mybir

F32 = mybir.dt.float32
BF16 = mybir.dt.bfloat16
I32 = mybir.dt.int32
ACT = mybir.ActivationFunctionType
ALU = mybir.AluOpType
AX = mybir.AxisListType

NB, S, D = 8, 100, 256
T = NB * S
P = 128
KD = D // P
KV = 361
KT = 121
NKT = 3
KVP = KT * NKT
NH = 16
HALF = T // 2
IT = 704
NI = 6
IP = NI * P
EPS = 1e-5
MAGIC = 1.5 * 2.0 ** 23


class Event:
    def __init__(self, handle, head):
        self.sem, self.head = handle, head

    def at(self, count, step=1):
        return count * step + self.head


class Chain:

    def __init__(self, eng, event):
        self.eng, self.sem, self.base, self.k, self.turn, self.per = eng, event.sem, 0, 0, 0, 0

    def loop(self, turn, per):
        self.base, self.turn, self.per, self.k = self.base + self.k, turn, per, 0

    def end(self, turns):
        assert self.k == self.per, (self.k, self.per)
        self.base, self.turn, self.per, self.k = self.base + turns * self.per, 0, 0, 0

    def step(self, ins):
        ins.then_inc(self.sem, 1)
        self.k += 1
        self.eng.wait_ge(self.sem, self.base + self.turn * self.per + self.k)


class Stage:

    def __init__(self, core):
        self.core, self.nc, self.ctx, self.used = core, core.nc, ExitStack(), []

    def __enter__(self):
        return self

    def sb(self, name, shape, dt=F32):
        return self.ctx.enter_context(self.nc.sbuf_tensor(f"{name}_{self.core.stage}", shape, dt))

    def event(self, head=0):
        e = Event(self.core.pool[len(self.used)], head)
        self.used.append(e)
        return e

    def block(self):
        return self.nc.Block()

    def __exit__(self, *a):
        self.ctx.close()
        self.core.stage += 1
        if a[0] is not None:
            return
        with self.nc.Block() as block:
            @block.gpsimd
            def _(pool):
                for e in self.used:
                    pool.sem_clear(e.sem)

    def heads(self, eng):
        for e in self.used:
            if e.head:
                eng.sem_inc(e.sem, e.head)


class Core:

    def __init__(self, nc, ctx):
        self.nc, self.stage = nc, 0
        sb = lambda name, shape, dt=F32: ctx.enter_context(nc.sbuf_tensor(name, shape, dt))
        self.X = sb("X", [S, NB, D])
        self.N = sb("N", [S, NB, D])
        self.NT = sb("NT", [P, KD, T])
        self.ident = sb("ident", [P, P])
        self.identb = sb("identb", [P, P], BF16)
        self.ones = sb("ones", [P, P])
        self.below = sb("below", [S, 9, 9])
        self.head_mask = sb("head_mask", [P, 8])
        self.minus_half = sb("minus_half", [S, NB])
        self.half = sb("half", [S, 64])
        self.rows = sb("rows", [P, 9, D])
        self.ps = [ctx.enter_context(nc.psum_tensor(f"bank{i}", [P, 512], F32)) for i in range(8)]
        self.sem = lambda name: ctx.enter_context(nc.semaphore(name))
        self.pool = [self.sem(f"event{i}") for i in range(44)]


def batches(eng, body, chain=None, steps=0):
    with eng.Fori(0, NB // 2 - 1) as i:
        if chain:
            chain.loop(i, 2 * steps)
        for j in range(2):
            body(2 * i + j, j, i, True)
    if chain:
        chain.end(NB // 2 - 1)
    body(NB - 2, 0, NB // 2 - 1, True)
    body(NB - 1, 1, NB // 2 - 1, False)


def pair(ap, n):
    return ap.unsqueeze(1).broadcast_to([ap.shape[0], n, ap.shape[1]])


def wide(ap, n):
    return ap.unsqueeze(2).broadcast_to([ap.shape[0], ap.shape[1], n])


def token(b):
    return bass.ds(b * S, S)


def variance(dve, chain, stats, mean, gap, var):
    chain.step(dve.tensor_tensor(mean, stats[:, :, 1], stats[:, :, 4], ALU.add))
    chain.step(dve.tensor_tensor(gap, stats[:, :, 1], stats[:, :, 4], ALU.subtract))
    chain.step(dve.tensor_tensor(var, stats[:, :, 2], stats[:, :, 5], ALU.add))
    chain.step(dve.tensor_tensor(gap, gap, gap, ALU.mult))
    chain.step(dve.tensor_scalar(gap, gap, 0.25, EPS, ALU.mult, ALU.add))
    return dve.scalar_tensor_tensor(var, var, 1.0 / D, gap, ALU.mult, ALU.add)


def layer_norm(core):
    X, N, NT, ps = core.X, core.N, core.NT, core.ps
    with Stage(core) as st:
        stats = st.sb("stats", [S, NB, 6])
        mean = st.sb("mean", [S, NB])
        gap = st.sb("gap", [S, NB])
        var = st.sb("var", [S, NB])
        rstd = st.sb("rstd", [S, NB])
        stats_ready, var_ready, rstd_ready, n_ready, nt_psum = (st.event() for _ in range(5))
        own, nt_ready = st.event(), st.event()
        with st.block() as block:
            @block.vector
            def _(dve):
                chain = Chain(dve, own)
                with dve.Fori(0, NB) as b:
                    dve.bn_stats(stats[:, bass.ds(b, 1), :], core.X[:, bass.ds(b, 1), :]).then_inc(stats_ready.sem, 1)
                dve.wait_ge(stats_ready.sem, NB)
                variance(dve, chain, stats[:, :, :], mean[:, :], gap[:, :], var[:, :]).then_inc(var_ready.sem, 1)
                chain.step(dve.tensor_scalar(mean[:, :], mean[:, :], 0.5, None, ALU.mult))
                dve.wait_ge(rstd_ready.sem, 1)
                with dve.Fori(0, NB) as b:
                    dve.tensor_scalar(N[:, bass.ds(b, 1), :], X[:, bass.ds(b, 1), :], mean[:, bass.ds(b, 1)],
                                      rstd[:, bass.ds(b, 1)], ALU.subtract, ALU.mult).then_inc(n_ready.sem, 1)

            @block.gpsimd
            def _(pool):
                pool.wait_ge(var_ready.sem, 1)
                pool.tensor_tensor(rstd[:, :], var[:, :], core.minus_half[:, 0:NB], ALU.pow).then_inc(rstd_ready.sem, 1)

            @block.tensor
            def _(pe):
                for q in range(NB // 2):
                    pe.wait_ge(n_ready.sem, 2 * q + 2)
                    for j in range(2):
                        for k in range(KD):
                            ins = pe.transpose(ps[q][:, (2 * k + j) * S:(2 * k + j + 1) * S],
                                               N[:, 2 * q + j, k * P:(k + 1) * P], core.ident[0:S, 0:S])
                    ins.then_inc(nt_psum.sem, 1)

            @block.scalar
            def _(act):
                for q in range(NB // 2):
                    act.wait_ge(nt_psum.sem, q + 1)
                    act.activation(NT[:, :, 2 * q * S:2 * (q + 1) * S],
                                   ps[q][:, 0:4 * S].rearrange("p (k t) -> p k t", k=KD),
                                   ACT.Copy).then_inc(nt_ready.sem, 1)
                act.wait_ge(nt_ready.sem, NB // 2)


def setup(core, io):
    with Stage(core) as st:
        loaded, zeroed, made = st.event(), st.event(), st.event()
        with st.block() as block:
            @block.sync
            def _(sp):
                sp.dma_start(core.X[:, :, :], io["x"]).then_inc(loaded.sem, 16)
                sp.dma_start(core.head_mask[:, :], io["head_mask"]).then_inc(loaded.sem, 16)
                sp.dma_start(core.below[:, :, :], io["below"].partition_broadcast(S)).then_inc(loaded.sem, 16)
                sp.dma_start(core.rows[:, :, :], io["rows"].partition_broadcast(P)).then_inc(loaded.sem, 16)
                core.load(sp, "sim", io)
                core.load(sp, "gated", io)
                core.load(sp, "head64", io)
                sp.wait_ge(loaded.sem, 64)

            @block.gpsimd
            def _(pool):
                pool.memset(core.ident[:, :], 0.0).then_inc(zeroed.sem, 1)
                pool.memset(core.ones[:, :], 1.0)
                pool.memset(core.minus_half[:, :], -0.5)
                pool.memset(core.half[:, :], 0.5)
                pool.wait_ge(zeroed.sem, 1)
                pool.affine_select(out=core.ident[:, :], in_=core.ident[:, :], compare_op=ALU.not_equal, fill=1.0,
                                   base=0, pattern=[[-1, P]], channel_multiplier=1).then_inc(made.sem, 1)
                pool.wait_ge(made.sem, 1)
                pool.tensor_copy(core.identb[:, :], core.ident[:, :])


def sim_attention(core, io):
    X, N, NT, ps = core.X, core.N, core.NT, core.ps
    w = core.weights
    with Stage(core) as st:
        ctT = [st.sb(f"ctT{j}", [P, KD, KVP]) for j in range(2)]
        ctk = [st.sb(f"ctk{j}", [KT, NKT, D]) for j in range(2)]
        EW = [st.sb(f"EW{j}", [P, KD, S]) for j in range(2)]
        A = [st.sb(f"A{j}", [S, KVP]) for j in range(2)]
        AT = [st.sb(f"AT{j}", [KT, NKT, S]) for j in range(2)]
        F = [st.sb(f"F{j}", [P, 8, S]) for j in range(2)]
        HQ = st.sb("HQ", [P, KD, T])
        neg_max, total, inv = st.sb("neg_max", [S, NB]), st.sb("total", [S, NB]), st.sb("inv", [S, NB])
        enc_w1 = st.sb("enc_w1", [S, NB, D])
        row_max, best, per_batch = st.sb("row_max", [S, NB]), st.sb("best", [NB, 4]), st.sb("per_batch", [NB, S])
        beta = st.sb("beta", [S, NB])
        hc = st.sb("hc", [P, KD, NB])
        ctx_loaded = [st.event(), st.event()]
        ctk_loaded = [st.event(), st.event()]
        ew_ready, sim_ready, max_ready, norm_ready = st.event(), st.event(2), st.event(), st.event()
        exp_ready, at_psum, at_ready, hq_psum, hq_ready = (st.event(2) for _ in range(5))
        own, own_act, pads, w1_ready, bias_ready = (st.event() for _ in range(5))
        m_ready, mt_psum, top_ready, e_ready, share_ready, share_psum, beta_ready, hc_psum, hc_ready = \
            (st.event() for _ in range(9))
        f_act, f_pool, f_dve, out_psum, x_ready = st.event(), st.event(), st.event(), st.event(2), st.event(2)
        heads_set = st.event()
        with st.block() as block:
            @block.sync
            def _(sp):
                st.heads(sp)
                with sp.Fori(0, NB // 2) as i:
                    for j in range(2):
                        b = 2 * i + j
                        sp.wait_ge(hq_psum.sem, hq_psum.at(b - 1))
                        sp.dma_start(ctT[j][:, :, :], io["ctT"][bass.ds(b, 1)]).then_inc(ctx_loaded[j].sem, 16)
                        sp.dma_start(ctk[j][:, :, :], io["ctk"][bass.ds(b, 1)]).then_inc(ctk_loaded[j].sem, 16)

            @block.gpsimd
            def _(pool):
                pool.wait_ge(core.loaded["sim"], core.loads["sim"])
                for j in range(2):
                    pool.memset(A[j][:, KV:KVP], 0.0).then_inc(pads.sem, 1)
                pool.tensor_tensor(enc_w1[:, :, :], N[:, :, :], pair(core.rows[0:S, W1_SIM, :], NB),
                                   ALU.mult).then_inc(w1_ready.sem, 1)
                pool.tensor_tensor(X[:, :, :], X[:, :, :], pair(core.rows[0:S, B_QV, :], NB),
                                   ALU.add).then_inc(bias_ready.sem, 1)
                pool.wait_ge(hq_ready.sem, hq_ready.at(NB))
                with pool.Fori(0, NB // 2) as i:
                    for j in range(2):
                        b = 2 * i + j
                        pool.wait_ge(out_psum.sem, out_psum.at(b - 1))
                        pool.tensor_tensor(F[j][:, 4:6, :], NT[:, :, token(b)], HQ[:, :, token(b)],
                                           ALU.mult).then_inc(f_pool.sem, 1)

            @block.vector
            def _(dve):
                chain = Chain(dve, own)
                dve.wait_ge(core.loaded["sim"], core.loads["sim"])
                with dve.Fori(0, NB // 2) as i:
                    chain.loop(i, 2)
                    for j in range(2):
                        b = 2 * i + j
                        dve.wait_ge(sim_ready.sem, sim_ready.at(b - 1))
                        for k in range(KD):
                            dve.tensor_scalar(EW[j][:, k, :], NT[:, k, token(b)], w["w_sim"][:, KD + k:KD + k + 1],
                                              w["w_sim"][:, k:k + 1], ALU.mult, ALU.add).then_inc(ew_ready.sem, 1)
                        dve.wait_ge(sim_ready.sem, sim_ready.at(b + 1))
                        dve.tensor_reduce(neg_max[:, bass.ds(b, 1)], ps[j][0:S, 0:KV], AX.X, ALU.max,
                                          negate=True).then_inc(max_ready.sem, 1)
                        dve.wait_ge(exp_ready.sem, exp_ready.at(b + 1))
                        chain.step(dve.reciprocal(inv[:, bass.ds(b, 1)], total[:, bass.ds(b, 1)]))
                        dve.tensor_scalar(A[j][:, 0:KV], A[j][:, 0:KV], inv[:, bass.ds(b, 1)], None,
                                          ALU.mult).then_inc(norm_ready.sem, 1)
                chain.end(NB // 2)
                dve.wait_ge(w1_ready.sem, 1)
                chain.step(dve.tensor_reduce(row_max[:, :], enc_w1[:, :, :], AX.X, ALU.add))
                dve.wait_ge(max_ready.sem, NB)
                chain.step(dve.tensor_tensor(row_max[:, :], row_max[:, :], neg_max[:, :], ALU.subtract))
                dve.tensor_scalar(row_max[:, :], row_max[:, :], w["b_sim"][0:S, :], None, ALU.add).then_inc(m_ready.sem, 1)
                dve.wait_ge(mt_psum.sem, 1)
                dve.tensor_reduce(best[:, 0:1], ps[6][0:NB, 0:S], AX.X, ALU.max, negate=True).then_inc(top_ready.sem, 1)
                dve.wait_ge(e_ready.sem, 1)
                chain.step(dve.reciprocal(best[:, 2:3], best[:, 1:2]))
                dve.tensor_scalar(per_batch[:, :], per_batch[:, :], best[:, 2:3], None, ALU.mult).then_inc(share_ready.sem, 1)
                dve.wait_ge(share_psum.sem, 1)
                dve.tensor_copy(beta[:, :], ps[7][0:S, 0:NB]).then_inc(beta_ready.sem, 1)
                dve.wait_ge(hc_psum.sem, 1)
                chain.step(dve.tensor_copy(hc[:, :, :], ps[6][:, 0:KD * NB].rearrange("p (k b) -> p k b", k=KD)))
                dve.wait_ge(bias_ready.sem, 1)
                with dve.Fori(0, NB // 2) as i:
                    for j in range(2):
                        b = 2 * i + j
                        dve.wait_ge(out_psum.sem, out_psum.at(b - 1))
                        for k in range(KD):
                            dve.tensor_scalar(F[j][:, 6 + k, :], NT[:, k, token(b)], hc[:, k, bass.ds(b, 1)], None,
                                              ALU.mult).then_inc(f_dve.sem, 1)
                        dve.wait_ge(out_psum.sem, out_psum.at(b + 1))
                        dve.tensor_tensor(X[:, bass.ds(b, 1), :], X[:, bass.ds(b, 1), :], ps[j][0:S, 0:D].unsqueeze(1),
                                          ALU.add).then_inc(x_ready.sem, 1)

            @block.scalar
            def _(act):
                act.wait_ge(pads.sem, 2)
                with act.Fori(0, NB // 2) as i:
                    for j in range(2):
                        b = 2 * i + j
                        act.wait_ge(max_ready.sem, b + 1)
                        act.wait_ge(at_psum.sem, at_psum.at(b - 1))
                        act.activation(A[j][:, 0:KV], ps[j][0:S, 0:KV], ACT.Exp, bias=neg_max[:, bass.ds(b, 1)],
                                       accum_out=total[:, bass.ds(b, 1)]).then_inc(exp_ready.sem, 1)
                        act.wait_ge(at_psum.sem, at_psum.at(b + 1))
                        act.wait_ge(hq_psum.sem, hq_psum.at(b - 1))
                        act.activation(AT[j][:, :, :], ps[2 + j][0:KT, 0:NKT * S].rearrange("p (t s) -> p t s", t=NKT),
                                       ACT.Copy).then_inc(at_ready.sem, 1)
                        act.wait_ge(hq_psum.sem, hq_psum.at(b + 1))
                        act.activation(HQ[:, :, token(b)], ps[4 + j][:, 0:KD * S].rearrange("p (k s) -> p k s", k=KD),
                                       ACT.Copy).then_inc(hq_ready.sem, 1)
                act.wait_ge(top_ready.sem, 1)
                act.activation(per_batch[:, :], ps[6][0:NB, 0:S], ACT.Exp, bias=best[:, 0:1],
                               accum_out=best[:, 1:2]).then_inc(e_ready.sem, 1)
                act.wait_ge(hq_ready.sem, hq_ready.at(NB))
                with act.Fori(0, NB // 2) as i:
                    for j in range(2):
                        b = 2 * i + j
                        act.wait_ge(out_psum.sem, out_psum.at(b - 1))
                        act.activation(F[j][:, 0:2, :], NT[:, :, token(b)], ACT.Copy).then_inc(f_act.sem, 1)
                        act.activation(F[j][:, 2:4, :], HQ[:, :, token(b)], ACT.Copy).then_inc(f_act.sem, 1)

            @block.tensor
            def _(pe):
                pe.wait_ge(core.loaded["sim"], core.loads["sim"])
                with pe.Fori(0, NB // 2) as i:
                    for j in range(2):
                        b = 2 * i + j
                        pe.wait_ge(ew_ready.sem, KD * (b + 1))
                        pe.wait_ge(ctx_loaded[j].sem, 16 * (i + 1))
                        pe.wait_ge(exp_ready.sem, exp_ready.at(b - 1))
                        for k in range(KD):
                            ins = pe.matmul(ps[j][0:S, 0:KV], EW[j][:, k, :], ctT[j][:, k, 0:KV], start=k == 0,
                                            stop=k == KD - 1)
                        ins.then_inc(sim_ready.sem, 1)
                        pe.wait_ge(norm_ready.sem, b + 1)
                        pe.wait_ge(at_ready.sem, at_ready.at(b - 1))
                        for t in range(NKT):
                            ins = pe.transpose(ps[2 + j][0:KT, t * S:(t + 1) * S], A[j][:, t * KT:(t + 1) * KT],
                                               core.ident[0:S, 0:S])
                        ins.then_inc(at_psum.sem, 1)
                        pe.wait_ge(at_ready.sem, at_ready.at(b + 1))
                        pe.wait_ge(ctk_loaded[j].sem, 16 * (i + 1))
                        pe.wait_ge(hq_ready.sem, hq_ready.at(b - 1))
                        for m in range(KD):
                            for t in range(NKT):
                                ins = pe.matmul(ps[4 + j][:, m * S:(m + 1) * S], ctk[j][:, t, m * P:(m + 1) * P],
                                                AT[j][:, t, :], start=t == 0, stop=t == NKT - 1)
                        ins.then_inc(hq_psum.sem, 1)
                pe.wait_ge(m_ready.sem, 1)
                pe.transpose(ps[6][0:NB, 0:S], row_max[:, :], core.ident[0:S, 0:S]).then_inc(mt_psum.sem, 1)
                pe.wait_ge(share_ready.sem, 1)
                pe.transpose(ps[7][0:S, 0:NB], per_batch[:, :], core.ident[0:NB, 0:NB]).then_inc(share_psum.sem, 1)
                pe.wait_ge(beta_ready.sem, 1)
                for b in range(NB):
                    for k in range(KD):
                        ins = pe.matmul(ps[6][:, k * NB + b:k * NB + b + 1], N[:, b, k * P:(k + 1) * P],
                                        beta[:, b:b + 1], start=True, stop=True)
                ins.then_inc(hc_psum.sem, 1)
                with pe.Fori(0, NB // 2) as i:
                    for j in range(2):
                        b = 2 * i + j
                        pe.wait_ge(f_act.sem, 2 * (b + 1))
                        pe.wait_ge(f_pool.sem, b + 1)
                        pe.wait_ge(f_dve.sem, KD * (b + 1))
                        pe.wait_ge(x_ready.sem, x_ready.at(b - 1))
                        for k in range(8):
                            ins = pe.matmul(ps[j][0:S, 0:D], F[j][:, k, :], w["W_qv"][:, k, :], start=k == 0, stop=k == 7)
                        ins.then_inc(out_psum.sem, 1)


def top_mask(dve, chain, r, nb, ne, keep, above, same, rank, mask, below):
    full = [S, nb, ne, ne]
    other = r.unsqueeze(2).broadcast_to(full)
    this = r.unsqueeze(3).broadcast_to(full)
    chain.step(dve.tensor_tensor(above, other, this, ALU.is_gt))
    chain.step(dve.tensor_tensor(same, other, this, ALU.is_equal))
    chain.step(dve.tensor_tensor(same, same, below.unsqueeze(1).broadcast_to(full), ALU.mult))
    chain.step(dve.tensor_tensor(above, above, same, ALU.add))
    chain.step(dve.tensor_reduce(rank, above, AX.X, ALU.add))
    for n, m in zip(keep, mask):
        chain.step(dve.tensor_scalar(m, rank, float(n), None, ALU.is_lt))


def gated_experts(core, io):
    X, N, NT, ps = core.X, core.N, core.NT, core.ps
    w = core.weights
    E = 8
    with Stage(core) as st:
        xeT = [st.sb(f"xeT{j}", [P, 4, S]) for j in range(2)]
        DF = [st.sb(f"DF{j}", [S, 2, D]) for j in range(2)]
        R = st.sb("R", [S, NB, E])
        small = st.sb("small", [S, 6, NB])
        RW = st.sb("RW", [S, NB, E])
        above, same = st.sb("above", [S, NB, E, E]), st.sb("same", [S, NB, E, E])
        rank, top1, top2, over = (st.sb(n, [S, NB, E]) for n in ("rank", "top1", "top2", "over"))
        any_over, flag = st.sb("any_over", [S, 1]), st.sb("flag", [S, 1])
        NTs = [st.sb(f"NTs{j}", [P, KD, S]) for j in range(2)]
        wb = [st.sb(f"wb{j}", [S, E]) for j in range(2)]
        wT = [st.sb(f"wT{j}", [E, S]) for j in range(2)]
        xe_psum, xeT_ready, d_psum, d_ready, sq_done = st.event(), st.event(2), st.event(8), st.event(4), st.event(4)
        own, root_ready, e_in, e_ready, any_ready, flag_psum, bias_ready = (st.event() for _ in range(7))
        nts_ready, wb_ready, wt_psum, wt_ready = st.event(), st.event(), st.event(2), st.event(2)
        base_psum, ex_psum, base_used, ex_used = st.event(2), st.event(8), st.event(2), st.event(4)
        with st.block() as block:
            @block.sync
            def _(sp):
                st.heads(sp)

            @block.gpsimd
            def _(pool):
                pool.tensor_tensor(X[:, :, :], X[:, :, :], pair(core.rows[0:S, B_P, :], NB),
                                   ALU.add).then_inc(bias_ready.sem, 1)
                pool.wait_ge(sq_done.sem, sq_done.at(NB * E))
                pool.tensor_tensor(R[:, :, :], R[:, :, :], core.half[:, :].rearrange("s (b e) -> s b e", b=NB),
                                   ALU.pow).then_inc(root_ready.sem, 1)

            @block.tensor
            def _(pe):
                pe.wait_ge(core.loaded["gated"], core.loads["gated"])
                with pe.Fori(0, NB // 2) as i:
                    for j in range(2):
                        b = 2 * i + j
                        pe.wait_ge(xeT_ready.sem, xeT_ready.at(b - 1))
                        for q in range(4):
                            for k in range(KD):
                                ins = pe.matmul(ps[j][:, q * S:(q + 1) * S], w["Vg"][:, k, q * P:(q + 1) * P],
                                                NT[:, k, token(b)], start=k == 0, stop=k == KD - 1)
                        ins.then_inc(xe_psum.sem, 1)
                        pe.wait_ge(xeT_ready.sem, xeT_ready.at(b + 1))
                        for q in range(4):
                            pe.wait_ge(d_ready.sem, d_ready.at(4 * b + q - 3))
                            pe.matmul(ps[2 + q][0:S, :], xeT[j][:, q, :], w["VgT"][:, q, :], start=True,
                                      stop=True).then_inc(d_psum.sem, 1)
                pe.wait_ge(any_ready.sem, 1)
                pe.matmul(ps[6][0:S, 0:1], core.ones[0:S, 0:S], any_over[:, :], start=True,
                          stop=True).then_inc(flag_psum.sem, 1)
                with pe.Fori(0, NB // 2) as i:
                    for j in range(2):
                        b = 2 * i + j
                        pe.wait_ge(wb_ready.sem, b + 1)
                        pe.wait_ge(wt_ready.sem, wt_ready.at(b - 1))
                        pe.transpose(ps[6 + j][0:E, 0:S], wb[j][:, :], core.ident[0:S, 0:S]).then_inc(wt_psum.sem, 1)
                        pe.wait_ge(nts_ready.sem, b + 1)
                        pe.wait_ge(wt_ready.sem, wt_ready.at(b + 1))
                        pe.wait_ge(base_used.sem, base_used.at(b - 1))
                        for k in range(KD):
                            pe.matmul(ps[j][0:S, 0:D], NTs[j][:, k, :], w["Wp"][:, k, :], start=k == 0, stop=False)
                        pe.matmul(ps[j][0:S, 0:D], wT[j][:, :], w["be"][:, :], start=False,
                                  stop=True).then_inc(base_psum.sem, 1)
                        for q in range(4):
                            pe.wait_ge(ex_used.sem, ex_used.at(4 * b + q - 3))
                            for k in range(KD):
                                ins = pe.matmul(ps[2 + q][0:S, :], NTs[j][:, k, :],
                                                w["We"][:, k, q * 512:(q + 1) * 512], start=k == 0, stop=k == KD - 1)
                            ins.then_inc(ex_psum.sem, 1)

            @block.vector
            def _(dve):
                chain = Chain(dve, own)
                with dve.Fori(0, NB // 2) as i:
                    for j in range(2):
                        b = 2 * i + j
                        for q in range(4):
                            dve.wait_ge(d_psum.sem, d_psum.at(4 * b + q + 1))
                            dve.wait_ge(sq_done.sem, sq_done.at(8 * b + 2 * q - 2))
                            dve.tensor_tensor(DF[q % 2][:, :, :], ps[2 + q][0:S, :].rearrange("s (e d) -> s e d", e=2),
                                              N[:, bass.ds(b, 1), :].broadcast_to([S, 2, D]),
                                              ALU.subtract).then_inc(d_ready.sem, 1)
                dve.wait_ge(root_ready.sem, 1)
                chain.step(dve.tensor_reduce(small[:, 0, :], R[:, :, :], AX.X, ALU.min))
                dve.tensor_tensor(R[:, :, :], wide(small[:, 0, :], E), R[:, :, :], ALU.subtract).then_inc(e_in.sem, 1)
                dve.wait_ge(e_ready.sem, 1)
                chain.step(dve.tensor_reduce(small[:, 1, :], RW[:, :, :], AX.X, ALU.add))
                chain.step(dve.reciprocal(small[:, 2, :], small[:, 1, :]))
                chain.step(dve.tensor_tensor(RW[:, :, :], RW[:, :, :], wide(small[:, 2, :], E), ALU.mult))
                top_mask(dve, chain, RW[:, :, :], NB, E, (1, 2), above[:, :, :, :], same[:, :, :, :], rank[:, :, :],
                         (top1[:, :, :], top2[:, :, :]), core.below[:, 0:E, 0:E])
                chain.step(dve.tensor_scalar(over[:, :, :], RW[:, :, :], 1.0 / E, None, ALU.is_gt))
                dve.tensor_reduce(any_over[:, :], over[:, :, :], AX.XY, ALU.max).then_inc(any_ready.sem, 1)
                dve.wait_ge(flag_psum.sem, 1)
                chain.step(dve.tensor_scalar(flag[:, :], ps[6][0:S, 0:1], 0.0, None, ALU.is_gt))
                chain.step(dve.tensor_tensor(over[:, :, :], over[:, :, :], top1[:, :, :], ALU.subtract))
                chain.step(dve.scalar_tensor_tensor(over[:, :, :], over[:, :, :], flag[:, :], top1[:, :, :], ALU.mult,
                                                    ALU.add))
                chain.step(dve.tensor_tensor(over[:, :, :], over[:, :, :], top2[:, :, :], ALU.mult))
                chain.step(dve.tensor_tensor(RW[:, :, :], RW[:, :, :], over[:, :, :], ALU.mult))
                chain.step(dve.tensor_reduce(small[:, 3, :], RW[:, :, :], AX.X, ALU.add))
                chain.step(dve.tensor_scalar(small[:, 4, :], small[:, 3, :], 0.0, None, ALU.is_equal))
                chain.step(dve.tensor_tensor(small[:, 3, :], small[:, 3, :], small[:, 4, :], ALU.add))
                chain.step(dve.reciprocal(small[:, 5, :], small[:, 3, :]))
                chain.step(dve.tensor_tensor(RW[:, :, :], RW[:, :, :], wide(small[:, 5, :], E), ALU.mult))
                dve.wait_ge(bias_ready.sem, 1)
                with dve.Fori(0, NB // 2) as i:
                    chain.loop(i, 8)
                    for j in range(2):
                        b = 2 * i + j
                        dve.wait_ge(wt_psum.sem, wt_psum.at(b - 1))
                        dve.tensor_copy(wb[j][:, :].unsqueeze(1), RW[:, bass.ds(b, 1), :]).then_inc(wb_ready.sem, 1)
                        xb = X[:, bass.ds(b, 1), :]
                        dve.wait_ge(base_psum.sem, base_psum.at(b + 1))
                        dve.tensor_tensor(xb, xb, ps[j][0:S, 0:D].unsqueeze(1), ALU.add).then_inc(base_used.sem, 1)
                        dve.wait_ge(base_used.sem, base_used.at(b + 1))
                        dve.wait_ge(wb_ready.sem, b + 1)
                        for q in range(4):
                            dve.wait_ge(ex_psum.sem, ex_psum.at(4 * b + q + 1))
                            chain.step(dve.scalar_tensor_tensor(
                                xb, ps[2 + q][0:S, 0:D].unsqueeze(1), wb[j][:, 2 * q:2 * q + 1], xb, ALU.mult, ALU.add))
                            dve.scalar_tensor_tensor(
                                xb, ps[2 + q][0:S, D:2 * D].unsqueeze(1), wb[j][:, 2 * q + 1:2 * q + 2], xb, ALU.mult,
                                ALU.add).then_inc(ex_used.sem, 1)
                            dve.wait_ge(ex_used.sem, ex_used.at(4 * b + q + 1))
                chain.end(NB // 2)

            @block.scalar
            def _(act):
                with act.Fori(0, NB // 2) as i:
                    for j in range(2):
                        b = 2 * i + j
                        act.wait_ge(xe_psum.sem, b + 1)
                        act.wait_ge(d_psum.sem, d_psum.at(4 * (b - 1)))
                        act.activation(xeT[j][:, :, :], ps[j][:, 0:4 * S].rearrange("p (q s) -> p q s", q=4),
                                       ACT.Copy).then_inc(xeT_ready.sem, 1)
                        for q in range(4):
                            act.wait_ge(d_ready.sem, d_ready.at(4 * b + q + 1))
                            for c in range(2):
                                act.activation(DF[q % 2][:, c, :], DF[q % 2][:, c, :], ACT.Square,
                                               accum_out=R[:, bass.ds(b, 1), 2 * q + c]).then_inc(sq_done.sem, 1)
                act.wait_ge(e_in.sem, 1)
                act.activation(RW[:, :, :], R[:, :, :], ACT.Exp).then_inc(e_ready.sem, 1)
                with act.Fori(0, NB // 2) as i:
                    for j in range(2):
                        b = 2 * i + j
                        act.wait_ge(ex_psum.sem, ex_psum.at(4 * (b - 1)))
                        act.activation(NTs[j][:, :, :], NT[:, :, token(b)], ACT.Copy).then_inc(nts_ready.sem, 1)
                        act.wait_ge(wt_psum.sem, wt_psum.at(b + 1))
                        act.activation(wT[j][:, :], ps[6 + j][0:E, 0:S], ACT.Copy).then_inc(wt_ready.sem, 1)


LAG_T, LAG_V = 3, 5
ROUND = 4


def head64_attention(core, io):
    X, N, NT, ps = core.X, core.N, core.NT, core.ps
    w = core.weights
    with Stage(core) as st:
        ctT = [st.sb(f"ctT{j}", [P, KD, KVP]) for j in range(2)]
        QH = [st.sb(f"QH{c}", [P, 8, S]) for c in range(2)]
        KTr = st.sb("KTr", [P, 8, KVP])
        V = st.sb("V", [KT, NKT, 1024])
        A = [st.sb(f"A{c}", [S, KVP]) for c in range(4)]
        AT = [st.sb(f"AT{c}", [KT, NKT, 2, S]) for c in range(2)]
        OT = st.sb("OT", [P, 8, S])
        O = st.sb("O", [S, D])
        bq8 = st.sb("bq8", [P, 8])
        neg_max, total, inv = st.sb("neg_max", [S, 4]), st.sb("total", [S, 4]), st.sb("inv", [S, 4])
        stats, mv, rstd = st.sb("stats", [S, 1, 6]), st.sb("mv", [S, 3]), st.sb("rstd", [S, 1])
        ctx_loaded = [st.event(), st.event()]
        zeroed, rows_added = st.event(), st.event()
        q_psum, q_ready, k_psum, k_ready, v_psum, v_ready = (st.event(8) for _ in range(6))
        s_psum, max_ready, exp_ready, norm_ready, at_psum, at_ready = (st.event(4) for _ in range(6))
        av_psum, ot_ready, o_psum, o_used, var_ready, rstd_ready, own, x_ready = \
            st.event(2), st.event(4), st.event(1), st.event(1), st.event(), st.event(), st.event(), st.event()
        with st.block() as block:
            @block.sync
            def _(sp):
                st.heads(sp)
                with sp.Fori(0, NB // 2) as i:
                    for j in range(2):
                        b = 2 * i + j
                        sp.wait_ge(v_psum.sem, v_psum.at(6 * b - 6))
                        sp.dma_start(ctT[j][:, :, :], io["ctT"][bass.ds(b, 1)]).then_inc(ctx_loaded[j].sem, 16)

            @block.gpsimd
            def _(pool):
                pool.memset(QH[0][64:P, :, :], 0.0).then_inc(zeroed.sem, 1)
                pool.memset(QH[1][0:64, :, :], 0.0).then_inc(zeroed.sem, 1)
                pool.wait_ge(zeroed.sem, 2)
                for c in range(4):
                    pool.memset(A[c][:, KV:KVP], 0.0).then_inc(zeroed.sem, 1)
                pool.tensor_tensor(N[:, :, :], N[:, :, :], pair(core.rows[0:S, L1_BO, :], NB),
                                   ALU.add).then_inc(rows_added.sem, 1)
                pool.tensor_tensor(X[:, :, :], X[:, :, :], pair(core.rows[0:S, BETA, :], NB),
                                   ALU.add).then_inc(rows_added.sem, 1)
                with pool.Fori(0, NB) as b:
                    pool.wait_ge(var_ready.sem, b + 1)
                    pool.tensor_tensor(rstd[:, :], mv[:, 1:2], core.minus_half[:, 0:1], ALU.pow).then_inc(rstd_ready.sem, 1)

            def bank_free(eng, b, u):
                if u < 4:
                    eng.wait_ge(exp_ready.sem, exp_ready.at(NH * b + u - 3))
                elif u < 6:
                    eng.wait_ge(q_ready.sem, q_ready.at(4 * b + 2 * (u - 3)))
                elif u < 14:
                    eng.wait_ge(k_ready.sem, k_ready.at(8 * b + u - 5))
                elif u < 20:
                    eng.wait_ge(v_ready.sem, v_ready.at(6 * b + u - 13))
                else:
                    eng.wait_ge(exp_ready.sem, exp_ready.at(NH * b + u - 19))

            @block.tensor
            def _(pe):
                pe.wait_ge(core.loaded["head64"], core.loads["head64"])
                pe.wait_ge(zeroed.sem, 6)

                def query(b, u):
                    bank_free(pe, b, u)
                    for c in range(4):
                        t = 4 * u + c
                        for k in range(KD):
                            ins = pe.matmul(ps[u % 4][:, c * S:(c + 1) * S], w["Wq"][:, k, t * P:(t + 1) * P],
                                            NT[:, k, token(b)], start=k == 0, stop=k == KD - 1)
                    ins.then_inc(q_psum.sem, 1)

                def key(b, j, i, t):
                    u = 2 + t
                    if t == 0:
                        pe.wait_ge(ctx_loaded[j].sem, 16 * (i + 1))
                    bank_free(pe, b, u)
                    for k in range(KD):
                        ins = pe.matmul(ps[u % 4][:, 0:KV], w["Wk"][:, k, t * P:(t + 1) * P], ctT[j][:, k, 0:KV],
                                        start=k == 0, stop=k == KD - 1)
                    ins.then_inc(k_psum.sem, 1)

                def run(b, j, i, more):
                    for t in range(NKT):
                        for c in range(2):
                            u = 10 + 2 * t + c
                            bank_free(pe, b, u)
                            for k in range(KD):
                                ins = pe.matmul(ps[u % 4][0:KT, :], ctT[j][:, k, t * KT:(t + 1) * KT],
                                                w["Wv"][:, k, 512 * c:512 * (c + 1)], start=k == 0, stop=k == KD - 1)
                            ins.then_inc(v_psum.sem, 1)
                    for h in range(NH + LAG_V + 1):
                        if h < NH:
                            u = 16 + h
                            bank_free(pe, b, u)
                            if h == 0:
                                pe.wait_ge(q_ready.sem, q_ready.at(4 * b + 4))
                            pe.wait_ge(k_ready.sem, k_ready.at(8 * b + h // 2 + 1))
                            pe.matmul(ps[u % 4][0:S, 0:KV], QH[h % 2][:, h // 2, :], KTr[:, h // 2, 0:KV],
                                      start=True, stop=True).then_inc(s_psum.sem, 1)
                        g = h - LAG_T
                        if 0 <= g < NH:
                            pe.wait_ge(norm_ready.sem, norm_ready.at(NH * b + g + 1))
                            pe.wait_ge(at_ready.sem, at_ready.at(NH * b + g - 1))
                            for t in range(NKT):
                                ins = pe.transpose(ps[4 + g % 2][0:KT, t * S:(t + 1) * S],
                                                   A[g % 4][:, t * KT:(t + 1) * KT], core.ident[0:S, 0:S])
                            ins.then_inc(at_psum.sem, 1)
                        g = h - LAG_V
                        if 0 <= g < NH and g % 2:
                            m = g // 2
                            pe.wait_ge(at_ready.sem, at_ready.at(NH * b + g + 1))
                            pe.wait_ge(v_ready.sem, v_ready.at(6 * b + 6))
                            pe.wait_ge(ot_ready.sem, ot_ready.at(16 * b + 2 * m - 2))
                            if m == 0:
                                pe.wait_ge(o_used.sem, o_used.at(b))
                            for t in range(NKT):
                                ins = pe.matmul(ps[6 + m % 2][:, 0:2 * S], V[:, t, m * P:(m + 1) * P],
                                                AT[m % 2][:, t, :, :].rearrange("p c s -> p (c s)"), start=t == 0,
                                                stop=t == NKT - 1)
                            ins.then_inc(av_psum.sem, 1)
                        if more and h == NH:
                            query(b + 1, 0)
                            query(b + 1, 1)
                        if more and NH < h <= NH + 4:
                            key(b + 1, 1 - j, i + j, 2 * (h - NH) - 2)
                            key(b + 1, 1 - j, i + j, 2 * (h - NH) - 1)
                    pe.wait_ge(ot_ready.sem, ot_ready.at(16 * b + 16))
                    for t in range(8):
                        ins = pe.matmul(ps[6][0:S, 0:D], OT[:, t, :], w["Wo"][:, t, :], start=t == 0, stop=t == 7)
                    ins.then_inc(o_psum.sem, 1)

                query(0, 0)
                query(0, 1)
                for t in range(8):
                    key(0, 0, 0, t)
                batches(pe, run)

            @block.vector
            def _(dve):
                chain = Chain(dve, own)
                dve.wait_ge(core.loaded["head64"], core.loads["head64"])
                dve.wait_ge(zeroed.sem, 6)
                dve.wait_ge(rows_added.sem, 2)
                chain.step(dve.tensor_scalar(bq8[:, :], w["bq"][:, :], 0.125, None, ALU.mult))

                def query(b):
                    for u in range(2):
                        dve.wait_ge(q_psum.sem, q_psum.at(2 * b + u + 1))
                        if u == 0:
                            dve.wait_ge(s_psum.sem, s_psum.at(NH * b))
                        for c in range(2):
                            half = slice(64 * c, 64 * c + 64)
                            dve.scalar_tensor_tensor(
                                QH[c][half, 4 * u:4 * u + 4, :],
                                ps[u][half, 0:4 * S].rearrange("p (q s) -> p q s", q=4), 0.125,
                                wide(bq8[half, 4 * u:4 * u + 4], S), ALU.mult, ALU.add).then_inc(q_ready.sem, 1)

                def run(b, j, i, more):
                    for t in range(6):
                        dve.wait_ge(v_psum.sem, v_psum.at(6 * b + t + 1))
                        if t == 0:
                            dve.wait_ge(av_psum.sem, av_psum.at(8 * b))
                        dve.tensor_copy(V[:, t // 2, 512 * (t % 2):512 * (t % 2) + 512],
                                        ps[(10 + t) % 4][0:KT, :]).then_inc(v_ready.sem, 1)
                    for h in range(NH + LAG_V + 2):
                        if h < NH:
                            dve.wait_ge(s_psum.sem, s_psum.at(NH * b + h + 1))
                            dve.tensor_reduce(neg_max[:, h % 4:h % 4 + 1], ps[(16 + h) % 4][0:S, 0:KV], AX.X,
                                              ALU.max, negate=True).then_inc(max_ready.sem, 1)
                        g = h - 1
                        if 0 <= g < NH:
                            dve.wait_ge(exp_ready.sem, exp_ready.at(NH * b + g + 1))
                            chain.step(dve.reciprocal(inv[:, g % 4:g % 4 + 1], total[:, g % 4:g % 4 + 1]))
                            dve.tensor_scalar(A[g % 4][:, 0:KV], A[g % 4][:, 0:KV], inv[:, g % 4:g % 4 + 1], None,
                                              ALU.mult).then_inc(norm_ready.sem, 1)
                        g = h - LAG_V - 1
                        if 0 <= g < NH and g % 2:
                            m = g // 2
                            dve.wait_ge(av_psum.sem, av_psum.at(8 * b + m + 1))
                            if m == 0:
                                dve.wait_ge(o_psum.sem, o_psum.at(b))
                            for c in range(2):
                                half = slice(64 * c, 64 * c + 64)
                                dve.tensor_scalar(OT[half, m, :], ps[6 + m % 2][half, c * S:(c + 1) * S],
                                                  w["bv"][half, m:m + 1], None, ALU.add).then_inc(ot_ready.sem, 1)
                        if more and h == NH + 1:
                            query(b + 1)
                    dve.wait_ge(o_psum.sem, o_psum.at(b + 1))
                    dve.tensor_tensor(O[:, :], ps[6][0:S, 0:D], N[:, bass.ds(b, 1), :], ALU.add).then_inc(o_used.sem, 1)
                    dve.wait_ge(o_used.sem, o_used.at(b + 1))
                    chain.step(dve.bn_stats(stats[:, 0, :], O[:, :]))
                    variance(dve, chain, stats[:, :, :], mv[:, 0:1], mv[:, 2:3], mv[:, 1:2]).then_inc(var_ready.sem, 1)
                    chain.step(dve.tensor_scalar(mv[:, 0:1], mv[:, 0:1], 0.5, None, ALU.mult))
                    dve.wait_ge(rstd_ready.sem, b + 1)
                    chain.step(dve.tensor_scalar(O[:, :], O[:, :], mv[:, 0:1], rstd[:, :], ALU.subtract, ALU.mult))
                    dve.tensor_tensor(O[:, :], O[:, :], core.rows[0:S, GAMMA, :], ALU.mult).then_inc(x_ready.sem, 1)
                    dve.wait_ge(x_ready.sem, 2 * b + 1)
                    xb = X[:, bass.ds(b, 1), :]
                    dve.tensor_tensor(xb, xb, O[:, :].unsqueeze(1), ALU.add).then_inc(x_ready.sem, 1)
                    dve.wait_ge(x_ready.sem, 2 * b + 2)

                query(0)
                batches(dve, run, chain, NH + 8)

            @block.scalar
            def _(act):
                act.wait_ge(core.loaded["head64"], core.loads["head64"])

                def key(b, t):
                    act.wait_ge(k_psum.sem, k_psum.at(8 * b + t + 1))
                    if t == 0:
                        act.wait_ge(s_psum.sem, s_psum.at(NH * b))
                    act.activation(KTr[:, t, 0:KV], ps[(2 + t) % 4][:, 0:KV], ACT.Identity,
                                   bias=w["bk"][:, t:t + 1]).then_inc(k_ready.sem, 1)

                def run(b, j, i, more):
                    for h in range(NH + LAG_T + 2):
                        if h < NH:
                            act.wait_ge(max_ready.sem, max_ready.at(NH * b + h + 1))
                            act.wait_ge(at_psum.sem, at_psum.at(NH * b + h - 3))
                            act.activation(A[h % 4][:, 0:KV], ps[(16 + h) % 4][0:S, 0:KV], ACT.Exp,
                                           bias=neg_max[:, h % 4:h % 4 + 1],
                                           accum_out=total[:, h % 4:h % 4 + 1]).then_inc(exp_ready.sem, 1)
                        g = h - LAG_T
                        if 0 <= g < NH:
                            act.wait_ge(at_psum.sem, at_psum.at(NH * b + g + 1))
                            act.wait_ge(av_psum.sem, av_psum.at(8 * b + g // 2 - 1))
                            act.activation(AT[g // 2 % 2][:, :, g % 2, :],
                                           ps[4 + g % 2][0:KT, 0:NKT * S].rearrange("p (t s) -> p t s", t=NKT),
                                           ACT.Copy).then_inc(at_ready.sem, 1)
                        if more and NH < h <= NH + 4:
                            key(b + 1, 2 * (h - NH) - 2)
                            key(b + 1, 2 * (h - NH) - 1)

                for t in range(8):
                    key(0, t)
                batches(act, run)


def ternary_ffn(core, io):
    X, N, NT, ps = core.X, core.N, core.NT, core.ps
    HT = 8
    with Stage(core) as st:
        w1, w2 = st.sb("w1", [P, KD, 1024]), st.sb("w2", [P, HT, D])
        conv_w, conv_b = st.sb("conv_w", [P, HT, 3]), st.sb("conv_b", [P, HT])
        w1q, w2q = st.sb("w1q", [P, KD, 1024], BF16), st.sb("w2q", [P, HT, D], BF16)
        part = st.sb("part", [P, 2])
        wmean, winv = st.sb("wmean", [P, 2]), st.sb("winv", [P, 2])
        am, scale, inv, inv2 = (st.sb(n, [S, NB]) for n in ("am", "scale", "inv", "inv2"))
        am2, scale2 = st.sb("am2", [S, 4]), st.sb("scale2", [S, 1])
        tmp = st.sb("tmp", [S, D])
        Q = [st.sb(f"Q{j}", [S, D], BF16) for j in range(2)]
        QT = [st.sb(f"QT{j}", [P, KD, S], BF16) for j in range(2)]
        inv_rows = st.sb("inv_rows", [P, T])
        HP = st.sb("HP", [P, HT, S + 2])
        C = [st.sb(f"C{j}", [P, HT, S]) for j in range(2)]
        tmp2 = st.sb("tmp2", [S, 1024])
        Q2 = st.sb("Q2", [S, 1024], BF16)
        Q2T = [st.sb(f"Q2T{j}", [P, HT, S], BF16) for j in range(2)]
        w_loaded, c_loaded, own, own_pool, part_ready, mean_psum, w_ready, pads, inv_ready = (st.event() for _ in range(9))
        q_ready, qt_psum, qt_ready, rows_psum, h_psum, hp_ready = (st.event(4) for _ in range(6))
        rows_ready = st.event()
        c_ready, conv_ready, silu_ready, ht_psum, q2_ready, q2t_psum, q2t_ready, y_psum, x_ready = \
            (st.event(4) for _ in range(9))
        amax_ready, q2_used = st.event(2), st.event(2)
        with st.block() as block:
            @block.sync
            def _(sp):
                st.heads(sp)
                sp.dma_start(w1[:, :, :], io["w1"]).then_inc(w_loaded.sem, 16)
                sp.dma_start(w2[:, :, :], io["w2"]).then_inc(w_loaded.sem, 16)
                sp.dma_start(conv_w[:, :, :], io["conv_w"]).then_inc(c_loaded.sem, 16)
                sp.dma_start(conv_b[:, :], io["conv_b"]).then_inc(c_loaded.sem, 16)

            @block.gpsimd
            def _(pool):
                pool.memset(HP[:, :, 0:1], 0.0).then_inc(pads.sem, 1)
                pool.memset(HP[:, :, S + 1:S + 2], 0.0).then_inc(pads.sem, 1)

            @block.tensor
            def _(pe):
                pe.wait_ge(part_ready.sem, 2)
                pe.matmul(ps[7][:, 0:2], core.ones[:, :], part[:, :], start=True, stop=True).then_inc(mean_psum.sem, 1)
                pe.wait_ge(w_ready.sem, 2)
                pe.wait_ge(inv_ready.sem, 1)
                for b in range(NB):
                    ins = pe.matmul(ps[4 + b // 4][:, (b % 4) * S:(b % 4 + 1) * S],
                                    inv[:, b:b + 1].broadcast_to([S, P]), core.ident[0:S, 0:S], start=True, stop=True)
                ins.then_inc(rows_psum.sem, 1)
                pe.wait_ge(rows_ready.sem, 2)
                with pe.Fori(0, NB // 2) as i:
                    for j in range(2):
                        b = 2 * i + j
                        pe.wait_ge(q_ready.sem, q_ready.at(b + 1))
                        pe.wait_ge(qt_ready.sem, qt_ready.at(b))
                        for k in range(KD):
                            ins = pe.transpose(ps[0][:, :].bitcast(BF16)[:, k * S:(k + 1) * S], Q[j][:, k * P:(k + 1) * P],
                                               core.identb[0:S, 0:S])
                        ins.then_inc(qt_psum.sem, 1)
                        pe.wait_ge(qt_ready.sem, qt_ready.at(b + 1))
                        pe.wait_ge(hp_ready.sem, hp_ready.at(2 * b))
                        for t in range(HT):
                            for k in range(KD):
                                ins = pe.matmul(ps[2 + t // 4][:, (t % 4) * S:(t % 4 + 1) * S],
                                                w1q[:, k, t * P:(t + 1) * P], QT[j][:, k, :], start=k == 0, stop=k == KD - 1)
                            if t % 4 == 3:
                                ins.then_inc(h_psum.sem, 1)
                        pe.wait_ge(silu_ready.sem, silu_ready.at(b + 1))
                        pe.wait_ge(q2_used.sem, q2_used.at(2 * b))
                        for t in range(HT):
                            ins = pe.transpose(ps[4 + t // 4][0:S, (t % 4) * P:(t % 4 + 1) * P], C[j][:, t, :],
                                               core.ident[:, :])
                            if t % 4 == 3:
                                ins.then_inc(ht_psum.sem, 1)
                        pe.wait_ge(q2_ready.sem, q2_ready.at(b + 1))
                        pe.wait_ge(q2t_ready.sem, q2t_ready.at(b))
                        for t in range(HT):
                            ins = pe.transpose(ps[6][:, :].bitcast(BF16)[:, t * S:(t + 1) * S], Q2[:, t * P:(t + 1) * P],
                                               core.identb[0:S, 0:S])
                        ins.then_inc(q2t_psum.sem, 1)
                        pe.wait_ge(q2t_ready.sem, q2t_ready.at(b + 1))
                        pe.wait_ge(x_ready.sem, x_ready.at(b))
                        for t in range(HT):
                            ins = pe.matmul(ps[7][0:S, 0:D], Q2T[j][:, t, :], w2q[:, t, :], start=t == 0, stop=t == HT - 1)
                        ins.then_inc(y_psum.sem, 1)

            @block.vector
            def _(dve):
                chain = Chain(dve, own)
                dve.wait_ge(w_loaded.sem, 32)
                for n, wt in enumerate((w1, w2)):
                    dve.tensor_reduce(part[:, n:n + 1], wt[:, :, :], AX.XY, ALU.add,
                                      apply_absolute_value=True).then_inc(part_ready.sem, 1)
                dve.wait_ge(mean_psum.sem, 1)
                chain.step(dve.tensor_scalar(wmean[:, :], ps[7][:, 0:2], 1.0 / (D * 1024), 1e-5, ALU.mult, ALU.max))
                chain.step(dve.reciprocal(winv[:, :], wmean[:, :]))
                for n, (wt, wq) in enumerate(((w1, w1q), (w2, w2q))):
                    chain.step(dve.tensor_scalar(wt[:, :, :], wt[:, :, :], winv[:, n:n + 1], MAGIC, ALU.mult, ALU.add))
                    chain.step(dve.tensor_scalar(wt[:, :, :], wt[:, :, :], MAGIC - 1, MAGIC + 1, ALU.max, ALU.min))
                    dve.tensor_scalar(wq[:, :, :], wt[:, :, :], MAGIC, None, ALU.subtract).then_inc(w_ready.sem, 1)
                chain.step(dve.tensor_reduce(am[:, :], N[:, :, :], AX.X, ALU.max, apply_absolute_value=True))
                chain.step(dve.tensor_scalar(am[:, :], am[:, :], 1e-5, None, ALU.max))
                chain.step(dve.reciprocal(scale[:, :], am[:, :]))
                chain.step(dve.tensor_scalar(scale[:, :], scale[:, :], 127.0, None, ALU.mult))
                dve.tensor_scalar(inv[:, :], am[:, :], wmean[0:S, 0:1], 1.0 / 127, ALU.mult, ALU.mult).then_inc(inv_ready.sem, 1)
                dve.wait_ge(c_loaded.sem, 32)
                dve.wait_ge(pads.sem, 2)
                dve.wait_ge(rows_ready.sem, 2)
                with dve.Fori(0, NB // 2) as i:
                    chain.loop(i, 2 * (HT + 9))
                    for j in range(2):
                        b = 2 * i + j
                        sc = scale[:, bass.ds(b, 1)]
                        chain.step(dve.tensor_scalar(tmp[:, :].unsqueeze(1), N[:, bass.ds(b, 1), :], sc, MAGIC, ALU.mult,
                                                     ALU.add))
                        chain.step(dve.tensor_scalar(tmp[:, :], tmp[:, :], MAGIC - 128, MAGIC + 127, ALU.max, ALU.min))
                        dve.wait_ge(qt_psum.sem, qt_psum.at(b - 1))
                        dve.tensor_scalar(Q[j][:, :], tmp[:, :], MAGIC, None, ALU.subtract).then_inc(q_ready.sem, 1)
                        for u in range(2):
                            dve.wait_ge(h_psum.sem, h_psum.at(2 * b + u + 1))
                            dve.tensor_tensor(HP[:, 4 * u:4 * u + 4, 1:S + 1],
                                              ps[2 + u][:, 0:4 * S].rearrange("p (t s) -> p t s", t=4), pair(inv_rows[:, token(b)], 4),
                                              ALU.mult).then_inc(hp_ready.sem, 1)
                        for t in range(HT):
                            dve.wait_ge(c_ready.sem, c_ready.at(8 * b + t + 1))
                            chain.step(dve.scalar_tensor_tensor(C[j][:, t, :], HP[:, t, 1:S + 1], conv_w[:, t, 1:2],
                                                                C[j][:, t, :], ALU.mult, ALU.add))
                            dve.scalar_tensor_tensor(C[j][:, t, :], HP[:, t, 2:S + 2], conv_w[:, t, 2:3], C[j][:, t, :],
                                                     ALU.mult, ALU.add).then_inc(conv_ready.sem, 1)
                        for u in range(2):
                            dve.wait_ge(ht_psum.sem, ht_psum.at(2 * b + u + 1))
                            dve.tensor_reduce(am2[:, u:u + 1], ps[4 + u][0:S, :], AX.X, ALU.max,
                                              apply_absolute_value=True).then_inc(amax_ready.sem, 1)
                        dve.wait_ge(amax_ready.sem, amax_ready.at(2 * b + 2))
                        chain.step(dve.tensor_tensor(am2[:, 2:3], am2[:, 0:1], am2[:, 1:2], ALU.max))
                        chain.step(dve.tensor_scalar(am2[:, 2:3], am2[:, 2:3], 1e-5, None, ALU.max))
                        chain.step(dve.reciprocal(scale2[:, :], am2[:, 2:3]))
                        chain.step(dve.tensor_scalar(scale2[:, :], scale2[:, :], 127.0, None, ALU.mult))
                        chain.step(dve.tensor_scalar(am2[:, 3:4], am2[:, 2:3], wmean[0:S, 1:2], 1.0 / 127, ALU.mult, ALU.mult))
                        for u in range(2):
                            dve.tensor_scalar(tmp2[:, 512 * u:512 * u + 512], ps[4 + u][0:S, :], scale2[:, :], MAGIC,
                                              ALU.mult, ALU.add).then_inc(q2_used.sem, 1)
                        dve.wait_ge(q2_used.sem, q2_used.at(2 * b + 2))
                        chain.step(dve.tensor_scalar(tmp2[:, :], tmp2[:, :], MAGIC - 128, MAGIC + 127, ALU.max, ALU.min))
                        dve.wait_ge(q2t_psum.sem, q2t_psum.at(b))
                        dve.tensor_scalar(Q2[:, :], tmp2[:, :], MAGIC, None, ALU.subtract).then_inc(q2_ready.sem, 1)
                        dve.wait_ge(y_psum.sem, y_psum.at(b + 1))
                        xb = X[:, bass.ds(b, 1), :]
                        chain.step(dve.tensor_scalar(tmp[:, :], ps[7][0:S, 0:D], am2[:, 3:4], None, ALU.mult))
                        dve.tensor_tensor(xb, xb, tmp[:, :].unsqueeze(1), ALU.add).then_inc(x_ready.sem, 1)
                        dve.wait_ge(x_ready.sem, x_ready.at(b + 1))
                chain.end(NB // 2)

            @block.scalar
            def _(act):
                act.wait_ge(rows_psum.sem, rows_psum.at(1))
                for u in range(2):
                    act.activation(inv_rows[:, 4 * u * S:4 * (u + 1) * S], ps[4 + u][:, 0:4 * S],
                                   ACT.Copy).then_inc(rows_ready.sem, 1)
                act.wait_ge(c_loaded.sem, 32)
                with act.Fori(0, NB // 2) as i:
                    for j in range(2):
                        b = 2 * i + j
                        act.wait_ge(qt_psum.sem, qt_psum.at(b + 1))
                        act.wait_ge(h_psum.sem, h_psum.at(2 * b - 2))
                        act.activation(QT[j][:, :, :], ps[0][:, :].bitcast(BF16)[:, 0:KD * S].rearrange(
                            "p (k s) -> p k s", k=KD), ACT.Copy).then_inc(qt_ready.sem, 1)
                        for t in range(HT):
                            if t % 4 == 0:
                                act.wait_ge(hp_ready.sem, hp_ready.at(2 * b + t // 4 + 1))
                            if t == 0:
                                act.wait_ge(ht_psum.sem, ht_psum.at(2 * b - 2))
                            act.activation(C[j][:, t, :], HP[:, t, 0:S], ACT.Identity, scale=conv_w[:, t, 0:1],
                                           bias=conv_b[:, t:t + 1]).then_inc(c_ready.sem, 1)
                        act.wait_ge(conv_ready.sem, conv_ready.at(8 * b + 8))
                        act.activation(C[j][:, :, :], C[j][:, :, :], ACT.Silu).then_inc(silu_ready.sem, 1)
                        act.wait_ge(q2t_psum.sem, q2t_psum.at(b + 1))
                        act.wait_ge(y_psum.sem, y_psum.at(b - 1))
                        act.activation(Q2T[j][:, :, :], ps[6][:, :].bitcast(BF16)[:, 0:HT * S].rearrange(
                            "p (t s) -> p t s", t=HT), ACT.Copy).then_inc(q2t_ready.sem, 1)


def heads16(core, io, layer):
    X, N, NT, ps = core.X, core.N, core.NT, core.ps
    soft = layer == 2
    w = core.weights
    NHT = 8
    with Stage(core) as st:
        ctT = [st.sb(f"ctT{j}", [P, KD, KVP]) for j in range(2)]
        Kt = st.sb("Kt", [P, KD, KVP])
        Qz = st.sb("Qz", [P, KD, NHT, S])
        Vz = st.sb("Vz", [KT, NKT * KD * NHT * P + P])
        OT = [st.sb(f"OT{j}", [P, KD, S]) for j in range(2)]

        def v_blocks(t, k):
            at = (t * KD + k) * NHT * P
            return Vz[:, at:at + NHT * (P + 16)].rearrange("p (h e) -> p h e", e=P + 16)[:, :, 0:16]

        def v_head(t, h, rows=KT):
            at = (t * NH + h) * P
            return Vz[0:rows, at:at + P]

        loaded, ctx_loaded, mask_loaded = st.event(), [st.event(), st.event()], [st.event(), st.event()]
        zeroed, own = st.event(), st.event()
        q_psum, q_ready, k_psum, k_ready, v_psum, v_ready = (st.event(8) for _ in range(6))
        s_psum, max_ready, exp_ready, norm_ready, at_psum, at_ready = (st.event(4) for _ in range(6))
        masked, mask_ready = st.event(4), st.event(4)
        av_psum, ot_ready, o_psum, x_ready = (st.event(4) for _ in range(4))
        if soft:
            mask_i = [st.sb(f"mask_i{j}", [S, KV], I32) for j in range(2)]
            mask = [st.sb(f"mask{j}", [S, KV]) for j in range(2)]
            A = [st.sb(f"A{c}", [S, KVP]) for c in range(4)]
            AT = [st.sb(f"AT{c}", [KT, NKT, 2, S]) for c in range(2)]
            neg_max, total, inv = st.sb("neg_max", [S, 4]), st.sb("total", [S, 4]), st.sb("inv", [S, 4])
            wh, wo = st.sb("W_heads", [P, P]), st.sb("W_o", [P, KD, D])
        else:
            AS = st.sb("AS", [KT, NKT, NH, S])
            wq, wk, wv, wo = (st.sb(n, [P, KD, D]) for n in ("Wq", "Wk", "Wv", "Wo"))
            bq, bk = st.sb("bq", [P, KD]), st.sb("bk", [P, KD])

        with st.block() as block:
            @block.sync
            def _(sp):
                st.heads(sp)
                if soft:
                    sp.dma_start(wh[:, :], io["W_heads"]).then_inc(loaded.sem, 16)
                    sp.dma_start(wo[:, :, :], io["W_o"]).then_inc(loaded.sem, 16)
                else:
                    for name, t in (("L3_Wq", wq), ("L3_Wk", wk), ("L3_Wv", wv), ("L3_Wo", wo)):
                        sp.dma_start(t[:, :, :], io[name]).then_inc(loaded.sem, 16)
                    for name, t in (("L3_bq", bq), ("L3_bk", bk)):
                        sp.dma_start(t[:, :], io[name]).then_inc(loaded.sem, 16)
                with sp.Fori(0, NB // 2) as i:
                    for j in range(2):
                        b = 2 * i + j
                        sp.wait_ge(v_psum.sem, v_psum.at(4 * b - 4))
                        sp.dma_start(ctT[j][:, :, :], io["ctT"][bass.ds(b, 1)]).then_inc(ctx_loaded[j].sem, 16)
                        if soft:
                            sp.wait_ge(mask_ready.sem, mask_ready.at(b - 1))
                            sp.dma_start(mask_i[j][:, :], io["mask"][bass.ds(b, 1)]).then_inc(mask_loaded[j].sem, 16)

            @block.gpsimd
            def _(pool):
                pool.memset(Vz[:, :], 0.0).then_inc(zeroed.sem, 1)
                pool.wait_ge(zeroed.sem, 1)
                if not soft:
                    pool.tensor_tensor(X[:, :, :], X[:, :, :], pair(core.rows[0:S, L3_BO, :], NB),
                                       ALU.add).then_inc(zeroed.sem, 1)
                else:
                    for c in range(4):
                        pool.memset(A[c][:, KV:KVP], 0.0).then_inc(zeroed.sem, 1)

            heads_zeroed = 5 if soft else 2

            def bank_free(eng, b, u):
                n = NH if soft else 12
                if u < 4:
                    eng.wait_ge(exp_ready.sem, exp_ready.at(n * b + u - 3))
                elif u < 6:
                    eng.wait_ge(q_ready.sem, q_ready.at(2 * b + u - 3))
                elif u < 8:
                    eng.wait_ge(k_ready.sem, k_ready.at(2 * b + u - 5))
                elif u < 12:
                    eng.wait_ge(v_ready.sem, v_ready.at(4 * b + u - 7))
                else:
                    eng.wait_ge(exp_ready.sem, exp_ready.at(n * b + u - 11))

            V_USES = [[(0, 0), (0, 1)], [(0, 2)], [(1, 0), (1, 1)], [(1, 2)]]

            @block.tensor
            def _(pe):
                pe.wait_ge(loaded.sem, 32 if soft else 96)
                pe.wait_ge(zeroed.sem, heads_zeroed)

                def queries_and_keys(b, j, i):
                    pe.wait_ge(ctx_loaded[j].sem, 16 * (i + 1))
                    for m in range(KD):
                        bank_free(pe, b, m)
                        if soft:
                            ins = pe.matmul(ps[m][:, 0:S], wh[:, :], NT[:, m, token(b)], start=True, stop=True)
                        else:
                            for k in range(KD):
                                ins = pe.matmul(ps[m][:, 0:S], wq[:, k, m * P:(m + 1) * P], NT[:, k, token(b)],
                                                start=k == 0, stop=k == KD - 1)
                        ins.then_inc(q_psum.sem, 1)
                    for m in range(KD):
                        bank_free(pe, b, 2 + m)
                        if soft:
                            ins = pe.matmul(ps[2 + m][:, 0:KVP], wh[:, :], ctT[j][:, m, :], start=True, stop=True)
                        else:
                            for k in range(KD):
                                ins = pe.matmul(ps[2 + m][:, 0:KVP], wk[:, k, m * P:(m + 1) * P], ctT[j][:, k, :],
                                                start=k == 0, stop=k == KD - 1)
                        ins.then_inc(k_psum.sem, 1)
                def run(b, j, i, more):
                    for c, tiles in enumerate(V_USES):
                        bank_free(pe, b, 4 + c)
                        for n, (m, t) in enumerate(tiles):
                            out = ps[c][0:KT, n * P:(n + 1) * P]
                            rows = slice(t * KT, (t + 1) * KT)
                            if soft:
                                ins = pe.matmul(out, ctT[j][:, m, rows], wh[:, :], start=True, stop=True)
                            else:
                                for k in range(KD):
                                    ins = pe.matmul(out, ctT[j][:, k, rows], wv[:, k, m * P:(m + 1) * P],
                                                    start=k == 0, stop=k == KD - 1)
                        ins.then_inc(v_psum.sem, 1)
                    if soft:
                        for h in range(NH + LAG_V + 1):
                            if h < NH:
                                u = 8 + h
                                bank_free(pe, b, u)
                                pe.wait_ge(q_ready.sem, q_ready.at(2 * b + h // 8 + 1))
                                pe.wait_ge(k_ready.sem, k_ready.at(2 * b + h // 8 + 1))
                                pe.matmul(ps[u % 4][0:S, 0:KV], Qz[:, h // 8, h % 8, :], Kt[:, h // 8, 0:KV],
                                          start=True, stop=True).then_inc(s_psum.sem, 1)
                            g = h - LAG_T
                            if 0 <= g < NH:
                                pe.wait_ge(norm_ready.sem, norm_ready.at(NH * b + g + 1))
                                pe.wait_ge(at_ready.sem, at_ready.at(NH * b + g - 1))
                                for t in range(NKT):
                                    ins = pe.transpose(ps[4 + g % 2][0:KT, t * S:(t + 1) * S],
                                                       A[g % 4][:, t * KT:(t + 1) * KT], core.ident[0:S, 0:S])
                                ins.then_inc(at_psum.sem, 1)
                            g = h - LAG_V
                            if 0 <= g < NH:
                                pe.wait_ge(at_ready.sem, at_ready.at(NH * b + g + 1))
                                pe.wait_ge(v_ready.sem, v_ready.at(4 * b + 4))
                                if g == 0:
                                    pe.wait_ge(x_ready.sem, x_ready.at(b))
                                for t in range(NKT):
                                    ins = pe.matmul(ps[6 + g // 8][:, 0:S], v_head(t, g), AT[g // 2 % 2][:, t, g % 2, :],
                                                    start=g % 8 == 0 and t == 0, stop=g % 8 == 7 and t == NKT - 1)
                                ins.then_inc(av_psum.sem, 1)
                            if more and h == NH:
                                queries_and_keys(b + 1, 1 - j, i + j)
                    else:
                        pe.wait_ge(q_ready.sem, q_ready.at(2 * b + 2))
                        pe.wait_ge(k_ready.sem, k_ready.at(2 * b + 2))
                        for u in range(12):
                            m, t, half = u // 6, u // 2 % 3, u % 2
                            bank_free(pe, b, 8 + u)
                            rows = KT if t < NKT - 1 else KV - (NKT - 1) * KT
                            pe.matmul(ps[u % 4][0:rows, 0:4 * S], Kt[:, m, t * KT:t * KT + rows],
                                      Qz[:, m, 4 * half:4 * half + 4, :].rearrange("p h s -> p (h s)"), start=True,
                                      stop=True).then_inc(s_psum.sem, 1)
                        if more:
                            queries_and_keys(b + 1, 1 - j, i + j)
                        for m in range(KD):
                            pe.wait_ge(v_ready.sem, v_ready.at(4 * b + 4))
                            pe.wait_ge(exp_ready.sem, exp_ready.at(12 * b + 6 * m + 6))
                            if m == 0:
                                pe.wait_ge(x_ready.sem, x_ready.at(b))
                            for g in range(NHT):
                                for t in range(NKT):
                                    rows = KT if t < NKT - 1 else KV - (NKT - 1) * KT
                                    ins = pe.matmul(ps[6 + m][:, 0:S], v_head(t, NHT * m + g, rows),
                                                    AS[0:rows, t, NHT * m + g, :], start=g == 0 and t == 0,
                                                    stop=g == NHT - 1 and t == NKT - 1)
                            ins.then_inc(av_psum.sem, 1)
                    pe.wait_ge(ot_ready.sem, ot_ready.at(2 * b + 2))
                    for k in range(KD):
                        ins = pe.matmul(ps[6][0:S, 0:D], OT[j][:, k, :], wo[:, k, :], start=k == 0, stop=k == KD - 1)
                    ins.then_inc(o_psum.sem, 1)

                queries_and_keys(0, 0, 0)
                batches(pe, run)

            @block.vector
            def _(dve):
                chain = Chain(dve, own)
                dve.wait_ge(loaded.sem, 32 if soft else 96)
                dve.wait_ge(zeroed.sem, heads_zeroed)
                av_events = NH if soft else 2

                def queries(b):
                    for m in range(KD):
                        dve.wait_ge(q_psum.sem, q_psum.at(2 * b + m + 1))
                        if m == 0:
                            dve.wait_ge(s_psum.sem, s_psum.at((NH if soft else 12) * b))
                        dve.scalar_tensor_tensor(Qz[:, m, :, :], pair(ps[m][:, 0:S], NHT),
                                                 1.0 / 16 if soft else bq[:, m:m + 1], wide(core.head_mask[:, :], S),
                                                 ALU.mult if soft else ALU.add, ALU.mult).then_inc(q_ready.sem, 1)

                def run(b, j, i, more):
                    for c, tiles in enumerate(V_USES):
                        dve.wait_ge(v_psum.sem, v_psum.at(4 * b + c + 1))
                        if c == 0:
                            dve.wait_ge(av_psum.sem, av_psum.at(av_events * b))
                        for n, (m, t) in enumerate(tiles):
                            src = ps[c][0:KT, n * P:(n + 1) * P].rearrange("p (h e) -> p h e", e=16)
                            if soft:
                                ins = dve.tensor_copy(v_blocks(t, m), src)
                            else:
                                ins = dve.tensor_tensor(v_blocks(t, m), src, core.rows[
                                    0:KT, L3_BV, m * P:(m + 1) * P].rearrange("p (h e) -> p h e", e=16), ALU.add)
                        ins.then_inc(v_ready.sem, 1)
                    if soft:
                        dve.wait_ge(mask_loaded[j].sem, 16 * (i + 1))
                        dve.tensor_scalar(mask[j][:, :], mask_i[j][:, :], 0.0, None,
                                          ALU.not_equal).then_inc(mask_ready.sem, 1)
                        dve.wait_ge(mask_ready.sem, mask_ready.at(b + 1))
                        for h in range(NH + LAG_V + 2):
                            if h < NH:
                                bank = ps[(8 + h) % 4][0:S, 0:KV]
                                dve.wait_ge(s_psum.sem, s_psum.at(NH * b + h + 1))
                                dve.scalar_tensor_tensor(bank, bank, 1e-20 / 16, mask[j][:, :], ALU.add,
                                                         ALU.mult).then_inc(masked.sem, 1)
                                dve.wait_ge(masked.sem, masked.at(NH * b + h + 1))
                                dve.tensor_reduce(neg_max[:, h % 4:h % 4 + 1], bank, AX.X, ALU.max,
                                                  negate=True).then_inc(max_ready.sem, 1)
                            g = h - 1
                            if 0 <= g < NH:
                                dve.wait_ge(exp_ready.sem, exp_ready.at(NH * b + g + 1))
                                chain.step(dve.reciprocal(inv[:, g % 4:g % 4 + 1], total[:, g % 4:g % 4 + 1]))
                                dve.tensor_scalar(A[g % 4][:, 0:KV], A[g % 4][:, 0:KV], inv[:, g % 4:g % 4 + 1], None,
                                                  ALU.mult).then_inc(norm_ready.sem, 1)
                            if more and h == NH + 1:
                                queries(b + 1)
                            g = h - LAG_V - 1
                            if 0 <= g < NH and g % 8 == 7:
                                if g == 7:
                                    dve.wait_ge(o_psum.sem, o_psum.at(b - 1))
                                dve.wait_ge(av_psum.sem, av_psum.at(NH * b + g + 1))
                                dve.tensor_copy(OT[j][:, g // 8, :], ps[6 + g // 8][:, 0:S]).then_inc(ot_ready.sem, 1)
                    else:
                        if more:
                            queries(b + 1)
                        for m in range(KD):
                            if m == 0:
                                dve.wait_ge(o_psum.sem, o_psum.at(b - 1))
                            dve.wait_ge(av_psum.sem, av_psum.at(2 * b + m + 1))
                            dve.tensor_copy(OT[j][:, m, :], ps[6 + m][:, 0:S]).then_inc(ot_ready.sem, 1)
                    dve.wait_ge(o_psum.sem, o_psum.at(b + 1))
                    xb = X[:, bass.ds(b, 1), :]
                    dve.tensor_tensor(xb, xb, ps[6][0:S, 0:D].unsqueeze(1), ALU.add).then_inc(x_ready.sem, 1)

                queries(0)
                batches(dve, run, chain, NH if soft else 0)

            @block.scalar
            def _(act):
                act.wait_ge(loaded.sem, 32 if soft else 96)
                act.wait_ge(zeroed.sem, heads_zeroed)

                def keys(b):
                    for m in range(KD):
                        act.wait_ge(k_psum.sem, k_psum.at(2 * b + m + 1))
                        if m == 0:
                            act.wait_ge(s_psum.sem, s_psum.at((NH if soft else 12) * b))
                        if soft:
                            ins = act.activation(Kt[:, m, :], ps[2 + m][:, 0:KVP], ACT.Copy)
                        else:
                            ins = act.activation(Kt[:, m, :], ps[2 + m][:, 0:KVP], ACT.Identity, bias=bk[:, m:m + 1])
                        ins.then_inc(k_ready.sem, 1)

                def run(b, j, i, more):
                    if soft:
                        for h in range(NH + LAG_T):
                            if h < NH:
                                act.wait_ge(max_ready.sem, max_ready.at(NH * b + h + 1))
                                act.wait_ge(at_psum.sem, at_psum.at(NH * b + h - 3))
                                act.activation(A[h % 4][:, 0:KV], ps[(8 + h) % 4][0:S, 0:KV], ACT.Exp,
                                               bias=neg_max[:, h % 4:h % 4 + 1],
                                               accum_out=total[:, h % 4:h % 4 + 1]).then_inc(exp_ready.sem, 1)
                            g = h - LAG_T
                            if 0 <= g < NH:
                                act.wait_ge(at_psum.sem, at_psum.at(NH * b + g + 1))
                                act.wait_ge(av_psum.sem, av_psum.at(NH * b + 2 * (g // 2) - 2))
                                act.activation(AT[g // 2 % 2][:, :, g % 2, :],
                                               ps[4 + g % 2][0:KT, 0:NKT * S].rearrange("p (t s) -> p t s", t=NKT),
                                               ACT.Copy).then_inc(at_ready.sem, 1)
                            if more and h == NH + 1:
                                keys(b + 1)
                    else:
                        act.wait_ge(av_psum.sem, av_psum.at(2 * b))
                        for u in range(12):
                            m, t, half = u // 6, u // 2 % 3, u % 2
                            rows = KT if t < NKT - 1 else KV - (NKT - 1) * KT
                            act.wait_ge(s_psum.sem, s_psum.at(12 * b + u + 1))
                            h0 = NHT * m + 4 * half
                            act.activation(AS[0:rows, t, h0:h0 + 4, :],
                                           ps[u % 4][0:rows, 0:4 * S].rearrange("p (h s) -> p h s", h=4), ACT.Sigmoid,
                                           scale=0.25).then_inc(exp_ready.sem, 1)
                        if more:
                            keys(b + 1)

                keys(0)
                batches(act, run)


def head16_softmax(core, io):
    heads16(core, io, 2)


def head16_sigmoid(core, io):
    heads16(core, io, 3)


def routed_ffn(core, io, E, top, router, gu_name, down_name):
    X, N, NT, ps = core.X, core.N, core.NT, core.ps
    UNITS = NI * 2
    LAG = 2
    with Stage(core) as st:
        Wr = st.sb("Wr", [P, KD, E])
        gu = [st.sb(f"gu{j}", [P, 2, KD, IP]) for j in range(2)]
        wd = [st.sb(f"wd{j}", [P, NI, D]) for j in range(2)]
        L, CW = st.sb("L", [S, NB, E]), st.sb("CW", [S, NB, E])
        small = st.sb("small", [S, 3, NB])
        above, same = st.sb("above", [S, NB, E, E]), st.sb("same", [S, NB, E, E])
        rank, pick = st.sb("rank", [S, NB, E]), st.sb("pick", [S, NB, E])
        cwE = [st.sb(f"cwE{j}", [S, NB]) for j in range(2)]
        cwB = [st.sb(f"cwB{j}", [P, T]) for j in range(2)]
        XM = [st.sb(f"XM{j}", [P, KD, T]) for j in range(2)] if top == 1 else None
        G = [st.sb(f"G{j}", [P, HALF]) for j in range(2)]
        U = [st.sb(f"U{j}", [P, HALF]) for j in range(2)]
        Hh = [st.sb(f"Hh{j}", [P, HALF]) for j in range(4)]
        YT = st.sb("YT", [P, KD, T])
        zero = st.sb("zero", [P, HALF])
        loaded, w_loaded = st.event(), [st.event(), st.event()]
        zeroed, own = st.event(), st.event()
        l_psum, e_in, e_ready, cw_ready = (st.event() for _ in range(4))
        cwe_ready, cwb_psum, cwb_ready, xm_ready = st.event(), st.event(4), st.event(4), st.event()
        gate_psum, up_psum, g_ready, u_ready, h_ready, down_done = (st.event(4 * UNITS) for _ in range(6))
        y_done, yt_ready, y_psum, x_ready = st.event(), st.event(), st.event(), st.event(2)
        if top == 1:
            h_ready = u_ready
        PAIRS = E // 2

        def experts(eng, body):
            with eng.Fori(0, PAIRS) as i:
                for j in range(2):
                    body(2 * i + j, j, i)
            if E % 2:
                body(E - 1, 0, PAIRS)

        with st.block() as block:
            @block.sync
            def _(sp):
                st.heads(sp)
                sp.dma_start(Wr[:, :, :], io[router]).then_inc(loaded.sem, 16)

                def load(e, j, i):
                    sp.wait_ge(down_done.sem, down_done.at(UNITS * (e - 1)))
                    sp.dma_start(gu[j][:, :, :, :], io[gu_name][bass.ds(e, 1)]).then_inc(w_loaded[j].sem, 16)
                    sp.dma_start(wd[j][:, :, :], io[down_name][bass.ds(e, 1)]).then_inc(w_loaded[j].sem, 16)
                experts(sp, load)

            @block.gpsimd
            def _(pool):
                pool.memset(zero[:, :], 0.0).then_inc(zeroed.sem, 1)
                if top == 2:
                    def scale(e, j, i):
                        for u in range(UNITS):
                            n = UNITS * e + u
                            if u == 0:
                                pool.wait_ge(cwb_ready.sem, cwb_ready.at(2 * e + 2))
                            pool.wait_ge(u_ready.sem, u_ready.at(n + 1))
                            pool.wait_ge(down_done.sem, down_done.at(n - 3))
                            half = u % 2
                            pool.tensor_tensor(Hh[u % 4][:, :], U[u % 2][:, :], cwB[j][:, half * HALF:(half + 1) * HALF],
                                               ALU.mult).then_inc(h_ready.sem, 1)
                    experts(pool, scale)

            @block.tensor
            def _(pe):
                pe.wait_ge(loaded.sem, 16)
                for b in range(NB):
                    for k in range(KD):
                        ins = pe.matmul(ps[0][0:S, 16 * b:16 * b + E], NT[:, k, b * S:(b + 1) * S], Wr[:, k, :],
                                        start=k == 0, stop=k == KD - 1)
                ins.then_inc(l_psum.sem, 1)
                pe.wait_ge(zeroed.sem, 1)
                for q in range(4):
                    pe.matmul(ps[4 + q][:, 0:HALF], zero[:, 0:P], zero[:, :], start=True, stop=False,
                              skip_group_check=True)
                pe.wait_ge(e_ready.sem, 1)

                def spread(e, j):
                    pe.wait_ge(cwe_ready.sem, e + 1)
                    for half in range(2):
                        pe.wait_ge(g_ready.sem, g_ready.at(UNITS * e - 1 + half))
                        for c in range(4):
                            ins = pe.matmul(ps[2 * half][:, c * S:(c + 1) * S],
                                            cwE[j][:, 4 * half + c:4 * half + c + 1].broadcast_to([S, P]),
                                            core.ident[0:S, 0:S], start=True, stop=True)
                        ins.then_inc(cwb_psum.sem, 1)

                def run(e, j, i):
                    spread(e, j)
                    pe.wait_ge(w_loaded[j].sem, 32 * (i + 1))
                    if top == 1:
                        pe.wait_ge(xm_ready.sem, KD * e + KD)
                    pe.wait_ge(cwb_ready.sem, cwb_ready.at(2 * e + 2))
                    for u in range(UNITS + LAG):
                        n = UNITS * e + u
                        if u < UNITS:
                            t, half = u // 2, u % 2
                            cols = slice(half * HALF, (half + 1) * HALF)
                            src = XM[j] if top == 1 else NT
                            pe.wait_ge(g_ready.sem, g_ready.at(n - 1))
                            for k in range(KD):
                                ins = pe.matmul(ps[2 * (u % 2)][:, 0:HALF], gu[j][:, 0, k, t * P:(t + 1) * P],
                                                src[:, k, cols], start=k == 0, stop=k == KD - 1)
                            ins.then_inc(gate_psum.sem, 1)
                            pe.wait_ge(u_ready.sem, u_ready.at(n - 1))
                            for k in range(KD):
                                ins = pe.matmul(ps[2 * (u % 2) + 1][:, 0:HALF], gu[j][:, 1, k, t * P:(t + 1) * P],
                                                src[:, k, cols], start=k == 0, stop=k == KD - 1)
                            ins.then_inc(up_psum.sem, 1)
                        g = u - LAG
                        if g >= 0:
                            t, half = g // 2, g % 2
                            pe.wait_ge(h_ready.sem, h_ready.at(UNITS * e + g + 1))
                            for m in range(KD):
                                ins = pe.matmul(ps[4 + 2 * m + half][:, 0:HALF], wd[j][:, t, m * P:(m + 1) * P],
                                                Hh[g % 4][:, :], start=False, stop=False, skip_group_check=True)
                            ins.then_inc(down_done.sem, 1)
                experts(pe, run)
                pe.wait_ge(yt_ready.sem, 4)
                for b in range(NB):
                    pe.wait_ge(x_ready.sem, x_ready.at(b - 1))
                    for m in range(KD):
                        ins = pe.transpose(ps[b % 2][0:S, m * P:(m + 1) * P], YT[:, m, b * S:(b + 1) * S],
                                           core.ident[:, :])
                    ins.then_inc(y_psum.sem, 1)

            @block.vector
            def _(dve):
                chain = Chain(dve, own)
                dve.wait_ge(l_psum.sem, 1)
                logits = ps[0][0:S, 0:16 * NB].rearrange("s (b e) -> s b e", e=16)[:, :, 0:E]
                chain.step(dve.tensor_copy(L[:, :, :], logits))
                if top == 2:
                    chain.step(dve.tensor_reduce(small[:, 0, :], L[:, :, :], AX.X, ALU.max))
                    dve.tensor_tensor(L[:, :, :], L[:, :, :], wide(small[:, 0, :], E), ALU.subtract).then_inc(e_in.sem, 1)
                    dve.wait_ge(e_ready.sem, 1)
                    chain.step(dve.tensor_reduce(small[:, 1, :], CW[:, :, :], AX.X, ALU.add))
                    chain.step(dve.reciprocal(small[:, 2, :], small[:, 1, :]))
                    chain.step(dve.tensor_tensor(L[:, :, :], CW[:, :, :], wide(small[:, 2, :], E), ALU.mult))
                top_mask(dve, chain, L[:, :, :], NB, E, (top,), above[:, :, :, :], same[:, :, :, :], rank[:, :, :],
                         (pick[:, :, :],), core.below[:, 0:E, 0:E])
                if top == 2:
                    chain.step(dve.tensor_tensor(CW[:, :, :], L[:, :, :], pick[:, :, :], ALU.mult))
                    chain.step(dve.tensor_reduce(small[:, 1, :], CW[:, :, :], AX.X, ALU.add))
                    chain.step(dve.reciprocal(small[:, 2, :], small[:, 1, :]))
                    chain.step(dve.tensor_tensor(CW[:, :, :], CW[:, :, :], wide(small[:, 2, :], E), ALU.mult))
                else:
                    dve.tensor_copy(CW[:, :, :], pick[:, :, :]).then_inc(e_ready.sem, 1)
                    dve.wait_ge(e_ready.sem, 1)

                def prepare(e, j):
                    dve.wait_ge(cwb_psum.sem, cwb_psum.at(2 * e - 2))
                    dve.tensor_copy(cwE[j][:, :].unsqueeze(2), CW[:, :, bass.ds(e, 1)]).then_inc(cwe_ready.sem, 1)

                def run(e, j, i):
                    prepare(e, j)
                    if top == 1:
                        dve.wait_ge(cwb_ready.sem, cwb_ready.at(2 * e + 2))
                        dve.wait_ge(up_psum.sem, up_psum.at(UNITS * (e - 1)))
                        for k in range(KD):
                            dve.tensor_tensor(XM[j][:, k, :], NT[:, k, :], cwB[j][:, :], ALU.mult).then_inc(xm_ready.sem, 1)
                    for u in range(UNITS):
                        n = UNITS * e + u
                        dve.wait_ge(g_ready.sem, g_ready.at(n + 1))
                        dve.wait_ge(up_psum.sem, up_psum.at(n + 1))
                        up = ps[2 * (u % 2) + 1][:, 0:HALF]
                        if top == 2:
                            dve.wait_ge(h_ready.sem, h_ready.at(n - 1))
                            dve.tensor_tensor(U[u % 2][:, :], G[u % 2][:, :], up, ALU.mult).then_inc(u_ready.sem, 1)
                        else:
                            dve.wait_ge(down_done.sem, down_done.at(n - 3))
                            dve.tensor_tensor(Hh[u % 4][:, :], G[u % 2][:, :], up, ALU.mult).then_inc(u_ready.sem, 1)
                experts(dve, run)
                for b in range(NB):
                    dve.wait_ge(y_psum.sem, b + 1)
                    dve.tensor_tensor(X[:, b, :], X[:, b, :], ps[b % 2][0:S, 0:D], ALU.add).then_inc(x_ready.sem, 1)

            @block.scalar
            def _(act):
                if top == 2:
                    act.wait_ge(e_in.sem, 1)
                    act.activation(CW[:, :, :], L[:, :, :], ACT.Exp).then_inc(e_ready.sem, 1)

                def run(e, j, i):
                    for half in range(2):
                        act.wait_ge(cwb_psum.sem, cwb_psum.at(2 * e + half + 1))
                        if half == 0:
                            act.wait_ge(h_ready.sem, h_ready.at(UNITS * (e - 1)))
                        act.activation(cwB[j][:, half * HALF:(half + 1) * HALF], ps[2 * half][:, 0:HALF],
                                       ACT.Copy).then_inc(cwb_ready.sem, 1)
                    for u in range(UNITS):
                        n = UNITS * e + u
                        act.wait_ge(gate_psum.sem, gate_psum.at(n + 1))
                        act.wait_ge(u_ready.sem, u_ready.at(n - 1))
                        act.activation(G[u % 2][:, :], ps[2 * (u % 2)][:, 0:HALF], ACT.Silu).then_inc(g_ready.sem, 1)
                experts(act, run)
                act.wait_ge(down_done.sem, down_done.at(UNITS * E))
                for m in range(KD):
                    for half in range(2):
                        act.activation(YT[:, m, half * HALF:(half + 1) * HALF], ps[4 + 2 * m + half][:, 0:HALF],
                                       ACT.Copy).then_inc(yt_ready.sem, 1)


def routed_ffn_2(core, io):
    routed_ffn(core, io, 9, 2, "Wr2", "gu2", "down2")


def routed_ffn_3(core, io):
    routed_ffn(core, io, 8, 1, "Wr3", "gu3", "down3")


ROWS = ["w1_sim", "b_qv", "bp", "L1_bo", "gamma", "beta", "L3_bv", "L3_bo", "zero"]
W1_SIM, B_QV, B_P, L1_BO, GAMMA, BETA, L3_BV, L3_BO = range(8)

WEIGHTS = {
    "sim": {"w_sim": [P, 2 * KD], "b_sim": [P, 1], "W_qv": [P, 8, D]},
    "gated": {"Vg": [P, KD, 512], "VgT": [P, 4, 512], "We": [P, KD, 8 * D], "Wp": [P, KD, D], "be": [8, D]},
    "head64": {"Wq": [P, KD, 1024], "Wk": [P, KD, 1024], "Wv": [P, KD, 1024], "Wo": [P, 8, D], "bq": [P, 8],
               "bk": [P, 8], "bv": [P, 8]},
}


def program(nc, io, out):
    with ExitStack() as ctx:
        core = Core(nc, ctx)
        core.weights, core.loaded, core.loads = {}, {}, {}
        for stage, tensors in WEIGHTS.items():
            core.loaded[stage] = core.sem(f"loaded_{stage}")
            core.loads[stage] = 16 * len(tensors)
            for name, shape in tensors.items():
                core.weights[name] = ctx.enter_context(nc.sbuf_tensor(name, shape, F32))

        def load(eng, stage, io):
            for name, shape in WEIGHTS[stage].items():
                eng.dma_start(core.weights[name][:], io[name]).then_inc(core.loaded[stage], 16)
        core.load = load
        stages = [sim_attention, gated_experts, head64_attention, ternary_ffn, head16_softmax, routed_ffn_2, head16_sigmoid, routed_ffn_3]
        setup(core, io)
        for stage in stages:
            layer_norm(core)
            stage(core, io)
        with Stage(core) as st:
            stored = st.event()
            with st.block() as block:
                @block.sync
                def _(sp):
                    sp.dma_start(out, core.X[:, :, :]).then_inc(stored.sem, 16)
                    for name, sem in core.loaded.items():
                        sp.wait_ge(sem, core.loads[name])
                    sp.wait_ge(stored.sem, 16)


def arrays_of(v, np):
    f = {k: np.asarray(a) for k, a in v.items()}
    a = {}

    def tiles(w):
        return w.reshape(-1, P, w.shape[1]).transpose(1, 0, 2)

    def cols(w):
        return w.reshape(-1, P).T

    a["x"] = f["x"].transpose(1, 0, 2)
    ctx = np.zeros((NB, KVP, D), np.float32)
    ctx[:, :KV] = f["ctx_1024"]
    a["ctT"] = ctx.transpose(0, 2, 1).reshape(NB, KD, P, KVP).transpose(0, 2, 1, 3)
    a["ctk"] = ctx.reshape(NB, NKT, KT, D).transpose(0, 2, 1, 3)
    a["mask"] = f["mask_Bx1xSxS2_ik1"][:, 0]
    a["head_mask"] = (np.arange(P)[:, None] // 16 == np.arange(8)[None, :]).astype(np.float32)
    a["below"] = (np.arange(9)[None, :] < np.arange(9)[:, None]).astype(np.float32)
    w = f["L0_xattn_w_sim"]
    rows = np.zeros((len(ROWS), D), np.float32)
    for n, r in enumerate([w[:D], f["L0_xattn_b_qv"], f["L0_ffn_bp"], f["L1_xattn_bo"], f["L1_xattn_ln_gamma"],
                           f["L1_xattn_ln_beta"], f["L3_xattn_bv"], f["L3_xattn_bo"]]):
        rows[n] = r
    a["rows"] = rows
    a["w_sim"] = cols(w[D:])
    a["b_sim"] = np.broadcast_to(f["L0_xattn_b_sim"][None, :], (P, 1))
    a["W_qv"] = tiles(f["L0_xattn_W_qv"])
    vg = f["L0_ffn_Vg"]
    a["Vg"] = tiles(vg.transpose(1, 0, 2).reshape(D, 512))
    vgt = np.zeros((P, 4, 2, D), np.float32)
    for e in range(8):
        vgt[64 * (e % 2):64 * (e % 2) + 64, e // 2, e % 2] = vg[e].T
    a["VgT"] = vgt.reshape(P, 4, 512)
    a["We"] = tiles(f["L0_ffn_We"].transpose(2, 0, 1).reshape(D, 8 * D))
    a["Wp"] = tiles(f["L0_ffn_Wp"].T)
    a["be"] = f["L0_ffn_be"]
    for n in ("Wq", "Wk", "Wv", "Wo"):
        a[n] = tiles(f["L1_xattn_" + n])
    for n in ("bq", "bk", "bv"):
        a[n] = cols(f["L1_xattn_" + n])
    a["w1"] = tiles(f["L1_ffn_w1"].T)
    a["w2"] = tiles(f["L1_ffn_w2"].T)
    a["conv_w"] = f["L1_ffn_conv_w"][:, 0].reshape(8, P, 3).transpose(1, 0, 2)
    a["conv_b"] = cols(f["L1_ffn_conv_b"])
    blocks = np.zeros((P, P), np.float32)
    for n in range(8):
        blocks[16 * n:16 * n + 16, 16 * n:16 * n + 16] = f["L2_xattn_W_v"].T
    a["W_heads"] = blocks
    a["W_o"] = tiles(f["L2_xattn_W_o"].T)
    for n in ("Wq", "Wk", "Wv", "Wo"):
        a["L3_" + n] = tiles(f["L3_xattn_" + n])
    for n in ("bq", "bk"):
        a["L3_" + n] = cols(f["L3_xattn_" + n])
    a["Wr2"] = tiles(f["L2_ffn_Wr"])
    a["Wr3"] = tiles(f["L3_ffn_router_w"].T)

    def experts(gate, up, down):
        E, _, I = gate.shape
        gu = np.zeros((E, 2, D, IP), np.float32)
        gu[:, 0, :, :I], gu[:, 1, :, :I] = gate, up
        wd = np.zeros((E, IP, D), np.float32)
        wd[:, :I] = down
        return (gu.reshape(E, 2, KD, P, IP).transpose(0, 3, 1, 2, 4),
                wd.reshape(E, NI, P, D).transpose(0, 2, 1, 3))

    a["gu2"], a["down2"] = experts(f["L2_ffn_Wg"], f["L2_ffn_Wu"], f["L2_ffn_Wd"])
    a["gu3"], a["down3"] = experts(f["L3_ffn_gate_w"].transpose(0, 2, 1), f["L3_ffn_up_w"].transpose(0, 2, 1),
                                   f["L3_ffn_down_w"].transpose(0, 2, 1))
    return {k: np.ascontiguousarray(x) for k, x in a.items()}


def kernel(**inputs):
    import numpy as np
    import concourse.bacc as bacc
    from concourse.bass_utils import run_bass_kernel_spmd

    nc = bacc.Bacc("TRN2", target_bir_lowering=False, num_devices=1)
    arrays = arrays_of(inputs, np)
    io = {k: nc.dram_tensor(f"in_{k}", a.shape, mybir.dt.from_np(a.dtype), kind="ExternalInput").ap()
          for k, a in arrays.items()}
    out = nc.dram_tensor("out_x", (S, NB, D), F32, kind="ExternalOutput").ap()
    program(nc, io, out)
    got = run_bass_kernel_spmd(nc, [{f"in_{k}": a for k, a in arrays.items()}], core_ids=[0])
    return np.ascontiguousarray(got.results[0]["out_x"].transpose(1, 0, 2))
```

```python
from contextlib import ExitStack

import concourse.bass as bass
from concourse import mybir

F32 = mybir.dt.float32
BF16 = mybir.dt.bfloat16
I32 = mybir.dt.int32
ACT = mybir.ActivationFunctionType
ALU = mybir.AluOpType
AX = mybir.AxisListType

NB, S, D = 8, 100, 256
T = NB * S
P = 128
KD = D // P
KV = 361
KT = 121
NKT = 3
KVP = KT * NKT
NH = 16
HALF = T // 2
IT = 704
HU = 118
NI = 6
IP = NI * HU
TS = 2 * S
MAX_TILES = 16
EPS = 1e-5
MAGIC = 1.5 * 2.0 ** 23


class Event:
    def __init__(self, handle, head):
        self.sem, self.head = handle, head

    def at(self, count, step=1):
        return count * step + self.head


class Chain:

    def __init__(self, eng, event):
        self.eng, self.sem, self.base, self.k, self.turn, self.per = eng, event.sem, 0, 0, 0, 0

    def loop(self, turn, per):
        self.base, self.turn, self.per, self.k = self.base + self.k, turn, per, 0

    def end(self, turns):
        assert self.k == self.per, (self.k, self.per)
        self.base, self.turn, self.per, self.k = self.base + turns * self.per, 0, 0, 0

    def step(self, ins):
        ins.then_inc(self.sem, 1)
        self.k += 1
        self.eng.wait_ge(self.sem, self.base + self.turn * self.per + self.k)


class Stage:

    def __init__(self, core):
        self.core, self.nc, self.ctx, self.used = core, core.nc, ExitStack(), []

    def __enter__(self):
        return self

    def sb(self, name, shape, dt=F32):
        return self.ctx.enter_context(self.nc.sbuf_tensor(f"{name}_{self.core.stage}", shape, dt))

    def event(self, head=0):
        e = Event(self.core.pool[len(self.used)], head)
        self.used.append(e)
        return e

    def block(self):
        return self.nc.Block()

    def __exit__(self, *a):
        self.ctx.close()
        self.core.stage += 1
        if a[0] is not None:
            return
        with self.nc.Block() as block:
            @block.gpsimd
            def _(pool):
                for e in self.used:
                    pool.sem_clear(e.sem)

    def heads(self, eng):
        for e in self.used:
            if e.head:
                eng.sem_inc(e.sem, e.head)


class Core:

    def __init__(self, nc, ctx):
        self.nc, self.stage = nc, 0
        sb = lambda name, shape, dt=F32: ctx.enter_context(nc.sbuf_tensor(name, shape, dt))
        self.X = sb("X", [S, NB, D])
        self.N = sb("N", [S, NB, D])
        self.NT = sb("NT", [P, KD, T])
        self.ident = sb("ident", [P, P])
        self.identb = sb("identb", [P, P], BF16)
        self.ones = sb("ones", [P, P])
        self.below = sb("below", [S, 9, 9])
        self.before = sb("before", [S, S], BF16)
        self.ones_b = sb("ones_b", [S, S], BF16)
        self.counts = sb("counts", [S, MAX_TILES])
        self.head_mask = sb("head_mask", [P, 8])
        self.minus_half = sb("minus_half", [S, NB])
        self.half = sb("half", [S, 64])
        self.rows = sb("rows", [P, 9, D])
        self.ps = [ctx.enter_context(nc.psum_tensor(f"bank{i}", [P, 512], F32)) for i in range(8)]
        self.sem = lambda name: ctx.enter_context(nc.semaphore(name))
        self.soft_events = [[Event(self.sem(f"soft{n}_{m}"), 0) for m in range(2 + NB // 2)] for n in range(2)]
        self.pool = [self.sem(f"event{i}") for i in range(44)]


def batches(eng, body, chain=None, steps=0):
    with eng.Fori(0, NB // 2 - 1) as i:
        if chain:
            chain.loop(i, 2 * steps)
        for j in range(2):
            body(2 * i + j, j, i, True)
    if chain:
        chain.end(NB // 2 - 1)
    body(NB - 2, 0, NB // 2 - 1, True)
    body(NB - 1, 1, NB // 2 - 1, False)


def pair(ap, n):
    return ap.unsqueeze(1).broadcast_to([ap.shape[0], n, ap.shape[1]])


def wide(ap, n):
    return ap.unsqueeze(2).broadcast_to([ap.shape[0], ap.shape[1], n])


def token(b):
    return bass.ds(b * S, S)


def variance(dve, chain, stats, mean, gap, var):
    chain.step(dve.tensor_tensor(mean, stats[:, :, 1], stats[:, :, 4], ALU.add))
    chain.step(dve.tensor_tensor(gap, stats[:, :, 1], stats[:, :, 4], ALU.subtract))
    chain.step(dve.tensor_tensor(var, stats[:, :, 2], stats[:, :, 5], ALU.add))
    chain.step(dve.tensor_tensor(gap, gap, gap, ALU.mult))
    chain.step(dve.tensor_scalar(gap, gap, 0.25, EPS, ALU.mult, ALU.add))
    return dve.scalar_tensor_tensor(var, var, 1.0 / D, gap, ALU.mult, ALU.add)


def layer_norm(core):
    X, N, NT, ps = core.X, core.N, core.NT, core.ps
    with Stage(core) as st:
        stats = st.sb("stats", [S, NB, 6])
        mean = st.sb("mean", [S, NB])
        gap = st.sb("gap", [S, NB])
        var = st.sb("var", [S, NB])
        rstd = st.sb("rstd", [S, NB])
        stats_ready, var_ready, rstd_ready, n_ready, nt_psum = (st.event() for _ in range(5))
        own, nt_ready = st.event(), st.event()
        with st.block() as block:
            @block.vector
            def _(dve):
                chain = Chain(dve, own)
                with dve.Fori(0, NB) as b:
                    dve.bn_stats(stats[:, bass.ds(b, 1), :], core.X[:, bass.ds(b, 1), :]).then_inc(stats_ready.sem, 1)
                dve.wait_ge(stats_ready.sem, NB)
                variance(dve, chain, stats[:, :, :], mean[:, :], gap[:, :], var[:, :]).then_inc(var_ready.sem, 1)
                chain.step(dve.tensor_scalar(mean[:, :], mean[:, :], 0.5, None, ALU.mult))
                dve.wait_ge(rstd_ready.sem, 1)
                with dve.Fori(0, NB) as b:
                    dve.tensor_scalar(N[:, bass.ds(b, 1), :], X[:, bass.ds(b, 1), :], mean[:, bass.ds(b, 1)],
                                      rstd[:, bass.ds(b, 1)], ALU.subtract, ALU.mult).then_inc(n_ready.sem, 1)

            @block.gpsimd
            def _(pool):
                pool.wait_ge(var_ready.sem, 1)
                pool.tensor_tensor(rstd[:, :], var[:, :], core.minus_half[:, 0:NB], ALU.pow).then_inc(rstd_ready.sem, 1)

            @block.tensor
            def _(pe):
                for q in range(NB // 2):
                    pe.wait_ge(n_ready.sem, 2 * q + 2)
                    for j in range(2):
                        for k in range(KD):
                            ins = pe.transpose(ps[q][:, (2 * k + j) * S:(2 * k + j + 1) * S],
                                               N[:, 2 * q + j, k * P:(k + 1) * P], core.ident[0:S, 0:S])
                    ins.then_inc(nt_psum.sem, 1)

            @block.scalar
            def _(act):
                for q in range(NB // 2):
                    act.wait_ge(nt_psum.sem, q + 1)
                    act.activation(NT[:, :, 2 * q * S:2 * (q + 1) * S],
                                   ps[q][:, 0:4 * S].rearrange("p (k t) -> p k t", k=KD),
                                   ACT.Copy).then_inc(nt_ready.sem, 1)
                act.wait_ge(nt_ready.sem, NB // 2)


def setup(core, io):
    with Stage(core) as st:
        loaded, zeroed, made = st.event(), st.event(), st.event()
        with st.block() as block:
            @block.sync
            def _(sp):
                sp.dma_start(core.X[:, :, :], io["x"]).then_inc(loaded.sem, 16)
                sp.dma_start(core.head_mask[:, :], io["head_mask"]).then_inc(loaded.sem, 16)
                sp.dma_start(core.below[:, :, :], io["below"].partition_broadcast(S)).then_inc(loaded.sem, 16)
                sp.dma_start(core.rows[:, :, :], io["rows"].partition_broadcast(P)).then_inc(loaded.sem, 16)
                sp.dma_start(core.counts[:, :], io["counts"].partition_broadcast(S)).then_inc(loaded.sem, 16)
                core.load(sp, "sim", io)
                core.load(sp, "gated", io)
                core.load(sp, "head64", io)
                sp.wait_ge(loaded.sem, 80)

            @block.gpsimd
            def _(pool):
                pool.memset(core.ident[:, :], 0.0).then_inc(zeroed.sem, 1)
                pool.memset(core.ones[:, :], 1.0)
                pool.memset(core.ones_b[:, :], 1.0).then_inc(zeroed.sem, 1)
                pool.memset(core.minus_half[:, :], -0.5)
                pool.memset(core.half[:, :], 0.5)
                pool.wait_ge(zeroed.sem, 2)
                pool.affine_select(out=core.before[:, :], in_=core.ones_b[:, :], compare_op=ALU.is_gt, fill=0.0,
                                   base=0, pattern=[[1, S]], channel_multiplier=-1)
                pool.affine_select(out=core.ident[:, :], in_=core.ident[:, :], compare_op=ALU.not_equal, fill=1.0,
                                   base=0, pattern=[[-1, P]], channel_multiplier=1).then_inc(made.sem, 1)
                pool.wait_ge(made.sem, 1)
                pool.tensor_copy(core.identb[:, :], core.ident[:, :])


def sim_attention(core, io):
    X, N, NT, ps = core.X, core.N, core.NT, core.ps
    w = core.weights
    with Stage(core) as st:
        ctT = [st.sb(f"ctT{j}", [P, KD, KVP]) for j in range(2)]
        ctk = [st.sb(f"ctk{j}", [KT, NKT, D]) for j in range(2)]
        EW = [st.sb(f"EW{j}", [P, KD, S]) for j in range(2)]
        A = [st.sb(f"A{j}", [S, KVP]) for j in range(2)]
        AT = [st.sb(f"AT{j}", [KT, NKT, S]) for j in range(2)]
        F = [st.sb(f"F{j}", [P, 8, S]) for j in range(2)]
        HQ = st.sb("HQ", [P, KD, T])
        neg_max, total, inv = st.sb("neg_max", [S, NB]), st.sb("total", [S, NB]), st.sb("inv", [S, NB])
        enc_w1 = st.sb("enc_w1", [S, NB, D])
        row_max, best, per_batch = st.sb("row_max", [S, NB]), st.sb("best", [NB, 4]), st.sb("per_batch", [NB, S])
        beta = st.sb("beta", [S, NB])
        hc = st.sb("hc", [P, KD, NB])
        ctx_loaded = [st.event(), st.event()]
        ctk_loaded = [st.event(), st.event()]
        ew_ready, sim_ready, max_ready, norm_ready = st.event(), st.event(2), st.event(), st.event()
        exp_ready, at_psum, at_ready, hq_psum, hq_ready = (st.event(2) for _ in range(5))
        own, own_act, pads, w1_ready, bias_ready = (st.event() for _ in range(5))
        m_ready, mt_psum, top_ready, e_ready, share_ready, share_psum, beta_ready, hc_psum, hc_ready = \
            (st.event() for _ in range(9))
        f_act, f_pool, f_dve, out_psum, x_ready = st.event(), st.event(), st.event(), st.event(2), st.event(2)
        heads_set = st.event()
        with st.block() as block:
            @block.sync
            def _(sp):
                st.heads(sp)
                with sp.Fori(0, NB // 2) as i:
                    for j in range(2):
                        b = 2 * i + j
                        sp.wait_ge(hq_psum.sem, hq_psum.at(b - 1))
                        sp.dma_start(ctT[j][:, :, :], io["ctT"][bass.ds(b, 1)]).then_inc(ctx_loaded[j].sem, 16)
                        sp.dma_start(ctk[j][:, :, :], io["ctk"][bass.ds(b, 1)]).then_inc(ctk_loaded[j].sem, 16)

            @block.gpsimd
            def _(pool):
                pool.wait_ge(core.loaded["sim"], core.loads["sim"])
                for j in range(2):
                    pool.memset(A[j][:, KV:KVP], 0.0).then_inc(pads.sem, 1)
                pool.tensor_tensor(enc_w1[:, :, :], N[:, :, :], pair(core.rows[0:S, W1_SIM, :], NB),
                                   ALU.mult).then_inc(w1_ready.sem, 1)
                pool.tensor_tensor(X[:, :, :], X[:, :, :], pair(core.rows[0:S, B_QV, :], NB),
                                   ALU.add).then_inc(bias_ready.sem, 1)
                pool.wait_ge(hq_ready.sem, hq_ready.at(NB))
                with pool.Fori(0, NB // 2) as i:
                    for j in range(2):
                        b = 2 * i + j
                        pool.wait_ge(out_psum.sem, out_psum.at(b - 1))
                        pool.tensor_tensor(F[j][:, 4:6, :], NT[:, :, token(b)], HQ[:, :, token(b)],
                                           ALU.mult).then_inc(f_pool.sem, 1)

            @block.vector
            def _(dve):
                chain = Chain(dve, own)
                dve.wait_ge(core.loaded["sim"], core.loads["sim"])
                with dve.Fori(0, NB // 2) as i:
                    chain.loop(i, 2)
                    for j in range(2):
                        b = 2 * i + j
                        dve.wait_ge(sim_ready.sem, sim_ready.at(b - 1))
                        for k in range(KD):
                            dve.tensor_scalar(EW[j][:, k, :], NT[:, k, token(b)], w["w_sim"][:, KD + k:KD + k + 1],
                                              w["w_sim"][:, k:k + 1], ALU.mult, ALU.add).then_inc(ew_ready.sem, 1)
                        dve.wait_ge(sim_ready.sem, sim_ready.at(b + 1))
                        dve.tensor_reduce(neg_max[:, bass.ds(b, 1)], ps[j][0:S, 0:KV], AX.X, ALU.max,
                                          negate=True).then_inc(max_ready.sem, 1)
                        dve.wait_ge(exp_ready.sem, exp_ready.at(b + 1))
                        chain.step(dve.reciprocal(inv[:, bass.ds(b, 1)], total[:, bass.ds(b, 1)]))
                        dve.tensor_scalar(A[j][:, 0:KV], A[j][:, 0:KV], inv[:, bass.ds(b, 1)], None,
                                          ALU.mult).then_inc(norm_ready.sem, 1)
                chain.end(NB // 2)
                dve.wait_ge(w1_ready.sem, 1)
                chain.step(dve.tensor_reduce(row_max[:, :], enc_w1[:, :, :], AX.X, ALU.add))
                dve.wait_ge(max_ready.sem, NB)
                chain.step(dve.tensor_tensor(row_max[:, :], row_max[:, :], neg_max[:, :], ALU.subtract))
                dve.tensor_scalar(row_max[:, :], row_max[:, :], w["b_sim"][0:S, :], None, ALU.add).then_inc(m_ready.sem, 1)
                dve.wait_ge(mt_psum.sem, 1)
                dve.tensor_reduce(best[:, 0:1], ps[6][0:NB, 0:S], AX.X, ALU.max, negate=True).then_inc(top_ready.sem, 1)
                dve.wait_ge(e_ready.sem, 1)
                chain.step(dve.reciprocal(best[:, 2:3], best[:, 1:2]))
                dve.tensor_scalar(per_batch[:, :], per_batch[:, :], best[:, 2:3], None, ALU.mult).then_inc(share_ready.sem, 1)
                dve.wait_ge(share_psum.sem, 1)
                dve.tensor_copy(beta[:, :], ps[7][0:S, 0:NB]).then_inc(beta_ready.sem, 1)
                dve.wait_ge(hc_psum.sem, 1)
                chain.step(dve.tensor_copy(hc[:, :, :], ps[6][:, 0:KD * NB].rearrange("p (k b) -> p k b", k=KD)))
                dve.wait_ge(bias_ready.sem, 1)
                with dve.Fori(0, NB // 2) as i:
                    for j in range(2):
                        b = 2 * i + j
                        dve.wait_ge(out_psum.sem, out_psum.at(b - 1))
                        for k in range(KD):
                            dve.tensor_scalar(F[j][:, 6 + k, :], NT[:, k, token(b)], hc[:, k, bass.ds(b, 1)], None,
                                              ALU.mult).then_inc(f_dve.sem, 1)
                        dve.wait_ge(out_psum.sem, out_psum.at(b + 1))
                        dve.tensor_tensor(X[:, bass.ds(b, 1), :], X[:, bass.ds(b, 1), :], ps[j][0:S, 0:D].unsqueeze(1),
                                          ALU.add).then_inc(x_ready.sem, 1)

            @block.scalar
            def _(act):
                act.wait_ge(pads.sem, 2)
                with act.Fori(0, NB // 2) as i:
                    for j in range(2):
                        b = 2 * i + j
                        act.wait_ge(max_ready.sem, b + 1)
                        act.wait_ge(at_psum.sem, at_psum.at(b - 1))
                        act.activation(A[j][:, 0:KV], ps[j][0:S, 0:KV], ACT.Exp, bias=neg_max[:, bass.ds(b, 1)],
                                       accum_out=total[:, bass.ds(b, 1)]).then_inc(exp_ready.sem, 1)
                        act.wait_ge(at_psum.sem, at_psum.at(b + 1))
                        act.wait_ge(hq_psum.sem, hq_psum.at(b - 1))
                        act.activation(AT[j][:, :, :], ps[2 + j][0:KT, 0:NKT * S].rearrange("p (t s) -> p t s", t=NKT),
                                       ACT.Copy).then_inc(at_ready.sem, 1)
                        act.wait_ge(hq_psum.sem, hq_psum.at(b + 1))
                        act.activation(HQ[:, :, token(b)], ps[4 + j][:, 0:KD * S].rearrange("p (k s) -> p k s", k=KD),
                                       ACT.Copy).then_inc(hq_ready.sem, 1)
                act.wait_ge(top_ready.sem, 1)
                act.activation(per_batch[:, :], ps[6][0:NB, 0:S], ACT.Exp, bias=best[:, 0:1],
                               accum_out=best[:, 1:2]).then_inc(e_ready.sem, 1)
                act.wait_ge(hq_ready.sem, hq_ready.at(NB))
                with act.Fori(0, NB // 2) as i:
                    for j in range(2):
                        b = 2 * i + j
                        act.wait_ge(out_psum.sem, out_psum.at(b - 1))
                        act.activation(F[j][:, 0:2, :], NT[:, :, token(b)], ACT.Copy).then_inc(f_act.sem, 1)
                        act.activation(F[j][:, 2:4, :], HQ[:, :, token(b)], ACT.Copy).then_inc(f_act.sem, 1)

            @block.tensor
            def _(pe):
                pe.wait_ge(core.loaded["sim"], core.loads["sim"])
                with pe.Fori(0, NB // 2) as i:
                    for j in range(2):
                        b = 2 * i + j
                        pe.wait_ge(ew_ready.sem, KD * (b + 1))
                        pe.wait_ge(ctx_loaded[j].sem, 16 * (i + 1))
                        pe.wait_ge(exp_ready.sem, exp_ready.at(b - 1))
                        for k in range(KD):
                            ins = pe.matmul(ps[j][0:S, 0:KV], EW[j][:, k, :], ctT[j][:, k, 0:KV], start=k == 0,
                                            stop=k == KD - 1)
                        ins.then_inc(sim_ready.sem, 1)
                        pe.wait_ge(norm_ready.sem, b + 1)
                        pe.wait_ge(at_ready.sem, at_ready.at(b - 1))
                        for t in range(NKT):
                            ins = pe.transpose(ps[2 + j][0:KT, t * S:(t + 1) * S], A[j][:, t * KT:(t + 1) * KT],
                                               core.ident[0:S, 0:S])
                        ins.then_inc(at_psum.sem, 1)
                        pe.wait_ge(at_ready.sem, at_ready.at(b + 1))
                        pe.wait_ge(ctk_loaded[j].sem, 16 * (i + 1))
                        pe.wait_ge(hq_ready.sem, hq_ready.at(b - 1))
                        for m in range(KD):
                            for t in range(NKT):
                                ins = pe.matmul(ps[4 + j][:, m * S:(m + 1) * S], ctk[j][:, t, m * P:(m + 1) * P],
                                                AT[j][:, t, :], start=t == 0, stop=t == NKT - 1)
                        ins.then_inc(hq_psum.sem, 1)
                pe.wait_ge(m_ready.sem, 1)
                pe.transpose(ps[6][0:NB, 0:S], row_max[:, :], core.ident[0:S, 0:S]).then_inc(mt_psum.sem, 1)
                pe.wait_ge(share_ready.sem, 1)
                pe.transpose(ps[7][0:S, 0:NB], per_batch[:, :], core.ident[0:NB, 0:NB]).then_inc(share_psum.sem, 1)
                pe.wait_ge(beta_ready.sem, 1)
                for b in range(NB):
                    for k in range(KD):
                        ins = pe.matmul(ps[6][:, k * NB + b:k * NB + b + 1], N[:, b, k * P:(k + 1) * P],
                                        beta[:, b:b + 1], start=True, stop=True)
                ins.then_inc(hc_psum.sem, 1)
                with pe.Fori(0, NB // 2) as i:
                    for j in range(2):
                        b = 2 * i + j
                        pe.wait_ge(f_act.sem, 2 * (b + 1))
                        pe.wait_ge(f_pool.sem, b + 1)
                        pe.wait_ge(f_dve.sem, KD * (b + 1))
                        pe.wait_ge(x_ready.sem, x_ready.at(b - 1))
                        for k in range(8):
                            ins = pe.matmul(ps[j][0:S, 0:D], F[j][:, k, :], w["W_qv"][:, k, :], start=k == 0, stop=k == 7)
                        ins.then_inc(out_psum.sem, 1)


def top_mask(dve, chain, r, nb, ne, keep, above, same, rank, mask, below):
    full = [S, nb, ne, ne]
    other = r.unsqueeze(2).broadcast_to(full)
    this = r.unsqueeze(3).broadcast_to(full)
    chain.step(dve.tensor_tensor(above, other, this, ALU.is_gt))
    chain.step(dve.tensor_tensor(same, other, this, ALU.is_equal))
    chain.step(dve.tensor_tensor(same, same, below.unsqueeze(1).broadcast_to(full), ALU.mult))
    chain.step(dve.tensor_tensor(above, above, same, ALU.add))
    chain.step(dve.tensor_reduce(rank, above, AX.X, ALU.add))
    for n, m in zip(keep, mask):
        chain.step(dve.tensor_scalar(m, rank, float(n), None, ALU.is_lt))


def gated_experts(core, io):
    X, N, NT, ps = core.X, core.N, core.NT, core.ps
    w = core.weights
    E = 8
    with Stage(core) as st:
        xeT = [st.sb(f"xeT{j}", [P, 4, S]) for j in range(2)]
        DF = [st.sb(f"DF{j}", [S, 2, D]) for j in range(2)]
        R = st.sb("R", [S, NB, E])
        small = st.sb("small", [S, 6, NB])
        RW = st.sb("RW", [S, NB, E])
        above, same = st.sb("above", [S, NB, E, E]), st.sb("same", [S, NB, E, E])
        rank, top1, top2, over = (st.sb(n, [S, NB, E]) for n in ("rank", "top1", "top2", "over"))
        any_over, flag = st.sb("any_over", [S, 1]), st.sb("flag", [S, 1])
        NTs = [st.sb(f"NTs{j}", [P, KD, S]) for j in range(2)]
        wb = [st.sb(f"wb{j}", [S, E]) for j in range(2)]
        wT = [st.sb(f"wT{j}", [E, S]) for j in range(2)]
        xe_psum, xeT_ready, d_psum, d_ready, sq_done = st.event(), st.event(2), st.event(8), st.event(4), st.event(4)
        own, root_ready, e_in, e_ready, any_ready, flag_psum, bias_ready = (st.event() for _ in range(7))
        nts_ready, wb_ready, wt_psum, wt_ready = st.event(), st.event(), st.event(2), st.event(2)
        base_psum, ex_psum, base_used, ex_used = st.event(2), st.event(8), st.event(2), st.event(4)
        zeros = st.sb("zeros", [S, 512])
        zeros_ready, slots_zeroed = st.event(), st.event()
        with st.block() as block:
            @block.sync
            def _(sp):
                st.heads(sp)
                sp.wait_ge(zeros_ready.sem, 1)
                for slots in core.slots_in:
                    flat = slots.rearrange("(s n) d -> s (n d)", s=S).rearrange("s (m w) -> s m w", w=512)
                    sp.dma_start(flat, pair(zeros[:, :], flat.shape[1])).then_inc(slots_zeroed.sem, 16)
                sp.wait_ge(slots_zeroed.sem, 16 * len(core.slots_in))

            @block.gpsimd
            def _(pool):
                pool.memset(zeros[:, :], 0.0).then_inc(zeros_ready.sem, 1)
                pool.tensor_tensor(X[:, :, :], X[:, :, :], pair(core.rows[0:S, B_P, :], NB),
                                   ALU.add).then_inc(bias_ready.sem, 1)
                pool.wait_ge(sq_done.sem, sq_done.at(NB * E))
                pool.tensor_tensor(R[:, :, :], R[:, :, :], core.half[:, :].rearrange("s (b e) -> s b e", b=NB),
                                   ALU.pow).then_inc(root_ready.sem, 1)

            @block.tensor
            def _(pe):
                pe.wait_ge(core.loaded["gated"], core.loads["gated"])
                with pe.Fori(0, NB // 2) as i:
                    for j in range(2):
                        b = 2 * i + j
                        pe.wait_ge(xeT_ready.sem, xeT_ready.at(b - 1))
                        for q in range(4):
                            for k in range(KD):
                                ins = pe.matmul(ps[j][:, q * S:(q + 1) * S], w["Vg"][:, k, q * P:(q + 1) * P],
                                                NT[:, k, token(b)], start=k == 0, stop=k == KD - 1)
                        ins.then_inc(xe_psum.sem, 1)
                        pe.wait_ge(xeT_ready.sem, xeT_ready.at(b + 1))
                        for q in range(4):
                            pe.wait_ge(d_ready.sem, d_ready.at(4 * b + q - 3))
                            pe.matmul(ps[2 + q][0:S, :], xeT[j][:, q, :], w["VgT"][:, q, :], start=True,
                                      stop=True).then_inc(d_psum.sem, 1)
                pe.wait_ge(any_ready.sem, 1)
                pe.matmul(ps[6][0:S, 0:1], core.ones[0:S, 0:S], any_over[:, :], start=True,
                          stop=True).then_inc(flag_psum.sem, 1)
                with pe.Fori(0, NB // 2) as i:
                    for j in range(2):
                        b = 2 * i + j
                        pe.wait_ge(wb_ready.sem, b + 1)
                        pe.wait_ge(wt_ready.sem, wt_ready.at(b - 1))
                        pe.transpose(ps[6 + j][0:E, 0:S], wb[j][:, :], core.ident[0:S, 0:S]).then_inc(wt_psum.sem, 1)
                        pe.wait_ge(nts_ready.sem, b + 1)
                        pe.wait_ge(wt_ready.sem, wt_ready.at(b + 1))
                        pe.wait_ge(base_used.sem, base_used.at(b - 1))
                        for k in range(KD):
                            pe.matmul(ps[j][0:S, 0:D], NTs[j][:, k, :], w["Wp"][:, k, :], start=k == 0, stop=False)
                        pe.matmul(ps[j][0:S, 0:D], wT[j][:, :], w["be"][:, :], start=False,
                                  stop=True).then_inc(base_psum.sem, 1)
                        for q in range(4):
                            pe.wait_ge(ex_used.sem, ex_used.at(4 * b + q - 3))
                            for k in range(KD):
                                ins = pe.matmul(ps[2 + q][0:S, :], NTs[j][:, k, :],
                                                w["We"][:, k, q * 512:(q + 1) * 512], start=k == 0, stop=k == KD - 1)
                            ins.then_inc(ex_psum.sem, 1)

            @block.vector
            def _(dve):
                chain = Chain(dve, own)
                with dve.Fori(0, NB // 2) as i:
                    for j in range(2):
                        b = 2 * i + j
                        for q in range(4):
                            dve.wait_ge(d_psum.sem, d_psum.at(4 * b + q + 1))
                            dve.wait_ge(sq_done.sem, sq_done.at(8 * b + 2 * q - 2))
                            dve.tensor_tensor(DF[q % 2][:, :, :], ps[2 + q][0:S, :].rearrange("s (e d) -> s e d", e=2),
                                              N[:, bass.ds(b, 1), :].broadcast_to([S, 2, D]),
                                              ALU.subtract).then_inc(d_ready.sem, 1)
                dve.wait_ge(root_ready.sem, 1)
                chain.step(dve.tensor_reduce(small[:, 0, :], R[:, :, :], AX.X, ALU.min))
                dve.tensor_tensor(R[:, :, :], wide(small[:, 0, :], E), R[:, :, :], ALU.subtract).then_inc(e_in.sem, 1)
                dve.wait_ge(e_ready.sem, 1)
                chain.step(dve.tensor_reduce(small[:, 1, :], RW[:, :, :], AX.X, ALU.add))
                chain.step(dve.reciprocal(small[:, 2, :], small[:, 1, :]))
                chain.step(dve.tensor_tensor(RW[:, :, :], RW[:, :, :], wide(small[:, 2, :], E), ALU.mult))
                top_mask(dve, chain, RW[:, :, :], NB, E, (1, 2), above[:, :, :, :], same[:, :, :, :], rank[:, :, :],
                         (top1[:, :, :], top2[:, :, :]), core.below[:, 0:E, 0:E])
                chain.step(dve.tensor_scalar(over[:, :, :], RW[:, :, :], 1.0 / E, None, ALU.is_gt))
                dve.tensor_reduce(any_over[:, :], over[:, :, :], AX.XY, ALU.max).then_inc(any_ready.sem, 1)
                dve.wait_ge(flag_psum.sem, 1)
                chain.step(dve.tensor_scalar(flag[:, :], ps[6][0:S, 0:1], 0.0, None, ALU.is_gt))
                chain.step(dve.tensor_tensor(over[:, :, :], over[:, :, :], top1[:, :, :], ALU.subtract))
                chain.step(dve.scalar_tensor_tensor(over[:, :, :], over[:, :, :], flag[:, :], top1[:, :, :], ALU.mult,
                                                    ALU.add))
                chain.step(dve.tensor_tensor(over[:, :, :], over[:, :, :], top2[:, :, :], ALU.mult))
                chain.step(dve.tensor_tensor(RW[:, :, :], RW[:, :, :], over[:, :, :], ALU.mult))
                chain.step(dve.tensor_reduce(small[:, 3, :], RW[:, :, :], AX.X, ALU.add))
                chain.step(dve.tensor_scalar(small[:, 4, :], small[:, 3, :], 0.0, None, ALU.is_equal))
                chain.step(dve.tensor_tensor(small[:, 3, :], small[:, 3, :], small[:, 4, :], ALU.add))
                chain.step(dve.reciprocal(small[:, 5, :], small[:, 3, :]))
                chain.step(dve.tensor_tensor(RW[:, :, :], RW[:, :, :], wide(small[:, 5, :], E), ALU.mult))
                dve.wait_ge(bias_ready.sem, 1)
                with dve.Fori(0, NB // 2) as i:
                    chain.loop(i, 8)
                    for j in range(2):
                        b = 2 * i + j
                        dve.wait_ge(wt_psum.sem, wt_psum.at(b - 1))
                        dve.tensor_copy(wb[j][:, :].unsqueeze(1), RW[:, bass.ds(b, 1), :]).then_inc(wb_ready.sem, 1)
                        xb = X[:, bass.ds(b, 1), :]
                        dve.wait_ge(base_psum.sem, base_psum.at(b + 1))
                        dve.tensor_tensor(xb, xb, ps[j][0:S, 0:D].unsqueeze(1), ALU.add).then_inc(base_used.sem, 1)
                        dve.wait_ge(base_used.sem, base_used.at(b + 1))
                        dve.wait_ge(wb_ready.sem, b + 1)
                        for q in range(4):
                            dve.wait_ge(ex_psum.sem, ex_psum.at(4 * b + q + 1))
                            chain.step(dve.scalar_tensor_tensor(
                                xb, ps[2 + q][0:S, 0:D].unsqueeze(1), wb[j][:, 2 * q:2 * q + 1], xb, ALU.mult, ALU.add))
                            dve.scalar_tensor_tensor(
                                xb, ps[2 + q][0:S, D:2 * D].unsqueeze(1), wb[j][:, 2 * q + 1:2 * q + 2], xb, ALU.mult,
                                ALU.add).then_inc(ex_used.sem, 1)
                            dve.wait_ge(ex_used.sem, ex_used.at(4 * b + q + 1))
                chain.end(NB // 2)

            @block.scalar
            def _(act):
                with act.Fori(0, NB // 2) as i:
                    for j in range(2):
                        b = 2 * i + j
                        act.wait_ge(xe_psum.sem, b + 1)
                        act.wait_ge(d_psum.sem, d_psum.at(4 * (b - 1)))
                        act.activation(xeT[j][:, :, :], ps[j][:, 0:4 * S].rearrange("p (q s) -> p q s", q=4),
                                       ACT.Copy).then_inc(xeT_ready.sem, 1)
                        for q in range(4):
                            act.wait_ge(d_ready.sem, d_ready.at(4 * b + q + 1))
                            for c in range(2):
                                act.activation(DF[q % 2][:, c, :], DF[q % 2][:, c, :], ACT.Square,
                                               accum_out=R[:, bass.ds(b, 1), 2 * q + c]).then_inc(sq_done.sem, 1)
                act.wait_ge(e_in.sem, 1)
                act.activation(RW[:, :, :], R[:, :, :], ACT.Exp).then_inc(e_ready.sem, 1)
                with act.Fori(0, NB // 2) as i:
                    for j in range(2):
                        b = 2 * i + j
                        act.wait_ge(ex_psum.sem, ex_psum.at(4 * (b - 1)))
                        act.activation(NTs[j][:, :, :], NT[:, :, token(b)], ACT.Copy).then_inc(nts_ready.sem, 1)
                        act.wait_ge(wt_psum.sem, wt_psum.at(b + 1))
                        act.activation(wT[j][:, :], ps[6 + j][0:E, 0:S], ACT.Copy).then_inc(wt_ready.sem, 1)


LAG_T, LAG_V = 3, 5
ROUND = 4


def head64_attention(core, io):
    X, N, NT, ps = core.X, core.N, core.NT, core.ps
    w = core.weights
    with Stage(core) as st:
        ctT = [st.sb(f"ctT{j}", [P, KD, KVP]) for j in range(2)]
        QH = [st.sb(f"QH{c}", [P, 8, S]) for c in range(2)]
        KTr = st.sb("KTr", [P, 8, KVP])
        V = st.sb("V", [KT, NKT, 1024])
        A = [st.sb(f"A{c}", [S, KVP]) for c in range(4)]
        AT = [st.sb(f"AT{c}", [KT, NKT, 2, S]) for c in range(2)]
        OT = st.sb("OT", [P, 8, S])
        O = st.sb("O", [S, D])
        bq8 = st.sb("bq8", [P, 8])
        neg_max, total, inv = st.sb("neg_max", [S, 4]), st.sb("total", [S, 4]), st.sb("inv", [S, 4])
        stats, mv, rstd = st.sb("stats", [S, 1, 6]), st.sb("mv", [S, 3]), st.sb("rstd", [S, 1])
        ctx_loaded = [st.event(), st.event()]
        zeroed, rows_added = st.event(), st.event()
        q_psum, q_ready, k_psum, k_ready, v_psum, v_ready = (st.event(8) for _ in range(6))
        s_psum, max_ready, exp_ready, norm_ready, at_psum, at_ready = (st.event(4) for _ in range(6))
        av_psum, ot_ready, o_psum, o_used, var_ready, rstd_ready, own, x_ready = \
            st.event(2), st.event(4), st.event(1), st.event(1), st.event(), st.event(), st.event(), st.event()
        with st.block() as block:
            @block.sync
            def _(sp):
                st.heads(sp)
                with sp.Fori(0, NB // 2) as i:
                    for j in range(2):
                        b = 2 * i + j
                        sp.wait_ge(v_psum.sem, v_psum.at(6 * b - 6))
                        sp.dma_start(ctT[j][:, :, :], io["ctT"][bass.ds(b, 1)]).then_inc(ctx_loaded[j].sem, 16)

            @block.gpsimd
            def _(pool):
                pool.memset(QH[0][64:P, :, :], 0.0).then_inc(zeroed.sem, 1)
                pool.memset(QH[1][0:64, :, :], 0.0).then_inc(zeroed.sem, 1)
                pool.wait_ge(zeroed.sem, 2)
                for c in range(4):
                    pool.memset(A[c][:, KV:KVP], 0.0).then_inc(zeroed.sem, 1)
                pool.tensor_tensor(N[:, :, :], N[:, :, :], pair(core.rows[0:S, L1_BO, :], NB),
                                   ALU.add).then_inc(rows_added.sem, 1)
                pool.tensor_tensor(X[:, :, :], X[:, :, :], pair(core.rows[0:S, BETA, :], NB),
                                   ALU.add).then_inc(rows_added.sem, 1)
                with pool.Fori(0, NB) as b:
                    pool.wait_ge(var_ready.sem, b + 1)
                    pool.tensor_tensor(rstd[:, :], mv[:, 1:2], core.minus_half[:, 0:1], ALU.pow).then_inc(rstd_ready.sem, 1)

            def bank_free(eng, b, u):
                if u < 4:
                    eng.wait_ge(exp_ready.sem, exp_ready.at(NH * b + u - 3))
                elif u < 6:
                    eng.wait_ge(q_ready.sem, q_ready.at(4 * b + 2 * (u - 3)))
                elif u < 14:
                    eng.wait_ge(k_ready.sem, k_ready.at(8 * b + u - 5))
                elif u < 20:
                    eng.wait_ge(v_ready.sem, v_ready.at(6 * b + u - 13))
                else:
                    eng.wait_ge(exp_ready.sem, exp_ready.at(NH * b + u - 19))

            @block.tensor
            def _(pe):
                pe.wait_ge(core.loaded["head64"], core.loads["head64"])
                pe.wait_ge(zeroed.sem, 6)

                def query(b, u):
                    bank_free(pe, b, u)
                    for c in range(4):
                        t = 4 * u + c
                        for k in range(KD):
                            ins = pe.matmul(ps[u % 4][:, c * S:(c + 1) * S], w["Wq"][:, k, t * P:(t + 1) * P],
                                            NT[:, k, token(b)], start=k == 0, stop=k == KD - 1)
                    ins.then_inc(q_psum.sem, 1)

                def key(b, j, i, t):
                    u = 2 + t
                    if t == 0:
                        pe.wait_ge(ctx_loaded[j].sem, 16 * (i + 1))
                    bank_free(pe, b, u)
                    for k in range(KD):
                        ins = pe.matmul(ps[u % 4][:, 0:KV], w["Wk"][:, k, t * P:(t + 1) * P], ctT[j][:, k, 0:KV],
                                        start=k == 0, stop=k == KD - 1)
                    ins.then_inc(k_psum.sem, 1)

                def run(b, j, i, more):
                    for t in range(NKT):
                        for c in range(2):
                            u = 10 + 2 * t + c
                            bank_free(pe, b, u)
                            for k in range(KD):
                                ins = pe.matmul(ps[u % 4][0:KT, :], ctT[j][:, k, t * KT:(t + 1) * KT],
                                                w["Wv"][:, k, 512 * c:512 * (c + 1)], start=k == 0, stop=k == KD - 1)
                            ins.then_inc(v_psum.sem, 1)
                    for h in range(NH + LAG_V + 1):
                        if h < NH:
                            u = 16 + h
                            bank_free(pe, b, u)
                            if h == 0:
                                pe.wait_ge(q_ready.sem, q_ready.at(4 * b + 4))
                            pe.wait_ge(k_ready.sem, k_ready.at(8 * b + h // 2 + 1))
                            pe.matmul(ps[u % 4][0:S, 0:KV], QH[h % 2][:, h // 2, :], KTr[:, h // 2, 0:KV],
                                      start=True, stop=True).then_inc(s_psum.sem, 1)
                        g = h - LAG_T
                        if 0 <= g < NH:
                            pe.wait_ge(norm_ready.sem, norm_ready.at(NH * b + g + 1))
                            pe.wait_ge(at_ready.sem, at_ready.at(NH * b + g - 1))
                            for t in range(NKT):
                                ins = pe.transpose(ps[4 + g % 2][0:KT, t * S:(t + 1) * S],
                                                   A[g % 4][:, t * KT:(t + 1) * KT], core.ident[0:S, 0:S])
                            ins.then_inc(at_psum.sem, 1)
                        g = h - LAG_V
                        if 0 <= g < NH and g % 2:
                            m = g // 2
                            pe.wait_ge(at_ready.sem, at_ready.at(NH * b + g + 1))
                            pe.wait_ge(v_ready.sem, v_ready.at(6 * b + 6))
                            pe.wait_ge(ot_ready.sem, ot_ready.at(16 * b + 2 * m - 2))
                            if m == 0:
                                pe.wait_ge(o_used.sem, o_used.at(b))
                            for t in range(NKT):
                                ins = pe.matmul(ps[6 + m % 2][:, 0:2 * S], V[:, t, m * P:(m + 1) * P],
                                                AT[m % 2][:, t, :, :].rearrange("p c s -> p (c s)"), start=t == 0,
                                                stop=t == NKT - 1)
                            ins.then_inc(av_psum.sem, 1)
                        if more and h == NH:
                            query(b + 1, 0)
                            query(b + 1, 1)
                        if more and NH < h <= NH + 4:
                            key(b + 1, 1 - j, i + j, 2 * (h - NH) - 2)
                            key(b + 1, 1 - j, i + j, 2 * (h - NH) - 1)
                    pe.wait_ge(ot_ready.sem, ot_ready.at(16 * b + 16))
                    for t in range(8):
                        ins = pe.matmul(ps[6][0:S, 0:D], OT[:, t, :], w["Wo"][:, t, :], start=t == 0, stop=t == 7)
                    ins.then_inc(o_psum.sem, 1)

                query(0, 0)
                query(0, 1)
                for t in range(8):
                    key(0, 0, 0, t)
                batches(pe, run)

            @block.vector
            def _(dve):
                chain = Chain(dve, own)
                dve.wait_ge(core.loaded["head64"], core.loads["head64"])
                dve.wait_ge(zeroed.sem, 6)
                dve.wait_ge(rows_added.sem, 2)
                chain.step(dve.tensor_scalar(bq8[:, :], w["bq"][:, :], 0.125, None, ALU.mult))

                def query(b):
                    for u in range(2):
                        dve.wait_ge(q_psum.sem, q_psum.at(2 * b + u + 1))
                        if u == 0:
                            dve.wait_ge(s_psum.sem, s_psum.at(NH * b))
                        for c in range(2):
                            half = slice(64 * c, 64 * c + 64)
                            dve.scalar_tensor_tensor(
                                QH[c][half, 4 * u:4 * u + 4, :],
                                ps[u][half, 0:4 * S].rearrange("p (q s) -> p q s", q=4), 0.125,
                                wide(bq8[half, 4 * u:4 * u + 4], S), ALU.mult, ALU.add).then_inc(q_ready.sem, 1)

                def run(b, j, i, more):
                    for t in range(6):
                        dve.wait_ge(v_psum.sem, v_psum.at(6 * b + t + 1))
                        if t == 0:
                            dve.wait_ge(av_psum.sem, av_psum.at(8 * b))
                        dve.tensor_copy(V[:, t // 2, 512 * (t % 2):512 * (t % 2) + 512],
                                        ps[(10 + t) % 4][0:KT, :]).then_inc(v_ready.sem, 1)
                    for h in range(NH + LAG_V + 2):
                        if h < NH:
                            dve.wait_ge(s_psum.sem, s_psum.at(NH * b + h + 1))
                            dve.tensor_reduce(neg_max[:, h % 4:h % 4 + 1], ps[(16 + h) % 4][0:S, 0:KV], AX.X,
                                              ALU.max, negate=True).then_inc(max_ready.sem, 1)
                        g = h - 1
                        if 0 <= g < NH:
                            dve.wait_ge(exp_ready.sem, exp_ready.at(NH * b + g + 1))
                            chain.step(dve.reciprocal(inv[:, g % 4:g % 4 + 1], total[:, g % 4:g % 4 + 1]))
                            dve.tensor_scalar(A[g % 4][:, 0:KV], A[g % 4][:, 0:KV], inv[:, g % 4:g % 4 + 1], None,
                                              ALU.mult).then_inc(norm_ready.sem, 1)
                        g = h - LAG_V - 1
                        if 0 <= g < NH and g % 2:
                            m = g // 2
                            dve.wait_ge(av_psum.sem, av_psum.at(8 * b + m + 1))
                            if m == 0:
                                dve.wait_ge(o_psum.sem, o_psum.at(b))
                            for c in range(2):
                                half = slice(64 * c, 64 * c + 64)
                                dve.tensor_scalar(OT[half, m, :], ps[6 + m % 2][half, c * S:(c + 1) * S],
                                                  w["bv"][half, m:m + 1], None, ALU.add).then_inc(ot_ready.sem, 1)
                        if more and h == NH + 1:
                            query(b + 1)
                    dve.wait_ge(o_psum.sem, o_psum.at(b + 1))
                    dve.tensor_tensor(O[:, :], ps[6][0:S, 0:D], N[:, bass.ds(b, 1), :], ALU.add).then_inc(o_used.sem, 1)
                    dve.wait_ge(o_used.sem, o_used.at(b + 1))
                    chain.step(dve.bn_stats(stats[:, 0, :], O[:, :]))
                    variance(dve, chain, stats[:, :, :], mv[:, 0:1], mv[:, 2:3], mv[:, 1:2]).then_inc(var_ready.sem, 1)
                    chain.step(dve.tensor_scalar(mv[:, 0:1], mv[:, 0:1], 0.5, None, ALU.mult))
                    dve.wait_ge(rstd_ready.sem, b + 1)
                    chain.step(dve.tensor_scalar(O[:, :], O[:, :], mv[:, 0:1], rstd[:, :], ALU.subtract, ALU.mult))
                    dve.tensor_tensor(O[:, :], O[:, :], core.rows[0:S, GAMMA, :], ALU.mult).then_inc(x_ready.sem, 1)
                    dve.wait_ge(x_ready.sem, 2 * b + 1)
                    xb = X[:, bass.ds(b, 1), :]
                    dve.tensor_tensor(xb, xb, O[:, :].unsqueeze(1), ALU.add).then_inc(x_ready.sem, 1)
                    dve.wait_ge(x_ready.sem, 2 * b + 2)

                query(0)
                batches(dve, run, chain, NH + 8)

            @block.scalar
            def _(act):
                act.wait_ge(core.loaded["head64"], core.loads["head64"])

                def key(b, t):
                    act.wait_ge(k_psum.sem, k_psum.at(8 * b + t + 1))
                    if t == 0:
                        act.wait_ge(s_psum.sem, s_psum.at(NH * b))
                    act.activation(KTr[:, t, 0:KV], ps[(2 + t) % 4][:, 0:KV], ACT.Identity,
                                   bias=w["bk"][:, t:t + 1]).then_inc(k_ready.sem, 1)

                def run(b, j, i, more):
                    for h in range(NH + LAG_T + 2):
                        if h < NH:
                            act.wait_ge(max_ready.sem, max_ready.at(NH * b + h + 1))
                            act.wait_ge(at_psum.sem, at_psum.at(NH * b + h - 3))
                            act.activation(A[h % 4][:, 0:KV], ps[(16 + h) % 4][0:S, 0:KV], ACT.Exp,
                                           bias=neg_max[:, h % 4:h % 4 + 1],
                                           accum_out=total[:, h % 4:h % 4 + 1]).then_inc(exp_ready.sem, 1)
                        g = h - LAG_T
                        if 0 <= g < NH:
                            act.wait_ge(at_psum.sem, at_psum.at(NH * b + g + 1))
                            act.wait_ge(av_psum.sem, av_psum.at(8 * b + g // 2 - 1))
                            act.activation(AT[g // 2 % 2][:, :, g % 2, :],
                                           ps[4 + g % 2][0:KT, 0:NKT * S].rearrange("p (t s) -> p t s", t=NKT),
                                           ACT.Copy).then_inc(at_ready.sem, 1)
                        if more and NH < h <= NH + 4:
                            key(b + 1, 2 * (h - NH) - 2)
                            key(b + 1, 2 * (h - NH) - 1)

                for t in range(8):
                    key(0, t)
                batches(act, run)


def ternary_ffn(core, io):
    X, N, NT, ps = core.X, core.N, core.NT, core.ps
    HT = 8
    with Stage(core) as st:
        w1, w2 = st.sb("w1", [P, KD, 1024]), st.sb("w2", [P, HT, D])
        conv_w, conv_b = st.sb("conv_w", [P, HT, 3]), st.sb("conv_b", [P, HT])
        w1q, w2q = st.sb("w1q", [P, KD, 1024], BF16), st.sb("w2q", [P, HT, D], BF16)
        part = st.sb("part", [P, 2])
        wmean, winv = st.sb("wmean", [P, 2]), st.sb("winv", [P, 2])
        am, scale, inv, inv2 = (st.sb(n, [S, NB]) for n in ("am", "scale", "inv", "inv2"))
        am2, scale2 = st.sb("am2", [S, 4]), st.sb("scale2", [S, 1])
        tmp = st.sb("tmp", [S, D])
        Q = [st.sb(f"Q{j}", [S, D], BF16) for j in range(2)]
        QT = [st.sb(f"QT{j}", [P, KD, S], BF16) for j in range(2)]
        inv_rows = st.sb("inv_rows", [P, T])
        HP = st.sb("HP", [P, HT, S + 2])
        C = [st.sb(f"C{j}", [P, HT, S]) for j in range(2)]
        tmp2 = st.sb("tmp2", [S, 1024])
        Q2 = st.sb("Q2", [S, 1024], BF16)
        Q2T = [st.sb(f"Q2T{j}", [P, HT, S], BF16) for j in range(2)]
        w_loaded, c_loaded, own, own_pool, part_ready, mean_psum, w_ready, pads, inv_ready = (st.event() for _ in range(9))
        q_ready, qt_psum, qt_ready, rows_psum, h_psum, hp_ready = (st.event(4) for _ in range(6))
        rows_ready = st.event()
        c_ready, conv_ready, silu_ready, ht_psum, q2_ready, q2t_psum, q2t_ready, y_psum, x_ready = \
            (st.event(4) for _ in range(9))
        amax_ready, q2_used = st.event(2), st.event(2)
        with st.block() as block:
            @block.sync
            def _(sp):
                st.heads(sp)
                sp.dma_start(w1[:, :, :], io["w1"]).then_inc(w_loaded.sem, 16)
                sp.dma_start(w2[:, :, :], io["w2"]).then_inc(w_loaded.sem, 16)
                sp.dma_start(conv_w[:, :, :], io["conv_w"]).then_inc(c_loaded.sem, 16)
                sp.dma_start(conv_b[:, :], io["conv_b"]).then_inc(c_loaded.sem, 16)

            @block.gpsimd
            def _(pool):
                pool.memset(HP[:, :, 0:1], 0.0).then_inc(pads.sem, 1)
                pool.memset(HP[:, :, S + 1:S + 2], 0.0).then_inc(pads.sem, 1)

            @block.tensor
            def _(pe):
                pe.wait_ge(part_ready.sem, 2)
                pe.matmul(ps[7][:, 0:2], core.ones[:, :], part[:, :], start=True, stop=True).then_inc(mean_psum.sem, 1)
                pe.wait_ge(w_ready.sem, 2)
                pe.wait_ge(inv_ready.sem, 1)
                for b in range(NB):
                    ins = pe.matmul(ps[4 + b // 4][:, (b % 4) * S:(b % 4 + 1) * S],
                                    inv[:, b:b + 1].broadcast_to([S, P]), core.ident[0:S, 0:S], start=True, stop=True)
                ins.then_inc(rows_psum.sem, 1)
                pe.wait_ge(rows_ready.sem, 2)
                with pe.Fori(0, NB // 2) as i:
                    for j in range(2):
                        b = 2 * i + j
                        pe.wait_ge(q_ready.sem, q_ready.at(b + 1))
                        pe.wait_ge(qt_ready.sem, qt_ready.at(b))
                        for k in range(KD):
                            ins = pe.transpose(ps[0][:, :].bitcast(BF16)[:, k * S:(k + 1) * S], Q[j][:, k * P:(k + 1) * P],
                                               core.identb[0:S, 0:S])
                        ins.then_inc(qt_psum.sem, 1)
                        pe.wait_ge(qt_ready.sem, qt_ready.at(b + 1))
                        pe.wait_ge(hp_ready.sem, hp_ready.at(2 * b))
                        for t in range(HT):
                            for k in range(KD):
                                ins = pe.matmul(ps[2 + t // 4][:, (t % 4) * S:(t % 4 + 1) * S],
                                                w1q[:, k, t * P:(t + 1) * P], QT[j][:, k, :], start=k == 0, stop=k == KD - 1)
                            if t % 4 == 3:
                                ins.then_inc(h_psum.sem, 1)
                        pe.wait_ge(silu_ready.sem, silu_ready.at(b + 1))
                        pe.wait_ge(q2_used.sem, q2_used.at(2 * b))
                        for t in range(HT):
                            ins = pe.transpose(ps[4 + t // 4][0:S, (t % 4) * P:(t % 4 + 1) * P], C[j][:, t, :],
                                               core.ident[:, :])
                            if t % 4 == 3:
                                ins.then_inc(ht_psum.sem, 1)
                        pe.wait_ge(q2_ready.sem, q2_ready.at(b + 1))
                        pe.wait_ge(q2t_ready.sem, q2t_ready.at(b))
                        for t in range(HT):
                            ins = pe.transpose(ps[6][:, :].bitcast(BF16)[:, t * S:(t + 1) * S], Q2[:, t * P:(t + 1) * P],
                                               core.identb[0:S, 0:S])
                        ins.then_inc(q2t_psum.sem, 1)
                        pe.wait_ge(q2t_ready.sem, q2t_ready.at(b + 1))
                        pe.wait_ge(x_ready.sem, x_ready.at(b))
                        for t in range(HT):
                            ins = pe.matmul(ps[7][0:S, 0:D], Q2T[j][:, t, :], w2q[:, t, :], start=t == 0, stop=t == HT - 1)
                        ins.then_inc(y_psum.sem, 1)

            @block.vector
            def _(dve):
                chain = Chain(dve, own)
                dve.wait_ge(w_loaded.sem, 32)
                for n, wt in enumerate((w1, w2)):
                    dve.tensor_reduce(part[:, n:n + 1], wt[:, :, :], AX.XY, ALU.add,
                                      apply_absolute_value=True).then_inc(part_ready.sem, 1)
                dve.wait_ge(mean_psum.sem, 1)
                chain.step(dve.tensor_scalar(wmean[:, :], ps[7][:, 0:2], 1.0 / (D * 1024), 1e-5, ALU.mult, ALU.max))
                chain.step(dve.reciprocal(winv[:, :], wmean[:, :]))
                for n, (wt, wq) in enumerate(((w1, w1q), (w2, w2q))):
                    chain.step(dve.tensor_scalar(wt[:, :, :], wt[:, :, :], winv[:, n:n + 1], MAGIC, ALU.mult, ALU.add))
                    chain.step(dve.tensor_scalar(wt[:, :, :], wt[:, :, :], MAGIC - 1, MAGIC + 1, ALU.max, ALU.min))
                    dve.tensor_scalar(wq[:, :, :], wt[:, :, :], MAGIC, None, ALU.subtract).then_inc(w_ready.sem, 1)
                chain.step(dve.tensor_reduce(am[:, :], N[:, :, :], AX.X, ALU.max, apply_absolute_value=True))
                chain.step(dve.tensor_scalar(am[:, :], am[:, :], 1e-5, None, ALU.max))
                chain.step(dve.reciprocal(scale[:, :], am[:, :]))
                chain.step(dve.tensor_scalar(scale[:, :], scale[:, :], 127.0, None, ALU.mult))
                dve.tensor_scalar(inv[:, :], am[:, :], wmean[0:S, 0:1], 1.0 / 127, ALU.mult, ALU.mult).then_inc(inv_ready.sem, 1)
                dve.wait_ge(c_loaded.sem, 32)
                dve.wait_ge(pads.sem, 2)
                dve.wait_ge(rows_ready.sem, 2)
                with dve.Fori(0, NB // 2) as i:
                    chain.loop(i, 2 * (HT + 9))
                    for j in range(2):
                        b = 2 * i + j
                        sc = scale[:, bass.ds(b, 1)]
                        chain.step(dve.tensor_scalar(tmp[:, :].unsqueeze(1), N[:, bass.ds(b, 1), :], sc, MAGIC, ALU.mult,
                                                     ALU.add))
                        chain.step(dve.tensor_scalar(tmp[:, :], tmp[:, :], MAGIC - 128, MAGIC + 127, ALU.max, ALU.min))
                        dve.wait_ge(qt_psum.sem, qt_psum.at(b - 1))
                        dve.tensor_scalar(Q[j][:, :], tmp[:, :], MAGIC, None, ALU.subtract).then_inc(q_ready.sem, 1)
                        for u in range(2):
                            dve.wait_ge(h_psum.sem, h_psum.at(2 * b + u + 1))
                            dve.tensor_tensor(HP[:, 4 * u:4 * u + 4, 1:S + 1],
                                              ps[2 + u][:, 0:4 * S].rearrange("p (t s) -> p t s", t=4), pair(inv_rows[:, token(b)], 4),
                                              ALU.mult).then_inc(hp_ready.sem, 1)
                        for t in range(HT):
                            dve.wait_ge(c_ready.sem, c_ready.at(8 * b + t + 1))
                            chain.step(dve.scalar_tensor_tensor(C[j][:, t, :], HP[:, t, 1:S + 1], conv_w[:, t, 1:2],
                                                                C[j][:, t, :], ALU.mult, ALU.add))
                            dve.scalar_tensor_tensor(C[j][:, t, :], HP[:, t, 2:S + 2], conv_w[:, t, 2:3], C[j][:, t, :],
                                                     ALU.mult, ALU.add).then_inc(conv_ready.sem, 1)
                        for u in range(2):
                            dve.wait_ge(ht_psum.sem, ht_psum.at(2 * b + u + 1))
                            dve.tensor_reduce(am2[:, u:u + 1], ps[4 + u][0:S, :], AX.X, ALU.max,
                                              apply_absolute_value=True).then_inc(amax_ready.sem, 1)
                        dve.wait_ge(amax_ready.sem, amax_ready.at(2 * b + 2))
                        chain.step(dve.tensor_tensor(am2[:, 2:3], am2[:, 0:1], am2[:, 1:2], ALU.max))
                        chain.step(dve.tensor_scalar(am2[:, 2:3], am2[:, 2:3], 1e-5, None, ALU.max))
                        chain.step(dve.reciprocal(scale2[:, :], am2[:, 2:3]))
                        chain.step(dve.tensor_scalar(scale2[:, :], scale2[:, :], 127.0, None, ALU.mult))
                        chain.step(dve.tensor_scalar(am2[:, 3:4], am2[:, 2:3], wmean[0:S, 1:2], 1.0 / 127, ALU.mult, ALU.mult))
                        for u in range(2):
                            dve.tensor_scalar(tmp2[:, 512 * u:512 * u + 512], ps[4 + u][0:S, :], scale2[:, :], MAGIC,
                                              ALU.mult, ALU.add).then_inc(q2_used.sem, 1)
                        dve.wait_ge(q2_used.sem, q2_used.at(2 * b + 2))
                        chain.step(dve.tensor_scalar(tmp2[:, :], tmp2[:, :], MAGIC - 128, MAGIC + 127, ALU.max, ALU.min))
                        dve.wait_ge(q2t_psum.sem, q2t_psum.at(b))
                        dve.tensor_scalar(Q2[:, :], tmp2[:, :], MAGIC, None, ALU.subtract).then_inc(q2_ready.sem, 1)
                        dve.wait_ge(y_psum.sem, y_psum.at(b + 1))
                        xb = X[:, bass.ds(b, 1), :]
                        chain.step(dve.tensor_scalar(tmp[:, :], ps[7][0:S, 0:D], am2[:, 3:4], None, ALU.mult))
                        dve.tensor_tensor(xb, xb, tmp[:, :].unsqueeze(1), ALU.add).then_inc(x_ready.sem, 1)
                        dve.wait_ge(x_ready.sem, x_ready.at(b + 1))
                chain.end(NB // 2)

            @block.scalar
            def _(act):
                act.wait_ge(rows_psum.sem, rows_psum.at(1))
                for u in range(2):
                    act.activation(inv_rows[:, 4 * u * S:4 * (u + 1) * S], ps[4 + u][:, 0:4 * S],
                                   ACT.Copy).then_inc(rows_ready.sem, 1)
                act.wait_ge(c_loaded.sem, 32)
                with act.Fori(0, NB // 2) as i:
                    for j in range(2):
                        b = 2 * i + j
                        act.wait_ge(qt_psum.sem, qt_psum.at(b + 1))
                        act.wait_ge(h_psum.sem, h_psum.at(2 * b - 2))
                        act.activation(QT[j][:, :, :], ps[0][:, :].bitcast(BF16)[:, 0:KD * S].rearrange(
                            "p (k s) -> p k s", k=KD), ACT.Copy).then_inc(qt_ready.sem, 1)
                        for t in range(HT):
                            if t % 4 == 0:
                                act.wait_ge(hp_ready.sem, hp_ready.at(2 * b + t // 4 + 1))
                            if t == 0:
                                act.wait_ge(ht_psum.sem, ht_psum.at(2 * b - 2))
                            act.activation(C[j][:, t, :], HP[:, t, 0:S], ACT.Identity, scale=conv_w[:, t, 0:1],
                                           bias=conv_b[:, t:t + 1]).then_inc(c_ready.sem, 1)
                        act.wait_ge(conv_ready.sem, conv_ready.at(8 * b + 8))
                        act.activation(C[j][:, :, :], C[j][:, :, :], ACT.Silu).then_inc(silu_ready.sem, 1)
                        act.wait_ge(q2t_psum.sem, q2t_psum.at(b + 1))
                        act.wait_ge(y_psum.sem, y_psum.at(b - 1))
                        act.activation(Q2T[j][:, :, :], ps[6][:, :].bitcast(BF16)[:, 0:HT * S].rearrange(
                            "p (t s) -> p t s", t=HT), ACT.Copy).then_inc(q2t_ready.sem, 1)


def heads16(core, io, layer):
    X, N, NT, ps = core.X, core.N, core.NT, core.ps
    soft = layer == 2
    w = core.weights
    NHT = 8
    with Stage(core) as st:
        ctT = [st.sb(f"ctT{j}", [P, KD, KVP]) for j in range(2)]
        Kt = st.sb("Kt", [P, KD, KVP])
        Qz = st.sb("Qz", [P, KD, NHT, S])
        Vz = st.sb("Vz", [KT, NKT * KD * NHT * P + P])
        OT = [st.sb(f"OT{j}", [P, KD, S]) for j in range(2)]

        def v_blocks(t, k):
            at = (t * KD + k) * NHT * P
            return Vz[:, at:at + NHT * (P + 16)].rearrange("p (h e) -> p h e", e=P + 16)[:, :, 0:16]

        def v_head(t, h, rows=KT):
            at = (t * NH + h) * P
            return Vz[0:rows, at:at + P]

        loaded, ctx_loaded, mask_loaded = st.event(), [st.event(), st.event()], [st.event(), st.event()]
        zeroed, own = st.event(), st.event()
        q_psum, q_ready, k_psum, k_ready, v_psum, v_ready = (st.event(8) for _ in range(6))
        s_psum, max_ready, exp_ready, norm_ready, at_psum, at_ready = (st.event(4) for _ in range(6))
        masked, mask_ready = st.event(4), st.event(4)
        av_psum, ot_ready, o_psum, x_ready = (st.event(4) for _ in range(4))
        if soft:
            mask_i = [st.sb(f"mask_i{j}", [S, KV], I32) for j in range(2)]
            mask = [st.sb(f"mask{j}", [S, KV]) for j in range(2)]
            A = [st.sb(f"A{c}", [S, KVP]) for c in range(4)]
            AT = [st.sb(f"AT{c}", [KT, NKT, 2, S]) for c in range(2)]
            neg_max, total, inv = st.sb("neg_max", [S, 4]), st.sb("total", [S, 4]), st.sb("inv", [S, 4])
            wh, wo = st.sb("W_heads", [P, P]), st.sb("W_o", [P, KD, D])
        else:
            AS = st.sb("AS", [KT, NKT, NH, S])
            wq, wk, wv, wo = (st.sb(n, [P, KD, D]) for n in ("Wq", "Wk", "Wv", "Wo"))
            bq, bk = st.sb("bq", [P, KD]), st.sb("bk", [P, KD])

        with st.block() as block:
            @block.sync
            def _(sp):
                st.heads(sp)
                if soft:
                    sp.dma_start(wh[:, :], io["W_heads"]).then_inc(loaded.sem, 16)
                    sp.dma_start(wo[:, :, :], io["W_o"]).then_inc(loaded.sem, 16)
                else:
                    for name, t in (("L3_Wq", wq), ("L3_Wk", wk), ("L3_Wv", wv), ("L3_Wo", wo)):
                        sp.dma_start(t[:, :, :], io[name]).then_inc(loaded.sem, 16)
                    for name, t in (("L3_bq", bq), ("L3_bk", bk)):
                        sp.dma_start(t[:, :], io[name]).then_inc(loaded.sem, 16)
                with sp.Fori(0, NB // 2) as i:
                    for j in range(2):
                        b = 2 * i + j
                        sp.wait_ge(v_psum.sem, v_psum.at(4 * b - 4))
                        sp.dma_start(ctT[j][:, :, :], io["ctT"][bass.ds(b, 1)]).then_inc(ctx_loaded[j].sem, 16)
                        if soft:
                            sp.wait_ge(mask_ready.sem, mask_ready.at(b - 1))
                            sp.dma_start(mask_i[j][:, :], io["mask"][bass.ds(b, 1)]).then_inc(mask_loaded[j].sem, 16)

            @block.gpsimd
            def _(pool):
                pool.memset(Vz[:, :], 0.0).then_inc(zeroed.sem, 1)
                pool.wait_ge(zeroed.sem, 1)
                if not soft:
                    pool.tensor_tensor(X[:, :, :], X[:, :, :], pair(core.rows[0:S, L3_BO, :], NB),
                                       ALU.add).then_inc(zeroed.sem, 1)
                else:
                    for c in range(4):
                        pool.memset(A[c][:, KV:KVP], 0.0).then_inc(zeroed.sem, 1)

            heads_zeroed = 5 if soft else 2

            def bank_free(eng, b, u):
                n = NH if soft else 12
                if u < 4:
                    eng.wait_ge(exp_ready.sem, exp_ready.at(n * b + u - 3))
                elif u < 6:
                    eng.wait_ge(q_ready.sem, q_ready.at(2 * b + u - 3))
                elif u < 8:
                    eng.wait_ge(k_ready.sem, k_ready.at(2 * b + u - 5))
                elif u < 12:
                    eng.wait_ge(v_ready.sem, v_ready.at(4 * b + u - 7))
                else:
                    eng.wait_ge(exp_ready.sem, exp_ready.at(n * b + u - 11))

            V_USES = [[(0, 0), (0, 1)], [(0, 2)], [(1, 0), (1, 1)], [(1, 2)]]

            @block.tensor
            def _(pe):
                pe.wait_ge(loaded.sem, 32 if soft else 96)
                pe.wait_ge(zeroed.sem, heads_zeroed)

                def queries_and_keys(b, j, i):
                    pe.wait_ge(ctx_loaded[j].sem, 16 * (i + 1))
                    for m in range(KD):
                        bank_free(pe, b, m)
                        if soft:
                            ins = pe.matmul(ps[m][:, 0:S], wh[:, :], NT[:, m, token(b)], start=True, stop=True)
                        else:
                            for k in range(KD):
                                ins = pe.matmul(ps[m][:, 0:S], wq[:, k, m * P:(m + 1) * P], NT[:, k, token(b)],
                                                start=k == 0, stop=k == KD - 1)
                        ins.then_inc(q_psum.sem, 1)
                    for m in range(KD):
                        bank_free(pe, b, 2 + m)
                        if soft:
                            ins = pe.matmul(ps[2 + m][:, 0:KVP], wh[:, :], ctT[j][:, m, :], start=True, stop=True)
                        else:
                            for k in range(KD):
                                ins = pe.matmul(ps[2 + m][:, 0:KVP], wk[:, k, m * P:(m + 1) * P], ctT[j][:, k, :],
                                                start=k == 0, stop=k == KD - 1)
                        ins.then_inc(k_psum.sem, 1)
                def run(b, j, i, more):
                    for c, tiles in enumerate(V_USES):
                        bank_free(pe, b, 4 + c)
                        for n, (m, t) in enumerate(tiles):
                            out = ps[c][0:KT, n * P:(n + 1) * P]
                            rows = slice(t * KT, (t + 1) * KT)
                            if soft:
                                ins = pe.matmul(out, ctT[j][:, m, rows], wh[:, :], start=True, stop=True)
                            else:
                                for k in range(KD):
                                    ins = pe.matmul(out, ctT[j][:, k, rows], wv[:, k, m * P:(m + 1) * P],
                                                    start=k == 0, stop=k == KD - 1)
                        ins.then_inc(v_psum.sem, 1)
                    if soft:
                        for h in range(NH + LAG_V + 1):
                            if h < NH:
                                u = 8 + h
                                bank_free(pe, b, u)
                                pe.wait_ge(q_ready.sem, q_ready.at(2 * b + h // 8 + 1))
                                pe.wait_ge(k_ready.sem, k_ready.at(2 * b + h // 8 + 1))
                                pe.matmul(ps[u % 4][0:S, 0:KV], Qz[:, h // 8, h % 8, :], Kt[:, h // 8, 0:KV],
                                          start=True, stop=True).then_inc(s_psum.sem, 1)
                            g = h - LAG_T
                            if 0 <= g < NH:
                                pe.wait_ge(norm_ready.sem, norm_ready.at(NH * b + g + 1))
                                pe.wait_ge(at_ready.sem, at_ready.at(NH * b + g - 1))
                                for t in range(NKT):
                                    ins = pe.transpose(ps[4 + g % 2][0:KT, t * S:(t + 1) * S],
                                                       A[g % 4][:, t * KT:(t + 1) * KT], core.ident[0:S, 0:S])
                                ins.then_inc(at_psum.sem, 1)
                            g = h - LAG_V
                            if 0 <= g < NH:
                                pe.wait_ge(at_ready.sem, at_ready.at(NH * b + g + 1))
                                pe.wait_ge(v_ready.sem, v_ready.at(4 * b + 4))
                                if g == 0:
                                    pe.wait_ge(x_ready.sem, x_ready.at(b))
                                for t in range(NKT):
                                    ins = pe.matmul(ps[6 + g // 8][:, 0:S], v_head(t, g), AT[g // 2 % 2][:, t, g % 2, :],
                                                    start=g % 8 == 0 and t == 0, stop=g % 8 == 7 and t == NKT - 1)
                                ins.then_inc(av_psum.sem, 1)
                            if more and h == NH:
                                queries_and_keys(b + 1, 1 - j, i + j)
                    else:
                        pe.wait_ge(q_ready.sem, q_ready.at(2 * b + 2))
                        pe.wait_ge(k_ready.sem, k_ready.at(2 * b + 2))
                        for u in range(12):
                            m, t, half = u // 6, u // 2 % 3, u % 2
                            bank_free(pe, b, 8 + u)
                            rows = KT if t < NKT - 1 else KV - (NKT - 1) * KT
                            pe.matmul(ps[u % 4][0:rows, 0:4 * S], Kt[:, m, t * KT:t * KT + rows],
                                      Qz[:, m, 4 * half:4 * half + 4, :].rearrange("p h s -> p (h s)"), start=True,
                                      stop=True).then_inc(s_psum.sem, 1)
                        if more:
                            queries_and_keys(b + 1, 1 - j, i + j)
                        for m in range(KD):
                            pe.wait_ge(v_ready.sem, v_ready.at(4 * b + 4))
                            pe.wait_ge(exp_ready.sem, exp_ready.at(12 * b + 6 * m + 6))
                            if m == 0:
                                pe.wait_ge(x_ready.sem, x_ready.at(b))
                            for g in range(NHT):
                                for t in range(NKT):
                                    rows = KT if t < NKT - 1 else KV - (NKT - 1) * KT
                                    ins = pe.matmul(ps[6 + m][:, 0:S], v_head(t, NHT * m + g, rows),
                                                    AS[0:rows, t, NHT * m + g, :], start=g == 0 and t == 0,
                                                    stop=g == NHT - 1 and t == NKT - 1)
                            ins.then_inc(av_psum.sem, 1)
                    pe.wait_ge(ot_ready.sem, ot_ready.at(2 * b + 2))
                    for k in range(KD):
                        ins = pe.matmul(ps[6][0:S, 0:D], OT[j][:, k, :], wo[:, k, :], start=k == 0, stop=k == KD - 1)
                    ins.then_inc(o_psum.sem, 1)

                queries_and_keys(0, 0, 0)
                batches(pe, run)

            @block.vector
            def _(dve):
                chain = Chain(dve, own)
                dve.wait_ge(loaded.sem, 32 if soft else 96)
                dve.wait_ge(zeroed.sem, heads_zeroed)
                av_events = NH if soft else 2

                def queries(b):
                    for m in range(KD):
                        dve.wait_ge(q_psum.sem, q_psum.at(2 * b + m + 1))
                        if m == 0:
                            dve.wait_ge(s_psum.sem, s_psum.at((NH if soft else 12) * b))
                        dve.scalar_tensor_tensor(Qz[:, m, :, :], pair(ps[m][:, 0:S], NHT),
                                                 1.0 / 16 if soft else bq[:, m:m + 1], wide(core.head_mask[:, :], S),
                                                 ALU.mult if soft else ALU.add, ALU.mult).then_inc(q_ready.sem, 1)

                def run(b, j, i, more):
                    for c, tiles in enumerate(V_USES):
                        dve.wait_ge(v_psum.sem, v_psum.at(4 * b + c + 1))
                        if c == 0:
                            dve.wait_ge(av_psum.sem, av_psum.at(av_events * b))
                        for n, (m, t) in enumerate(tiles):
                            src = ps[c][0:KT, n * P:(n + 1) * P].rearrange("p (h e) -> p h e", e=16)
                            if soft:
                                ins = dve.tensor_copy(v_blocks(t, m), src)
                            else:
                                ins = dve.tensor_tensor(v_blocks(t, m), src, core.rows[
                                    0:KT, L3_BV, m * P:(m + 1) * P].rearrange("p (h e) -> p h e", e=16), ALU.add)
                        ins.then_inc(v_ready.sem, 1)
                    if soft:
                        dve.wait_ge(mask_loaded[j].sem, 16 * (i + 1))
                        dve.tensor_scalar(mask[j][:, :], mask_i[j][:, :], 0.0, None,
                                          ALU.not_equal).then_inc(mask_ready.sem, 1)
                        dve.wait_ge(mask_ready.sem, mask_ready.at(b + 1))
                        for h in range(NH + LAG_V + 2):
                            if h < NH:
                                bank = ps[(8 + h) % 4][0:S, 0:KV]
                                dve.wait_ge(s_psum.sem, s_psum.at(NH * b + h + 1))
                                dve.scalar_tensor_tensor(bank, bank, 1e-20 / 16, mask[j][:, :], ALU.add,
                                                         ALU.mult).then_inc(masked.sem, 1)
                                dve.wait_ge(masked.sem, masked.at(NH * b + h + 1))
                                dve.tensor_reduce(neg_max[:, h % 4:h % 4 + 1], bank, AX.X, ALU.max,
                                                  negate=True).then_inc(max_ready.sem, 1)
                            g = h - 1
                            if 0 <= g < NH:
                                dve.wait_ge(exp_ready.sem, exp_ready.at(NH * b + g + 1))
                                chain.step(dve.reciprocal(inv[:, g % 4:g % 4 + 1], total[:, g % 4:g % 4 + 1]))
                                dve.tensor_scalar(A[g % 4][:, 0:KV], A[g % 4][:, 0:KV], inv[:, g % 4:g % 4 + 1], None,
                                                  ALU.mult).then_inc(norm_ready.sem, 1)
                            if more and h == NH + 1:
                                queries(b + 1)
                            g = h - LAG_V - 1
                            if 0 <= g < NH and g % 8 == 7:
                                if g == 7:
                                    dve.wait_ge(o_psum.sem, o_psum.at(b - 1))
                                dve.wait_ge(av_psum.sem, av_psum.at(NH * b + g + 1))
                                dve.tensor_copy(OT[j][:, g // 8, :], ps[6 + g // 8][:, 0:S]).then_inc(ot_ready.sem, 1)
                    else:
                        if more:
                            queries(b + 1)
                        for m in range(KD):
                            if m == 0:
                                dve.wait_ge(o_psum.sem, o_psum.at(b - 1))
                            dve.wait_ge(av_psum.sem, av_psum.at(2 * b + m + 1))
                            dve.tensor_copy(OT[j][:, m, :], ps[6 + m][:, 0:S]).then_inc(ot_ready.sem, 1)
                    dve.wait_ge(o_psum.sem, o_psum.at(b + 1))
                    xb = X[:, bass.ds(b, 1), :]
                    dve.tensor_tensor(xb, xb, ps[6][0:S, 0:D].unsqueeze(1), ALU.add).then_inc(x_ready.sem, 1)

                queries(0)
                batches(dve, run, chain, NH if soft else 0)

            @block.scalar
            def _(act):
                act.wait_ge(loaded.sem, 32 if soft else 96)
                act.wait_ge(zeroed.sem, heads_zeroed)

                def keys(b):
                    for m in range(KD):
                        act.wait_ge(k_psum.sem, k_psum.at(2 * b + m + 1))
                        if m == 0:
                            act.wait_ge(s_psum.sem, s_psum.at((NH if soft else 12) * b))
                        if soft:
                            ins = act.activation(Kt[:, m, :], ps[2 + m][:, 0:KVP], ACT.Copy)
                        else:
                            ins = act.activation(Kt[:, m, :], ps[2 + m][:, 0:KVP], ACT.Identity, bias=bk[:, m:m + 1])
                        ins.then_inc(k_ready.sem, 1)

                def run(b, j, i, more):
                    if soft:
                        for h in range(NH + LAG_T):
                            if h < NH:
                                act.wait_ge(max_ready.sem, max_ready.at(NH * b + h + 1))
                                act.wait_ge(at_psum.sem, at_psum.at(NH * b + h - 3))
                                act.activation(A[h % 4][:, 0:KV], ps[(8 + h) % 4][0:S, 0:KV], ACT.Exp,
                                               bias=neg_max[:, h % 4:h % 4 + 1],
                                               accum_out=total[:, h % 4:h % 4 + 1]).then_inc(exp_ready.sem, 1)
                            g = h - LAG_T
                            if 0 <= g < NH:
                                act.wait_ge(at_psum.sem, at_psum.at(NH * b + g + 1))
                                act.wait_ge(av_psum.sem, av_psum.at(NH * b + 2 * (g // 2) - 2))
                                act.activation(AT[g // 2 % 2][:, :, g % 2, :],
                                               ps[4 + g % 2][0:KT, 0:NKT * S].rearrange("p (t s) -> p t s", t=NKT),
                                               ACT.Copy).then_inc(at_ready.sem, 1)
                            if more and h == NH + 1:
                                keys(b + 1)
                    else:
                        act.wait_ge(av_psum.sem, av_psum.at(2 * b))
                        for u in range(12):
                            m, t, half = u // 6, u // 2 % 3, u % 2
                            rows = KT if t < NKT - 1 else KV - (NKT - 1) * KT
                            act.wait_ge(s_psum.sem, s_psum.at(12 * b + u + 1))
                            h0 = NHT * m + 4 * half
                            act.activation(AS[0:rows, t, h0:h0 + 4, :],
                                           ps[u % 4][0:rows, 0:4 * S].rearrange("p (h s) -> p h s", h=4), ACT.Sigmoid,
                                           scale=0.25).then_inc(exp_ready.sem, 1)
                        if more:
                            keys(b + 1)

                keys(0)
                batches(act, run)


def head16_softmax(core, io):
    heads16(core, io, 2)


def head16_sigmoid(core, io):
    heads16(core, io, 3)


def tiles(eng, n, body):
    peeled = 2 - n % 2
    with eng.Fori(0, (n - peeled) // 2) as i:
        for j in range(2):
            body(2 * i + j, j, i, True)
    for t in range(n - peeled, n):
        body(t, t % 2, t // 2, t < n - 1)


def tile_count(E, top):
    return (top * T + E * (TS - 1)) // TS


def tile_of(slots, t):
    return slots.rearrange("(t c s) d -> t s c d", c=TS // S, s=S)[bass.ds(t, 1)]


def routed_ffn(core, io, E, top, router, gu_name, down_name, slots_in, slots_out, soft):
    X, N, NT, ps = core.X, core.N, core.NT, core.ps
    TN = tile_count(E, top)
    PER = T // TS
    LAG = 2
    CH = TS // S
    with Stage(core) as st:
        Wr = st.sb("Wr", [P, KD, E])
        L, CW, masked = st.sb("L", [S, NB, E]), st.sb("CW", [S, NB, E]), st.sb("masked", [S, NB, E])
        small = st.sb("small", [S, 3, NB])
        above, same = st.sb("above", [S, NB, E, E]), st.sb("same", [S, NB, E, E])
        rank = st.sb("rank", [S, NB, E])
        upto = [st.sb(f"upto{k}", [S, NB, E], BF16) for k in range(top)]
        batch_picks = st.sb("batch_picks", [S, E])
        per_expert, first = st.sb("per_expert", [S, E]), st.sb("first", [S, E])
        full, more_than = st.sb("full", [S, PER]), st.sb("more_than", [S, E, PER])
        earlier, later = st.sb("earlier", [S, E, E]), st.sb("later", [S, MAX_TILES, E])
        slot_f = st.sb("slot_f", [S, top, NB])
        slot = st.sb("slot", [S, top, NB], I32)
        weight = st.sb("weight", [S, top, NB])
        expert_f, expert = st.sb("expert_f", [S, MAX_TILES]), st.sb("expert", [S, MAX_TILES], I32)
        gu = [st.sb(f"gu{j}", [P, 2, KD, IP]) for j in range(2)]
        wd = [st.sb(f"wd{j}", [HU, NI, D]) for j in range(2)]
        rows_in = [st.sb(f"rows_in{j}", [S, CH, D]) for j in range(2)]
        XT = [st.sb(f"XT{j}", [P, KD, TS]) for j in range(2)]
        G = [st.sb(f"G{j}", [HU, TS]) for j in range(2)]
        Hh = [st.sb(f"Hh{j}", [HU, TS]) for j in range(4)]
        Y = [st.sb(f"Y{j}", [S, CH, D]) for j in range(2)]
        picked = st.sb("picked", [S, top * NB, D])
        loaded, own = st.event(), st.event()
        gu_loaded, wd_loaded, rows_loaded = ([st.event(), st.event()] for _ in range(3))
        l_psum, e_in, e_ready, picks_ready, place_psum, slot_ready, expert_ready = (st.event() for _ in range(7))
        y_free = st.event(2)
        scattered, stored, gathered = soft[0], soft[1], soft[2:]
        xt_psum, xt_ready, gate_psum, up_psum, g_ready, h_ready, down_done = \
            st.event(2), st.event(1), st.event(4 * NI), st.event(4 * NI), st.event(2), st.event(2), st.event(4 * NI)
        y_ready, x_ready = st.event(1), st.event()
        with st.block() as block:
            @block.sync
            def _(sp):
                st.heads(sp)
                sp.dma_start(Wr[:, :, :], io[router]).then_inc(loaded.sem, 16)
                sp.wait_ge(expert_ready.sem, 1)

                def load(t, j, i, more):
                    e = sp.value_load(expert[0:1, bass.ds(t, 1)], min_val=0, max_val=E - 1)
                    sp.wait_ge(up_psum.sem, up_psum.at(NI * (t - 1)))
                    sp.dma_start(gu[j][:, :, :, :], io[gu_name][bass.ds(e, 1)]).then_inc(gu_loaded[j].sem, 16)
                    sp.wait_ge(scattered.sem, 16 * NB * top)
                    sp.wait_ge(xt_psum.sem, xt_psum.at(t - 1))
                    sp.dma_start(rows_in[j][:, :, :], tile_of(slots_in, t)).then_inc(rows_loaded[j].sem, 16)
                    sp.wait_ge(down_done.sem, down_done.at(NI * (t - 1)))
                    sp.dma_start(wd[j][:, :, :], io[down_name][bass.ds(e, 1)]).then_inc(wd_loaded[j].sem, 16)
                tiles(sp, TN, load)

            @block.gpsimd
            def _(pool):
                pool.wait_ge(slot_ready.sem, 1)
                for k in range(top):
                    for b in range(NB):
                        pool.indirect_dma_start(slots_in[:, :], bass.IndirectOffsetOnAxis(ap=slot[:, k, b:b + 1], axis=0),
                                                N[:, b, :], None).then_inc(scattered.sem, 16)

                def store(t, j, i, more):
                    pool.wait_ge(y_ready.sem, y_ready.at(CH * (t + 1)))
                    pool.dma_start(tile_of(slots_out, t), Y[j][:, :, :]).then_inc(stored.sem, 16)
                    pool.wait_ge(stored.sem, 16 * (t + 1))
                    pool.sem_inc(y_free.sem, 1)
                tiles(pool, TN, store)
                for b in range(NB):
                    for k in range(top):
                        pool.indirect_dma_start(picked[:, k * NB + b, :], None, slots_out[:, :],
                                                bass.IndirectOffsetOnAxis(ap=slot[:, k, b:b + 1], axis=0)
                                                ).then_inc(gathered[b // 2].sem, 16)

            @block.tensor
            def _(pe):
                pe.wait_ge(loaded.sem, 16)
                for b in range(NB):
                    for k in range(KD):
                        ins = pe.matmul(ps[0][0:S, 16 * b:16 * b + E], NT[:, k, b * S:(b + 1) * S], Wr[:, k, :],
                                        start=k == 0, stop=k == KD - 1)
                ins.then_inc(l_psum.sem, 1)
                pe.wait_ge(picks_ready.sem, 1)
                picks = upto[top - 1]
                pe.matmul(ps[1][0:S, 0:NB * E], core.before[:, :], picks[:, :, :], start=True, stop=False,
                          skip_group_check=True)
                for b in range(NB - 1):
                    left = NB - 1 - b
                    ins = pe.matmul(ps[1][0:S, (b + 1) * E:NB * E], core.ones_b[:, :],
                                    picks[:, b:b + 1, :].broadcast_to([S, left, E]), start=False, stop=b == NB - 2,
                                    skip_group_check=True)
                pe.wait_ge(picks_ready.sem, 2)
                pe.matmul(ps[2][0:S, 0:E], core.ones[0:S, 0:S], batch_picks[:, :], start=True,
                          stop=True).then_inc(place_psum.sem, 1)

                def turn(t, j, i):
                    pe.wait_ge(rows_loaded[j].sem, 16 * (i + 1))
                    pe.wait_ge(xt_ready.sem, xt_ready.at(t))
                    for c in range(CH):
                        for k in range(KD):
                            ins = pe.transpose(ps[6][:, k * TS + c * S:k * TS + (c + 1) * S],
                                               rows_in[j][:, c, k * P:(k + 1) * P], core.ident[0:S, 0:S])
                    ins.then_inc(xt_psum.sem, 1)
                turn(0, 0, 0)

                def run(t, j, i, more):
                    pe.wait_ge(xt_ready.sem, xt_ready.at(t + 1))
                    pe.wait_ge(gu_loaded[j].sem, 16 * (i + 1))
                    for u in range(NI + LAG):
                        n = NI * t + u
                        if u < NI:
                            units = slice(u * HU, (u + 1) * HU)
                            pe.wait_ge(g_ready.sem, g_ready.at(n - 1))
                            for k in range(KD):
                                ins = pe.matmul(ps[2 * (u % 2)][0:HU, 0:TS], gu[j][:, 0, k, units], XT[j][:, k, :],
                                                start=k == 0, stop=k == KD - 1)
                            ins.then_inc(gate_psum.sem, 1)
                            pe.wait_ge(h_ready.sem, h_ready.at(n - 1))
                            for k in range(KD):
                                ins = pe.matmul(ps[2 * (u % 2) + 1][0:HU, 0:TS], gu[j][:, 1, k, units], XT[j][:, k, :],
                                                start=k == 0, stop=k == KD - 1)
                            ins.then_inc(up_psum.sem, 1)
                        if u == NI and more:
                            turn(t + 1, 1 - j, i + j)
                        g = u - LAG
                        if g >= 0:
                            pe.wait_ge(h_ready.sem, h_ready.at(NI * t + g + 1))
                            if g == 0:
                                pe.wait_ge(wd_loaded[j].sem, 16 * (i + 1))
                                pe.wait_ge(y_ready.sem, y_ready.at(CH * t))
                            for c in range(CH):
                                ins = pe.matmul(ps[4 + c][0:S, 0:D], Hh[g % 4][:, c * S:(c + 1) * S], wd[j][:, g, :],
                                                start=g == 0, stop=g == NI - 1)
                            ins.then_inc(down_done.sem, 1)
                tiles(pe, TN, run)

            @block.vector
            def _(dve):
                chain = Chain(dve, own)
                dve.wait_ge(l_psum.sem, 1)
                logits = ps[0][0:S, 0:16 * NB].rearrange("s (b e) -> s b e", e=16)[:, :, 0:E]
                chain.step(dve.tensor_copy(L[:, :, :], logits))
                if top == 2:
                    chain.step(dve.tensor_reduce(small[:, 0, :], L[:, :, :], AX.X, ALU.max))
                    dve.tensor_tensor(L[:, :, :], L[:, :, :], wide(small[:, 0, :], E), ALU.subtract).then_inc(e_in.sem, 1)
                    dve.wait_ge(e_ready.sem, 1)
                    chain.step(dve.tensor_reduce(small[:, 1, :], CW[:, :, :], AX.X, ALU.add))
                    chain.step(dve.reciprocal(small[:, 2, :], small[:, 1, :]))
                    chain.step(dve.tensor_tensor(L[:, :, :], CW[:, :, :], wide(small[:, 2, :], E), ALU.mult))
                top_mask(dve, chain, L[:, :, :], NB, E, range(1, top + 1), above[:, :, :, :], same[:, :, :, :],
                         rank[:, :, :], [m[:, :, :] for m in upto], core.below[:, 0:E, 0:E])
                picks = upto[top - 1]
                dve.tensor_scalar(full[:, :], core.counts[:, 0:PER], float(TS), None, ALU.mult).then_inc(picks_ready.sem, 1)
                dve.tensor_reduce(batch_picks[:, :], picks[:, :, :].rearrange("s b e -> s e b"), AX.X,
                                  ALU.add).then_inc(picks_ready.sem, 1)
                if top == 2:
                    chain.step(dve.tensor_tensor(CW[:, :, :], L[:, :, :], picks[:, :, :], ALU.mult))
                    chain.step(dve.tensor_reduce(small[:, 1, :], CW[:, :, :], AX.X, ALU.add))
                    chain.step(dve.reciprocal(small[:, 2, :], small[:, 1, :]))
                    chain.step(dve.tensor_tensor(CW[:, :, :], CW[:, :, :], wide(small[:, 2, :], E), ALU.mult))
                dve.wait_ge(place_psum.sem, 1)
                dve.wait_ge(picks_ready.sem, 1)
                chain.step(dve.tensor_tensor(more_than[:, :, :], wide(ps[2][0:S, 0:E], PER), pair(full[:, :], E), ALU.is_gt))
                chain.step(dve.tensor_reduce(per_expert[:, :], more_than[:, :, :], AX.X, ALU.add))
                chain.step(dve.tensor_tensor(earlier[:, :, :], pair(per_expert[:, :], E), core.below[:, 0:E, 0:E], ALU.mult))
                chain.step(dve.tensor_reduce(first[:, :], earlier[:, :, :], AX.X, ALU.add))
                chain.step(dve.tensor_tensor(later[:, 0:TN, 0:E - 1], wide(core.counts[:, 0:TN], E - 1),
                                             pair(first[:, 1:E], TN), ALU.is_ge))
                chain.step(dve.tensor_reduce(expert_f[:, 0:TN], later[:, 0:TN, 0:E - 1], AX.X, ALU.add))
                dve.tensor_copy(expert[:, 0:TN], expert_f[:, 0:TN]).then_inc(expert_ready.sem, 1)
                chain.step(dve.scalar_tensor_tensor(L[:, :, :], pair(first[:, :], NB), float(TS),
                                                    ps[1][0:S, 0:NB * E].rearrange("s (b e) -> s b e", e=E), ALU.mult,
                                                    ALU.add))
                if top == 2:
                    chain.step(dve.tensor_tensor(upto[1][:, :, :], upto[1][:, :, :], upto[0][:, :, :], ALU.subtract))
                for k in range(top):
                    chain.step(dve.tensor_tensor(masked[:, :, :], L[:, :, :], upto[k][:, :, :], ALU.mult))
                    chain.step(dve.tensor_reduce(slot_f[:, k, :], masked[:, :, :], AX.X, ALU.add))
                dve.tensor_copy(slot[:, :, :], slot_f[:, :, :]).then_inc(slot_ready.sem, 1)
                if top == 2:
                    for k in range(top):
                        chain.step(dve.tensor_tensor(masked[:, :, :], CW[:, :, :], upto[k][:, :, :], ALU.mult))
                        chain.step(dve.tensor_reduce(weight[:, k, :], masked[:, :, :], AX.X, ALU.add))

                def run(t, j, i, more):
                    for u in range(NI):
                        n = NI * t + u
                        dve.wait_ge(g_ready.sem, g_ready.at(n + 1))
                        dve.wait_ge(up_psum.sem, up_psum.at(n + 1))
                        dve.wait_ge(down_done.sem, down_done.at(n - 3))
                        dve.tensor_tensor(Hh[u % 4][:, :], G[u % 2][:, :], ps[2 * (u % 2) + 1][0:HU, 0:TS],
                                          ALU.mult).then_inc(h_ready.sem, 1)
                    dve.wait_ge(down_done.sem, down_done.at(NI * (t + 1)))
                    dve.wait_ge(y_free.sem, y_free.at(t - 1))
                    for c in range(CH):
                        dve.tensor_copy(Y[j][:, c, :], ps[4 + c][0:S, 0:D]).then_inc(y_ready.sem, 1)
                tiles(dve, TN, run)
                for b in range(NB):
                    dve.wait_ge(gathered[b // 2].sem, 16 * 2 * top)
                    for k in range(top):
                        if top == 2:
                            ins = dve.scalar_tensor_tensor(X[:, b, :], picked[:, k * NB + b, :], weight[:, k, b:b + 1],
                                                           X[:, b, :], ALU.mult, ALU.add)
                        else:
                            ins = dve.tensor_tensor(X[:, b, :], X[:, b, :], picked[:, b, :], ALU.add)
                        ins.then_inc(x_ready.sem, 1)
                        if k < top - 1:
                            dve.wait_ge(x_ready.sem, top * b + k + 1)

            @block.scalar
            def _(act):
                if top == 2:
                    act.wait_ge(e_in.sem, 1)
                    act.activation(CW[:, :, :], L[:, :, :], ACT.Exp).then_inc(e_ready.sem, 1)
                act.wait_ge(xt_psum.sem, xt_psum.at(1))
                act.activation(XT[0][:, :, :], ps[6][:, 0:KD * TS].rearrange("p (k s) -> p k s", k=KD),
                               ACT.Copy).then_inc(xt_ready.sem, 1)

                def run(t, j, i, more):
                    for u in range(NI):
                        n = NI * t + u
                        act.wait_ge(gate_psum.sem, gate_psum.at(n + 1))
                        act.wait_ge(h_ready.sem, h_ready.at(n - 1))
                        act.activation(G[u % 2][:, :], ps[2 * (u % 2)][0:HU, 0:TS], ACT.Silu).then_inc(g_ready.sem, 1)
                    if more:
                        act.wait_ge(xt_psum.sem, xt_psum.at(t + 2))
                        act.wait_ge(up_psum.sem, up_psum.at(NI * t))
                        act.activation(XT[1 - j][:, :, :], ps[6][:, 0:KD * TS].rearrange("p (k s) -> p k s", k=KD),
                                       ACT.Copy).then_inc(xt_ready.sem, 1)
                tiles(act, TN, run)


def routed_ffn_2(core, io):
    routed_ffn(core, io, 9, 2, "Wr2", "gu2", "down2", core.slots_in[0], core.slots_out[0],
               core.soft_events[0])


def routed_ffn_3(core, io):
    routed_ffn(core, io, 8, 1, "Wr3", "gu3", "down3", core.slots_in[1], core.slots_out[1],
               core.soft_events[1])


ROWS = ["w1_sim", "b_qv", "bp", "L1_bo", "gamma", "beta", "L3_bv", "L3_bo", "zero"]
W1_SIM, B_QV, B_P, L1_BO, GAMMA, BETA, L3_BV, L3_BO = range(8)

WEIGHTS = {
    "sim": {"w_sim": [P, 2 * KD], "b_sim": [P, 1], "W_qv": [P, 8, D]},
    "gated": {"Vg": [P, KD, 512], "VgT": [P, 4, 512], "We": [P, KD, 8 * D], "Wp": [P, KD, D], "be": [8, D]},
    "head64": {"Wq": [P, KD, 1024], "Wk": [P, KD, 1024], "Wv": [P, KD, 1024], "Wo": [P, 8, D], "bq": [P, 8],
               "bk": [P, 8], "bv": [P, 8]},
}


def program(nc, io, out):
    with ExitStack() as ctx:
        core = Core(nc, ctx)
        core.weights, core.loaded, core.loads = {}, {}, {}
        for stage, tensors in WEIGHTS.items():
            core.loaded[stage] = core.sem(f"loaded_{stage}")
            core.loads[stage] = 16 * len(tensors)
            for name, shape in tensors.items():
                core.weights[name] = ctx.enter_context(nc.sbuf_tensor(name, shape, F32))

        def load(eng, stage, io):
            for name, shape in WEIGHTS[stage].items():
                eng.dma_start(core.weights[name][:], io[name]).then_inc(core.loaded[stage], 16)
        core.load = load
        core.slots_in, core.slots_out = ([nc.dram_tensor(f"slots_{way}{n}", (tile_count(*picks) * TS, D), F32,
                                                         kind="Internal").ap()
                                          for n, picks in enumerate(((9, 2), (8, 1)))] for way in ("in", "out"))
        stages = [sim_attention, gated_experts, head64_attention, ternary_ffn, head16_softmax, routed_ffn_2, head16_sigmoid, routed_ffn_3]
        setup(core, io)
        for stage in stages:
            layer_norm(core)
            stage(core, io)
        with Stage(core) as st:
            stored = st.event()
            with st.block() as block:
                @block.sync
                def _(sp):
                    sp.dma_start(out, core.X[:, :, :]).then_inc(stored.sem, 16)
                    for name, sem in core.loaded.items():
                        sp.wait_ge(sem, core.loads[name])
                    sp.wait_ge(stored.sem, 16)


def arrays_of(v, np):
    f = {k: np.asarray(a) for k, a in v.items()}
    a = {}

    def tiles(w):
        return w.reshape(-1, P, w.shape[1]).transpose(1, 0, 2)

    def cols(w):
        return w.reshape(-1, P).T

    a["x"] = f["x"].transpose(1, 0, 2)
    ctx = np.zeros((NB, KVP, D), np.float32)
    ctx[:, :KV] = f["ctx_1024"]
    a["ctT"] = ctx.transpose(0, 2, 1).reshape(NB, KD, P, KVP).transpose(0, 2, 1, 3)
    a["ctk"] = ctx.reshape(NB, NKT, KT, D).transpose(0, 2, 1, 3)
    a["mask"] = f["mask_Bx1xSxS2_ik1"][:, 0]
    a["head_mask"] = (np.arange(P)[:, None] // 16 == np.arange(8)[None, :]).astype(np.float32)
    a["below"] = (np.arange(9)[None, :] < np.arange(9)[:, None]).astype(np.float32)
    a["counts"] = np.arange(MAX_TILES, dtype=np.float32)
    w = f["L0_xattn_w_sim"]
    rows = np.zeros((len(ROWS), D), np.float32)
    for n, r in enumerate([w[:D], f["L0_xattn_b_qv"], f["L0_ffn_bp"], f["L1_xattn_bo"], f["L1_xattn_ln_gamma"],
                           f["L1_xattn_ln_beta"], f["L3_xattn_bv"], f["L3_xattn_bo"]]):
        rows[n] = r
    a["rows"] = rows
    a["w_sim"] = cols(w[D:])
    a["b_sim"] = np.broadcast_to(f["L0_xattn_b_sim"][None, :], (P, 1))
    a["W_qv"] = tiles(f["L0_xattn_W_qv"])
    vg = f["L0_ffn_Vg"]
    a["Vg"] = tiles(vg.transpose(1, 0, 2).reshape(D, 512))
    vgt = np.zeros((P, 4, 2, D), np.float32)
    for e in range(8):
        vgt[64 * (e % 2):64 * (e % 2) + 64, e // 2, e % 2] = vg[e].T
    a["VgT"] = vgt.reshape(P, 4, 512)
    a["We"] = tiles(f["L0_ffn_We"].transpose(2, 0, 1).reshape(D, 8 * D))
    a["Wp"] = tiles(f["L0_ffn_Wp"].T)
    a["be"] = f["L0_ffn_be"]
    for n in ("Wq", "Wk", "Wv", "Wo"):
        a[n] = tiles(f["L1_xattn_" + n])
    for n in ("bq", "bk", "bv"):
        a[n] = cols(f["L1_xattn_" + n])
    a["w1"] = tiles(f["L1_ffn_w1"].T)
    a["w2"] = tiles(f["L1_ffn_w2"].T)
    a["conv_w"] = f["L1_ffn_conv_w"][:, 0].reshape(8, P, 3).transpose(1, 0, 2)
    a["conv_b"] = cols(f["L1_ffn_conv_b"])
    blocks = np.zeros((P, P), np.float32)
    for n in range(8):
        blocks[16 * n:16 * n + 16, 16 * n:16 * n + 16] = f["L2_xattn_W_v"].T
    a["W_heads"] = blocks
    a["W_o"] = tiles(f["L2_xattn_W_o"].T)
    for n in ("Wq", "Wk", "Wv", "Wo"):
        a["L3_" + n] = tiles(f["L3_xattn_" + n])
    for n in ("bq", "bk"):
        a["L3_" + n] = cols(f["L3_xattn_" + n])
    a["Wr2"] = tiles(f["L2_ffn_Wr"])
    a["Wr3"] = tiles(f["L3_ffn_router_w"].T)

    def experts(gate, up, down):
        E, _, I = gate.shape
        gu = np.zeros((E, 2, D, IP), np.float32)
        gu[:, 0, :, :I], gu[:, 1, :, :I] = gate, up
        wd = np.zeros((E, IP, D), np.float32)
        wd[:, :I] = down
        return (gu.reshape(E, 2, KD, P, IP).transpose(0, 3, 1, 2, 4),
                wd.reshape(E, NI, HU, D).transpose(0, 2, 1, 3))

    a["gu2"], a["down2"] = experts(f["L2_ffn_Wg"], f["L2_ffn_Wu"], f["L2_ffn_Wd"])
    a["gu3"], a["down3"] = experts(f["L3_ffn_gate_w"].transpose(0, 2, 1), f["L3_ffn_up_w"].transpose(0, 2, 1),
                                   f["L3_ffn_down_w"].transpose(0, 2, 1))
    return {k: np.ascontiguousarray(x) for k, x in a.items()}


def kernel(**inputs):
    import numpy as np
    import concourse.bacc as bacc
    from concourse.bass_utils import run_bass_kernel_spmd

    nc = bacc.Bacc("TRN2", target_bir_lowering=False, num_devices=1)
    arrays = arrays_of(inputs, np)
    io = {k: nc.dram_tensor(f"in_{k}", a.shape, mybir.dt.from_np(a.dtype), kind="ExternalInput").ap()
          for k, a in arrays.items()}
    out = nc.dram_tensor("out_x", (S, NB, D), F32, kind="ExternalOutput").ap()
    program(nc, io, out)
    got = run_bass_kernel_spmd(nc, [{f"in_{k}": a for k, a in arrays.items()}], core_ids=[0])
    return np.ascontiguousarray(got.results[0]["out_x"].transpose(1, 0, 2))
```

```python
from contextlib import ExitStack

import concourse.bass as bass
from concourse import mybir

F32 = mybir.dt.float32
BF16 = mybir.dt.bfloat16
I32 = mybir.dt.int32
ACT = mybir.ActivationFunctionType
ALU = mybir.AluOpType
AX = mybir.AxisListType

NB, S, D = 8, 100, 256
T = NB * S
P = 128
KD = D // P
KV = 361
KT = 121
NKT = 3
KVP = KT * NKT
NH = 16
IT = 704
NI = 6
HU = -(-IT // NI)
IP = NI * HU
TS = 2 * S
MAX_TILES = 16
EPS = 1e-5
MAGIC = 1.5 * 2.0 ** 23


class Event:
    def __init__(self, handle, head):
        self.sem, self.head = handle, head

    def at(self, count, step=1):
        return count * step + self.head


class Chain:

    def __init__(self, eng, event):
        self.eng, self.sem, self.base, self.k, self.turn, self.per = eng, event.sem, 0, 0, 0, 0

    def loop(self, turn, per):
        self.base, self.turn, self.per, self.k = self.base + self.k, turn, per, 0

    def end(self, turns):
        assert self.k == self.per, (self.k, self.per)
        self.base, self.turn, self.per, self.k = self.base + turns * self.per, 0, 0, 0

    def step(self, ins):
        ins.then_inc(self.sem, 1)
        self.k += 1
        self.eng.wait_ge(self.sem, self.base + self.turn * self.per + self.k)


class Stage:

    def __init__(self, core):
        self.core, self.nc, self.ctx, self.used = core, core.nc, ExitStack(), []

    def __enter__(self):
        return self

    def sb(self, name, shape, dt=F32):
        return self.ctx.enter_context(self.nc.sbuf_tensor(f"{name}_{self.core.stage}", shape, dt))

    def event(self, head=0):
        e = Event(self.core.pool[len(self.used)], head)
        self.used.append(e)
        return e

    def block(self):
        return self.nc.Block()

    def __exit__(self, *a):
        self.ctx.close()
        self.core.stage += 1
        if a[0] is not None:
            return
        with self.nc.Block() as block:
            @block.gpsimd
            def _(pool):
                for e in self.used:
                    pool.sem_clear(e.sem)

    def heads(self, eng):
        for e in self.used:
            if e.head:
                eng.sem_inc(e.sem, e.head)


class Core:

    def __init__(self, nc, ctx):
        self.nc, self.stage = nc, 0
        sb = lambda name, shape, dt=F32: ctx.enter_context(nc.sbuf_tensor(name, shape, dt))
        self.X = sb("X", [S, NB, D])
        self.N = sb("N", [S, NB, D])
        self.NT = sb("NT", [P, KD, T])
        self.ident = sb("ident", [P, P])
        self.identb = sb("identb", [P, P], BF16)
        self.ones = sb("ones", [P, P])
        self.below = sb("below", [S, 9, 9])
        self.before = sb("before", [S, S], BF16)
        self.ones_b = sb("ones_b", [S, S], BF16)
        self.counts = sb("counts", [S, MAX_TILES])
        self.head_mask = sb("head_mask", [P, 8])
        self.minus_half = sb("minus_half", [S, NB])
        self.half = sb("half", [S, 64])
        self.rows = sb("rows", [P, 8, D])
        self.ps = [ctx.enter_context(nc.psum_tensor(f"bank{i}", [P, 512], F32)) for i in range(8)]
        self.sem = lambda name: ctx.enter_context(nc.semaphore(name))
        self.soft_events = [[Event(self.sem(f"soft{n}_{m}"), 0) for m in range(2 + NB // 2)] for n in range(2)]
        self.constants_loaded = self.sem("constants_loaded")
        self.pool = [self.sem(f"event{i}") for i in range(44)]


def batches(eng, body, chain=None, steps=0):
    with eng.Fori(0, NB // 2 - 1) as i:
        if chain:
            chain.loop(i, 2 * steps)
        for j in range(2):
            body(2 * i + j, j, i, True)
    if chain:
        chain.end(NB // 2 - 1)
    body(NB - 2, 0, NB // 2 - 1, True)
    body(NB - 1, 1, NB // 2 - 1, False)


def pair(ap, n):
    return ap.unsqueeze(1).broadcast_to([ap.shape[0], n, ap.shape[1]])


def wide(ap, n):
    return ap.unsqueeze(2).broadcast_to([ap.shape[0], ap.shape[1], n])


def token(b):
    return bass.ds(b * S, S)


def variance(dve, chain, stats, mean, gap, var):
    chain.step(dve.tensor_tensor(mean, stats[:, :, 1], stats[:, :, 4], ALU.add))
    chain.step(dve.tensor_tensor(gap, stats[:, :, 1], stats[:, :, 4], ALU.subtract))
    chain.step(dve.tensor_tensor(var, stats[:, :, 2], stats[:, :, 5], ALU.add))
    chain.step(dve.tensor_tensor(gap, gap, gap, ALU.mult))
    chain.step(dve.tensor_scalar(gap, gap, 0.25, EPS, ALU.mult, ALU.add))
    return dve.scalar_tensor_tensor(var, var, 1.0 / D, gap, ALU.mult, ALU.add)


def layer_norm(core):
    X, N, NT, ps = core.X, core.N, core.NT, core.ps
    with Stage(core) as st:
        stats = st.sb("stats", [S, NB, 6])
        mean = st.sb("mean", [S, NB])
        gap = st.sb("gap", [S, NB])
        var = st.sb("var", [S, NB])
        rstd = st.sb("rstd", [S, NB])
        stats_ready, var_ready, rstd_ready, n_ready, nt_psum = (st.event() for _ in range(5))
        own, nt_ready = st.event(), st.event()
        with st.block() as block:
            @block.vector
            def _(dve):
                chain = Chain(dve, own)
                for b in range(NB):
                    dve.bn_stats(stats[:, b, :], X[:, b, :]).then_inc(stats_ready.sem, 1)
                dve.wait_ge(stats_ready.sem, NB)
                variance(dve, chain, stats[:, :, :], mean[:, :], gap[:, :], var[:, :]).then_inc(var_ready.sem, 1)
                chain.step(dve.tensor_scalar(mean[:, :], mean[:, :], 0.5, None, ALU.mult))
                dve.wait_ge(rstd_ready.sem, 1)
                for b in range(NB):
                    dve.tensor_scalar(N[:, b, :], X[:, b, :], mean[:, b:b + 1], rstd[:, b:b + 1], ALU.subtract,
                                      ALU.mult).then_inc(n_ready.sem, 1)

            @block.gpsimd
            def _(pool):
                pool.wait_ge(var_ready.sem, 1)
                pool.tensor_tensor(rstd[:, :], var[:, :], core.minus_half[:, 0:NB], ALU.pow).then_inc(rstd_ready.sem, 1)

            @block.tensor
            def _(pe):
                for q in range(NB // 2):
                    pe.wait_ge(n_ready.sem, 2 * q + 2)
                    for j in range(2):
                        for k in range(KD):
                            ins = pe.transpose(ps[q][:, (2 * k + j) * S:(2 * k + j + 1) * S],
                                               N[:, 2 * q + j, k * P:(k + 1) * P], core.ident[0:S, 0:S])
                    ins.then_inc(nt_psum.sem, 1)

            @block.scalar
            def _(act):
                for q in range(NB // 2):
                    act.wait_ge(nt_psum.sem, q + 1)
                    act.activation(NT[:, :, 2 * q * S:2 * (q + 1) * S],
                                   ps[q][:, 0:4 * S].rearrange("p (k t) -> p k t", k=KD),
                                   ACT.Copy).then_inc(nt_ready.sem, 1)
                act.wait_ge(nt_ready.sem, NB // 2)


def setup(core, io):
    with Stage(core) as st:
        loaded, zeroed, made = st.event(), st.event(), st.event()
        with st.block() as block:
            @block.sync
            def _(sp):
                sp.dma_start(core.X[:, :, :], io["x"]).then_inc(loaded.sem, 16)
                sp.dma_start(core.head_mask[:, :], io["head_mask"]).then_inc(core.constants_loaded, 16)
                sp.dma_start(core.below[:, :, :], io["below"].partition_broadcast(S)).then_inc(core.constants_loaded, 16)
                sp.dma_start(core.rows[:, :, :], io["rows"].partition_broadcast(P)).then_inc(core.constants_loaded, 16)
                sp.dma_start(core.counts[:, :], io["counts"].partition_broadcast(S)).then_inc(core.constants_loaded, 16)
                core.load(sp, "sim", io)
                sp.wait_ge(loaded.sem, 16)

            @block.gpsimd
            def _(pool):
                pool.memset(core.ident[:, :], 0.0).then_inc(zeroed.sem, 1)
                pool.memset(core.ones[:, :], 1.0)
                pool.memset(core.ones_b[:, :], 1.0).then_inc(zeroed.sem, 1)
                pool.memset(core.minus_half[:, :], -0.5)
                pool.memset(core.half[:, :], 0.5)
                pool.wait_ge(zeroed.sem, 2)
                pool.affine_select(out=core.before[:, :], in_=core.ones_b[:, :], compare_op=ALU.is_gt, fill=0.0,
                                   base=0, pattern=[[1, S]], channel_multiplier=-1)
                pool.affine_select(out=core.ident[:, :], in_=core.ident[:, :], compare_op=ALU.not_equal, fill=1.0,
                                   base=0, pattern=[[-1, P]], channel_multiplier=1).then_inc(made.sem, 1)
                pool.wait_ge(made.sem, 1)
                pool.tensor_copy(core.identb[:, :], core.ident[:, :])


def sim_attention(core, io):
    X, N, NT, ps = core.X, core.N, core.NT, core.ps
    w = core.weights
    with Stage(core) as st:
        ctT = [st.sb(f"ctT{j}", [P, KD, KVP]) for j in range(2)]
        ctk = [st.sb(f"ctk{j}", [KT, NKT, D]) for j in range(2)]
        EW = [st.sb(f"EW{j}", [P, KD, S]) for j in range(2)]
        A = [st.sb(f"A{j}", [S, KVP]) for j in range(2)]
        AT = [st.sb(f"AT{j}", [KT, NKT, S]) for j in range(2)]
        F = [st.sb(f"F{j}", [P, 8, S]) for j in range(2)]
        HQ = st.sb("HQ", [P, KD, T])
        neg_max, total, inv = st.sb("neg_max", [S, NB]), st.sb("total", [S, NB]), st.sb("inv", [S, NB])
        enc_w1 = st.sb("enc_w1", [S, NB, D])
        row_max, best, per_batch = st.sb("row_max", [S, NB]), st.sb("best", [NB, 4]), st.sb("per_batch", [NB, S])
        beta = st.sb("beta", [S, NB])
        hc = st.sb("hc", [P, KD, NB])
        ctx_loaded = [st.event(), st.event()]
        ctk_loaded = [st.event(), st.event()]
        ew_ready, sim_ready, max_ready, norm_ready = st.event(), st.event(2), st.event(), st.event()
        exp_ready, at_psum, at_ready, hq_psum, hq_ready = (st.event(2) for _ in range(5))
        own, pads, w1_ready, bias_ready = (st.event() for _ in range(4))
        m_ready, mt_psum, top_ready, e_ready, share_ready, share_psum, beta_ready, hc_psum = \
            (st.event() for _ in range(8))
        f_act, f_pool, f_dve, out_psum, x_ready = st.event(), st.event(), st.event(), st.event(2), st.event(2)
        with st.block() as block:
            @block.sync
            def _(sp):
                st.heads(sp)
                with sp.Fori(0, NB // 2) as i:
                    for j in range(2):
                        b = 2 * i + j
                        sp.wait_ge(sim_ready.sem, sim_ready.at(b - 1))
                        sp.dma_start(ctT[j][:, :, :], io["ctT"][bass.ds(b, 1)]).then_inc(ctx_loaded[j].sem, 16)
                        sp.wait_ge(hq_psum.sem, hq_psum.at(b - 1))
                        sp.dma_start(ctk[j][:, :, :], io["ctk"][bass.ds(b, 1)]).then_inc(ctk_loaded[j].sem, 16)
                core.load(sp, "gated", io)

            @block.gpsimd
            def _(pool):
                pool.wait_ge(core.constants_loaded, 64)
                pool.wait_ge(core.loaded["sim"], core.loads["sim"])
                for j in range(2):
                    pool.memset(A[j][:, KV:KVP], 0.0).then_inc(pads.sem, 1)
                pool.tensor_tensor(enc_w1[:, :, :], N[:, :, :], pair(core.rows[0:S, W1_SIM, :], NB),
                                   ALU.mult).then_inc(w1_ready.sem, 1)
                pool.tensor_tensor(X[:, :, :], X[:, :, :], pair(core.rows[0:S, B_QV, :], NB),
                                   ALU.add).then_inc(bias_ready.sem, 1)
                pool.wait_ge(hq_ready.sem, hq_ready.at(NB))
                with pool.Fori(0, NB // 2) as i:
                    for j in range(2):
                        b = 2 * i + j
                        pool.wait_ge(out_psum.sem, out_psum.at(b - 1))
                        pool.tensor_tensor(F[j][:, 4:6, :], NT[:, :, token(b)], HQ[:, :, token(b)],
                                           ALU.mult).then_inc(f_pool.sem, 1)

            @block.vector
            def _(dve):
                chain = Chain(dve, own)
                dve.wait_ge(core.loaded["sim"], core.loads["sim"])

                def encoder(b, j):
                    dve.wait_ge(sim_ready.sem, sim_ready.at(b - 1))
                    for k in range(KD):
                        dve.tensor_scalar(EW[j][:, k, :], NT[:, k, token(b)], w["w_sim"][:, KD + k:KD + k + 1],
                                          w["w_sim"][:, k:k + 1], ALU.mult, ALU.add).then_inc(ew_ready.sem, 1)

                def maximum(b, j):
                    dve.wait_ge(sim_ready.sem, sim_ready.at(b + 1))
                    dve.tensor_reduce(neg_max[:, bass.ds(b, 1)], ps[j][0:S, 0:KV], AX.X, ALU.max,
                                      negate=True).then_inc(max_ready.sem, 1)

                def attend(b, j, i, more):
                    if more:
                        encoder(b + 1, 1 - j)
                    dve.wait_ge(exp_ready.sem, exp_ready.at(b + 1))
                    chain.step(dve.reciprocal(inv[:, bass.ds(b, 1)], total[:, bass.ds(b, 1)]))
                    dve.tensor_scalar(A[j][:, 0:KV], A[j][:, 0:KV], inv[:, bass.ds(b, 1)], None,
                                      ALU.mult).then_inc(norm_ready.sem, 1)
                    if more:
                        maximum(b + 1, 1 - j)

                encoder(0, 0)
                maximum(0, 0)
                batches(dve, attend, chain, 1)
                dve.wait_ge(w1_ready.sem, 1)
                chain.step(dve.tensor_reduce(row_max[:, :], enc_w1[:, :, :], AX.X, ALU.add))
                dve.wait_ge(max_ready.sem, NB)
                chain.step(dve.tensor_tensor(row_max[:, :], row_max[:, :], neg_max[:, :], ALU.subtract))
                dve.tensor_scalar(row_max[:, :], row_max[:, :], w["b_sim"][0:S, :], None, ALU.add).then_inc(m_ready.sem, 1)
                dve.wait_ge(mt_psum.sem, 1)
                dve.tensor_reduce(best[:, 0:1], ps[6][0:NB, 0:S], AX.X, ALU.max, negate=True).then_inc(top_ready.sem, 1)
                dve.wait_ge(e_ready.sem, 1)
                chain.step(dve.reciprocal(best[:, 2:3], best[:, 1:2]))
                dve.tensor_scalar(per_batch[:, :], per_batch[:, :], best[:, 2:3], None, ALU.mult).then_inc(share_ready.sem, 1)
                dve.wait_ge(share_psum.sem, 1)
                dve.tensor_copy(beta[:, :], ps[7][0:S, 0:NB]).then_inc(beta_ready.sem, 1)
                dve.wait_ge(hc_psum.sem, 1)
                chain.step(dve.tensor_copy(hc[:, :, :], ps[6][:, 0:KD * NB].rearrange("p (k b) -> p k b", k=KD)))
                dve.wait_ge(bias_ready.sem, 1)

                def times_hc(b, j):
                    dve.wait_ge(out_psum.sem, out_psum.at(b - 1))
                    for k in range(KD):
                        dve.tensor_scalar(F[j][:, 6 + k, :], NT[:, k, token(b)], hc[:, k, bass.ds(b, 1)], None,
                                          ALU.mult).then_inc(f_dve.sem, 1)

                def add(b, j, i, more):
                    if more:
                        times_hc(b + 1, 1 - j)
                    dve.wait_ge(out_psum.sem, out_psum.at(b + 1))
                    dve.tensor_tensor(X[:, bass.ds(b, 1), :], X[:, bass.ds(b, 1), :], ps[j][0:S, 0:D].unsqueeze(1),
                                      ALU.add).then_inc(x_ready.sem, 1)

                times_hc(0, 0)
                batches(dve, add)

            @block.scalar
            def _(act):
                act.wait_ge(pads.sem, 2)

                def exponentials(b, j):
                    act.wait_ge(max_ready.sem, b + 1)
                    act.wait_ge(at_psum.sem, at_psum.at(b - 1))
                    act.activation(A[j][:, 0:KV], ps[j][0:S, 0:KV], ACT.Exp, bias=neg_max[:, bass.ds(b, 1)],
                                   accum_out=total[:, bass.ds(b, 1)]).then_inc(exp_ready.sem, 1)

                def attend(b, j, i, more):
                    act.wait_ge(at_psum.sem, at_psum.at(b + 1))
                    act.wait_ge(hq_psum.sem, hq_psum.at(b - 1))
                    act.activation(AT[j][:, :, :], ps[2 + j][0:KT, 0:NKT * S].rearrange("p (t s) -> p t s", t=NKT),
                                   ACT.Copy).then_inc(at_ready.sem, 1)
                    if more:
                        exponentials(b + 1, 1 - j)
                    act.wait_ge(hq_psum.sem, hq_psum.at(b + 1))
                    act.activation(HQ[:, :, token(b)], ps[4 + j][:, 0:KD * S].rearrange("p (k s) -> p k s", k=KD),
                                   ACT.Copy).then_inc(hq_ready.sem, 1)

                exponentials(0, 0)
                batches(act, attend)
                act.wait_ge(top_ready.sem, 1)
                act.activation(per_batch[:, :], ps[6][0:NB, 0:S], ACT.Exp, bias=best[:, 0:1],
                               accum_out=best[:, 1:2]).then_inc(e_ready.sem, 1)
                act.wait_ge(hq_ready.sem, hq_ready.at(NB))
                with act.Fori(0, NB // 2) as i:
                    for j in range(2):
                        b = 2 * i + j
                        act.wait_ge(out_psum.sem, out_psum.at(b - 1))
                        act.activation(F[j][:, 0:2, :], NT[:, :, token(b)], ACT.Copy).then_inc(f_act.sem, 1)
                        act.activation(F[j][:, 2:4, :], HQ[:, :, token(b)], ACT.Copy).then_inc(f_act.sem, 1)

            @block.tensor
            def _(pe):
                pe.wait_ge(core.loaded["sim"], core.loads["sim"])

                def scores(b, j, i):
                    pe.wait_ge(ew_ready.sem, KD * (b + 1))
                    pe.wait_ge(ctx_loaded[j].sem, 16 * (i + 1))
                    pe.wait_ge(exp_ready.sem, exp_ready.at(b - 1))
                    for k in range(KD):
                        ins = pe.matmul(ps[j][0:S, 0:KV], EW[j][:, k, :], ctT[j][:, k, 0:KV], start=k == 0,
                                        stop=k == KD - 1)
                    ins.then_inc(sim_ready.sem, 1)

                def attend(b, j, i, more):
                    pe.wait_ge(norm_ready.sem, b + 1)
                    pe.wait_ge(at_ready.sem, at_ready.at(b - 1))
                    for t in range(NKT):
                        ins = pe.transpose(ps[2 + j][0:KT, t * S:(t + 1) * S], A[j][:, t * KT:(t + 1) * KT],
                                           core.ident[0:S, 0:S])
                    ins.then_inc(at_psum.sem, 1)
                    if more:
                        scores(b + 1, 1 - j, i + j)
                    pe.wait_ge(at_ready.sem, at_ready.at(b + 1))
                    pe.wait_ge(ctk_loaded[j].sem, 16 * (i + 1))
                    pe.wait_ge(hq_ready.sem, hq_ready.at(b - 1))
                    for m in range(KD):
                        for t in range(NKT):
                            ins = pe.matmul(ps[4 + j][:, m * S:(m + 1) * S], ctk[j][:, t, m * P:(m + 1) * P],
                                            AT[j][:, t, :], start=t == 0, stop=t == NKT - 1)
                    ins.then_inc(hq_psum.sem, 1)

                scores(0, 0, 0)
                batches(pe, attend)
                pe.wait_ge(m_ready.sem, 1)
                pe.transpose(ps[6][0:NB, 0:S], row_max[:, :], core.ident[0:S, 0:S]).then_inc(mt_psum.sem, 1)
                pe.wait_ge(share_ready.sem, 1)
                pe.transpose(ps[7][0:S, 0:NB], per_batch[:, :], core.ident[0:NB, 0:NB]).then_inc(share_psum.sem, 1)
                pe.wait_ge(beta_ready.sem, 1)
                for b in range(NB):
                    for k in range(KD):
                        ins = pe.matmul(ps[6][:, k * NB + b:k * NB + b + 1], N[:, b, k * P:(k + 1) * P],
                                        beta[:, b:b + 1], start=True, stop=True)
                ins.then_inc(hc_psum.sem, 1)
                with pe.Fori(0, NB // 2) as i:
                    for j in range(2):
                        b = 2 * i + j
                        pe.wait_ge(f_act.sem, 2 * (b + 1))
                        pe.wait_ge(f_pool.sem, b + 1)
                        pe.wait_ge(f_dve.sem, KD * (b + 1))
                        pe.wait_ge(x_ready.sem, x_ready.at(b - 1))
                        for k in range(8):
                            ins = pe.matmul(ps[j][0:S, 0:D], F[j][:, k, :], w["W_qv"][:, k, :], start=k == 0, stop=k == 7)
                        ins.then_inc(out_psum.sem, 1)


def top_mask(dve, chain, r, nb, ne, keep, above, same, rank, mask, below):
    full = [S, nb, ne, ne]
    other = r.unsqueeze(2).broadcast_to(full)
    this = r.unsqueeze(3).broadcast_to(full)
    chain.step(dve.tensor_tensor(above, other, this, ALU.is_gt))
    chain.step(dve.tensor_tensor(same, other, this, ALU.is_equal))
    chain.step(dve.tensor_tensor(same, same, below.unsqueeze(1).broadcast_to(full), ALU.mult))
    chain.step(dve.tensor_tensor(above, above, same, ALU.add))
    chain.step(dve.tensor_reduce(rank, above, AX.X, ALU.add))
    for n, m in zip(keep, mask):
        chain.step(dve.tensor_scalar(m, rank, float(n), None, ALU.is_lt))


def gated_experts(core, io):
    X, N, NT, ps = core.X, core.N, core.NT, core.ps
    w = core.weights
    E = 8
    with Stage(core) as st:
        xeT = [st.sb(f"xeT{j}", [P, 4, S]) for j in range(2)]
        DF = [st.sb(f"DF{j}", [S, 2, D]) for j in range(2)]
        R = st.sb("R", [S, NB, E])
        small = st.sb("small", [S, 6, NB])
        RW = st.sb("RW", [S, NB, E])
        above, same = st.sb("above", [S, NB, E, E]), st.sb("same", [S, NB, E, E])
        rank, top1, top2, over = (st.sb(n, [S, NB, E]) for n in ("rank", "top1", "top2", "over"))
        any_over, flag = st.sb("any_over", [S, 1]), st.sb("flag", [S, 1])
        NTs = [st.sb(f"NTs{j}", [P, KD, S]) for j in range(2)]
        wb = [st.sb(f"wb{j}", [S, E]) for j in range(2)]
        wT = [st.sb(f"wT{j}", [E, S]) for j in range(2)]
        xe_psum, xeT_ready, d_psum, d_ready, sq_done = st.event(), st.event(2), st.event(8), st.event(4), st.event(4)
        own, root_ready, e_in, e_ready, any_ready, flag_psum, bias_ready = (st.event() for _ in range(7))
        nts_ready, wb_ready, wt_psum, wt_ready = st.event(), st.event(), st.event(2), st.event(2)
        base_psum, ex_psum, base_used, ex_used = st.event(2), st.event(8), st.event(2), st.event(4)
        zeros = st.sb("zeros", [S, 512])
        zeros_ready, slots_zeroed = st.event(), st.event()
        with st.block() as block:
            @block.sync
            def _(sp):
                st.heads(sp)
                core.load(sp, "head64", io)
                core.load(sp, "ternary", io)
                core.load(sp, "routers", io)
                core.load(sp, "context", io)
                core.load(sp, "heads16", io)
                sp.wait_ge(zeros_ready.sem, 1)
                for slots in core.slots_in:
                    flat = slots.rearrange("(s n) d -> s (n d)", s=S).rearrange("s (m w) -> s m w", w=512)
                    sp.dma_start(flat, pair(zeros[:, :], flat.shape[1])).then_inc(slots_zeroed.sem, 16)
                sp.wait_ge(slots_zeroed.sem, 16 * len(core.slots_in))

            @block.gpsimd
            def _(pool):
                pool.memset(zeros[:, :], 0.0).then_inc(zeros_ready.sem, 1)
                pool.tensor_tensor(X[:, :, :], X[:, :, :], pair(core.rows[0:S, B_P, :], NB),
                                   ALU.add).then_inc(bias_ready.sem, 1)
                for b in range(NB):
                    pool.wait_ge(sq_done.sem, sq_done.at(E * (b + 1)))
                    pool.tensor_tensor(R[:, b, :], R[:, b, :], core.half[:, 0:E], ALU.pow).then_inc(root_ready.sem, 1)

            @block.tensor
            def _(pe):
                pe.wait_ge(core.loaded["gated"], core.loads["gated"])

                def project(b, j):
                    pe.wait_ge(xeT_ready.sem, xeT_ready.at(b - 1))
                    for q in range(4):
                        for k in range(KD):
                            ins = pe.matmul(ps[j][:, q * S:(q + 1) * S], w["Vg"][:, k, q * P:(q + 1) * P],
                                            NT[:, k, token(b)], start=k == 0, stop=k == KD - 1)
                    ins.then_inc(xe_psum.sem, 1)

                def back(b, j, i, more):
                    if more:
                        project(b + 1, 1 - j)
                    pe.wait_ge(xeT_ready.sem, xeT_ready.at(b + 1))
                    for q in range(4):
                        pe.wait_ge(d_ready.sem, d_ready.at(4 * b + q - 3))
                        pe.matmul(ps[2 + q][0:S, :], xeT[j][:, q, :], w["VgT"][:, q, :], start=True,
                                  stop=True).then_inc(d_psum.sem, 1)

                project(0, 0)
                batches(pe, back)
                pe.wait_ge(any_ready.sem, 1)
                pe.matmul(ps[6][0:S, 0:1], core.ones[0:S, 0:S], any_over[:, :], start=True,
                          stop=True).then_inc(flag_psum.sem, 1)

                def turn(b, j):
                    pe.wait_ge(wb_ready.sem, b + 1)
                    pe.wait_ge(wt_ready.sem, wt_ready.at(b - 1))
                    pe.transpose(ps[6 + j][0:E, 0:S], wb[j][:, :], core.ident[0:S, 0:S]).then_inc(wt_psum.sem, 1)

                def experts(b, j, i, more):
                    pe.wait_ge(nts_ready.sem, b + 1)
                    pe.wait_ge(wt_ready.sem, wt_ready.at(b + 1))
                    pe.wait_ge(base_used.sem, base_used.at(b - 1))
                    for k in range(KD):
                        pe.matmul(ps[j][0:S, 0:D], NTs[j][:, k, :], w["Wp"][:, k, :], start=k == 0, stop=False)
                    pe.matmul(ps[j][0:S, 0:D], wT[j][:, :], w["be"][:, :], start=False,
                              stop=True).then_inc(base_psum.sem, 1)
                    for q in range(4):
                        pe.wait_ge(ex_used.sem, ex_used.at(4 * b + q - 3))
                        for k in range(KD):
                            ins = pe.matmul(ps[2 + q][0:S, :], NTs[j][:, k, :],
                                            w["We"][:, k, q * 512:(q + 1) * 512], start=k == 0, stop=k == KD - 1)
                        ins.then_inc(ex_psum.sem, 1)
                        if more and q == 1:
                            turn(b + 1, 1 - j)

                turn(0, 0)
                batches(pe, experts)

            @block.vector
            def _(dve):
                chain = Chain(dve, own)
                with dve.Fori(0, NB // 2) as i:
                    for j in range(2):
                        b = 2 * i + j
                        for q in range(4):
                            dve.wait_ge(d_psum.sem, d_psum.at(4 * b + q + 1))
                            dve.wait_ge(sq_done.sem, sq_done.at(8 * b + 2 * q - 2))
                            dve.tensor_tensor(DF[q % 2][:, :, :], ps[2 + q][0:S, :].rearrange("s (e d) -> s e d", e=2),
                                              N[:, bass.ds(b, 1), :].broadcast_to([S, 2, D]),
                                              ALU.subtract).then_inc(d_ready.sem, 1)
                dve.wait_ge(root_ready.sem, NB)
                chain.step(dve.tensor_reduce(small[:, 0, :], R[:, :, :], AX.X, ALU.min))
                dve.tensor_tensor(R[:, :, :], wide(small[:, 0, :], E), R[:, :, :], ALU.subtract).then_inc(e_in.sem, 1)
                dve.wait_ge(e_ready.sem, 1)
                chain.step(dve.tensor_reduce(small[:, 1, :], RW[:, :, :], AX.X, ALU.add))
                chain.step(dve.reciprocal(small[:, 2, :], small[:, 1, :]))
                chain.step(dve.tensor_tensor(RW[:, :, :], RW[:, :, :], wide(small[:, 2, :], E), ALU.mult))
                top_mask(dve, chain, RW[:, :, :], NB, E, (1, 2), above[:, :, :, :], same[:, :, :, :], rank[:, :, :],
                         (top1[:, :, :], top2[:, :, :]), core.below[:, 0:E, 0:E])
                chain.step(dve.tensor_scalar(over[:, :, :], RW[:, :, :], 1.0 / E, None, ALU.is_gt))
                dve.tensor_reduce(any_over[:, :], over[:, :, :], AX.XY, ALU.max).then_inc(any_ready.sem, 1)
                dve.wait_ge(flag_psum.sem, 1)
                chain.step(dve.tensor_scalar(flag[:, :], ps[6][0:S, 0:1], 0.0, None, ALU.is_gt))
                chain.step(dve.tensor_tensor(over[:, :, :], over[:, :, :], top1[:, :, :], ALU.subtract))
                chain.step(dve.scalar_tensor_tensor(over[:, :, :], over[:, :, :], flag[:, :], top1[:, :, :], ALU.mult,
                                                    ALU.add))
                chain.step(dve.tensor_tensor(over[:, :, :], over[:, :, :], top2[:, :, :], ALU.mult))
                chain.step(dve.tensor_tensor(RW[:, :, :], RW[:, :, :], over[:, :, :], ALU.mult))
                chain.step(dve.tensor_reduce(small[:, 3, :], RW[:, :, :], AX.X, ALU.add))
                chain.step(dve.tensor_scalar(small[:, 4, :], small[:, 3, :], 0.0, None, ALU.is_equal))
                chain.step(dve.tensor_tensor(small[:, 3, :], small[:, 3, :], small[:, 4, :], ALU.add))
                chain.step(dve.reciprocal(small[:, 5, :], small[:, 3, :]))
                chain.step(dve.tensor_tensor(RW[:, :, :], RW[:, :, :], wide(small[:, 5, :], E), ALU.mult))
                dve.wait_ge(bias_ready.sem, 1)

                def weights(b, j):
                    dve.wait_ge(wt_psum.sem, wt_psum.at(b - 1))
                    dve.tensor_copy(wb[j][:, :].unsqueeze(1), RW[:, bass.ds(b, 1), :]).then_inc(wb_ready.sem, 1)

                def add(b, j, i, more):
                    xb = X[:, bass.ds(b, 1), :]
                    dve.wait_ge(base_psum.sem, base_psum.at(b + 1))
                    dve.tensor_tensor(xb, xb, ps[j][0:S, 0:D].unsqueeze(1), ALU.add).then_inc(base_used.sem, 1)
                    if more:
                        weights(b + 1, 1 - j)
                    dve.wait_ge(base_used.sem, base_used.at(b + 1))
                    dve.wait_ge(wb_ready.sem, b + 1)
                    for q in range(4):
                        dve.wait_ge(ex_psum.sem, ex_psum.at(4 * b + q + 1))
                        chain.step(dve.scalar_tensor_tensor(
                            xb, ps[2 + q][0:S, 0:D].unsqueeze(1), wb[j][:, 2 * q:2 * q + 1], xb, ALU.mult, ALU.add))
                        dve.scalar_tensor_tensor(
                            xb, ps[2 + q][0:S, D:2 * D].unsqueeze(1), wb[j][:, 2 * q + 1:2 * q + 2], xb, ALU.mult,
                            ALU.add).then_inc(ex_used.sem, 1)
                        dve.wait_ge(ex_used.sem, ex_used.at(4 * b + q + 1))

                weights(0, 0)
                batches(dve, add, chain, 4)

            @block.scalar
            def _(act):

                def projected(b, j):
                    act.wait_ge(xe_psum.sem, b + 1)
                    act.wait_ge(d_psum.sem, d_psum.at(4 * (b - 1)))
                    act.activation(xeT[j][:, :, :], ps[j][:, 0:4 * S].rearrange("p (q s) -> p q s", q=4),
                                   ACT.Copy).then_inc(xeT_ready.sem, 1)

                def lengths(b, j, i, more):
                    if more:
                        projected(b + 1, 1 - j)
                    for q in range(4):
                        act.wait_ge(d_ready.sem, d_ready.at(4 * b + q + 1))
                        for c in range(2):
                            act.activation(DF[q % 2][:, c, :], DF[q % 2][:, c, :], ACT.Square,
                                           accum_out=R[:, bass.ds(b, 1), 2 * q + c]).then_inc(sq_done.sem, 1)

                projected(0, 0)
                batches(act, lengths)
                act.wait_ge(e_in.sem, 1)
                act.activation(RW[:, :, :], R[:, :, :], ACT.Exp).then_inc(e_ready.sem, 1)
                with act.Fori(0, NB // 2) as i:
                    for j in range(2):
                        b = 2 * i + j
                        act.wait_ge(ex_psum.sem, ex_psum.at(4 * (b - 1)))
                        act.activation(NTs[j][:, :, :], NT[:, :, token(b)], ACT.Copy).then_inc(nts_ready.sem, 1)
                        act.wait_ge(wt_psum.sem, wt_psum.at(b + 1))
                        act.activation(wT[j][:, :], ps[6 + j][0:E, 0:S], ACT.Copy).then_inc(wt_ready.sem, 1)


LAG_T, LAG_V = 3, 5


def head64_attention(core, io):
    X, N, NT, ps = core.X, core.N, core.NT, core.ps
    w = core.weights
    with Stage(core) as st:
        ctT = [st.sb(f"ctT{j}", [P, KD, KVP]) for j in range(2)]
        QH = [st.sb(f"QH{c}", [P, 8, S]) for c in range(2)]
        KTr = st.sb("KTr", [P, 8, KVP])
        V = st.sb("V", [KT, NKT, 1024])
        A = [st.sb(f"A{c}", [S, KVP]) for c in range(4)]
        AT = [st.sb(f"AT{c}", [KT, NKT, 2, S]) for c in range(2)]
        OT = st.sb("OT", [P, 8, S])
        O = st.sb("O", [S, D])
        bq8 = st.sb("bq8", [P, 8])
        neg_max, total, inv = st.sb("neg_max", [S, 4]), st.sb("total", [S, 4]), st.sb("inv", [S, 4])
        stats, mv, rstd = st.sb("stats", [S, 1, 6]), st.sb("mv", [S, 3]), st.sb("rstd", [S, 1])
        ctx_loaded = [st.event(), st.event()]
        zeroed, rows_added = st.event(), st.event()
        q_psum, q_ready, k_psum, k_ready, v_psum, v_ready = (st.event(8) for _ in range(6))
        s_psum, max_ready, exp_ready, norm_ready, at_psum, at_ready = (st.event(4) for _ in range(6))
        av_psum, ot_ready, o_psum, o_used, var_ready, rstd_ready, own, x_ready = \
            st.event(2), st.event(4), st.event(1), st.event(1), st.event(), st.event(), st.event(), st.event()
        with st.block() as block:
            @block.sync
            def _(sp):
                st.heads(sp)
                with sp.Fori(0, NB // 2) as i:
                    for j in range(2):
                        b = 2 * i + j
                        sp.wait_ge(v_psum.sem, v_psum.at(6 * b - 6))
                        sp.dma_start(ctT[j][:, :, :], io["ctT"][bass.ds(b, 1)]).then_inc(ctx_loaded[j].sem, 16)

            @block.gpsimd
            def _(pool):
                pool.memset(QH[0][64:P, :, :], 0.0).then_inc(zeroed.sem, 1)
                pool.memset(QH[1][0:64, :, :], 0.0).then_inc(zeroed.sem, 1)
                pool.wait_ge(zeroed.sem, 2)
                for c in range(4):
                    pool.memset(A[c][:, KV:KVP], 0.0).then_inc(zeroed.sem, 1)
                pool.tensor_tensor(N[:, :, :], N[:, :, :], pair(core.rows[0:S, L1_BO, :], NB),
                                   ALU.add).then_inc(rows_added.sem, 1)
                pool.tensor_tensor(X[:, :, :], X[:, :, :], pair(core.rows[0:S, BETA, :], NB),
                                   ALU.add).then_inc(rows_added.sem, 1)
                with pool.Fori(0, NB) as b:
                    pool.wait_ge(var_ready.sem, b + 1)
                    pool.tensor_tensor(rstd[:, :], mv[:, 1:2], core.minus_half[:, 0:1], ALU.pow).then_inc(rstd_ready.sem, 1)

            def bank_free(eng, b, u):
                if u < 4:
                    eng.wait_ge(exp_ready.sem, exp_ready.at(NH * b + u - 3))
                elif u < 6:
                    eng.wait_ge(q_ready.sem, q_ready.at(4 * b + 2 * (u - 3)))
                elif u < 14:
                    eng.wait_ge(k_ready.sem, k_ready.at(8 * b + u - 5))
                elif u < 20:
                    eng.wait_ge(v_ready.sem, v_ready.at(6 * b + u - 13))
                else:
                    eng.wait_ge(exp_ready.sem, exp_ready.at(NH * b + u - 19))

            @block.tensor
            def _(pe):
                pe.wait_ge(core.loaded["head64"], core.loads["head64"])
                pe.wait_ge(zeroed.sem, 6)

                def query(b, u):
                    bank_free(pe, b, u)
                    for c in range(4):
                        t = 4 * u + c
                        for k in range(KD):
                            ins = pe.matmul(ps[u % 4][:, c * S:(c + 1) * S], w["Wq"][:, k, t * P:(t + 1) * P],
                                            NT[:, k, token(b)], start=k == 0, stop=k == KD - 1)
                    ins.then_inc(q_psum.sem, 1)

                def key(b, j, i, t):
                    u = 2 + t
                    if t == 0:
                        pe.wait_ge(ctx_loaded[j].sem, 16 * (i + 1))
                    bank_free(pe, b, u)
                    for k in range(KD):
                        ins = pe.matmul(ps[u % 4][:, 0:KV], w["Wk"][:, k, t * P:(t + 1) * P], ctT[j][:, k, 0:KV],
                                        start=k == 0, stop=k == KD - 1)
                    ins.then_inc(k_psum.sem, 1)

                def run(b, j, i, more):
                    for t in range(NKT):
                        for c in range(2):
                            u = 10 + 2 * t + c
                            bank_free(pe, b, u)
                            for k in range(KD):
                                ins = pe.matmul(ps[u % 4][0:KT, :], ctT[j][:, k, t * KT:(t + 1) * KT],
                                                w["Wv"][:, k, 512 * c:512 * (c + 1)], start=k == 0, stop=k == KD - 1)
                            ins.then_inc(v_psum.sem, 1)
                    for h in range(NH + LAG_V + 1):
                        if h < NH:
                            u = 16 + h
                            bank_free(pe, b, u)
                            if h == 0:
                                pe.wait_ge(q_ready.sem, q_ready.at(4 * b + 4))
                            pe.wait_ge(k_ready.sem, k_ready.at(8 * b + h // 2 + 1))
                            pe.matmul(ps[u % 4][0:S, 0:KV], QH[h % 2][:, h // 2, :], KTr[:, h // 2, 0:KV],
                                      start=True, stop=True).then_inc(s_psum.sem, 1)
                        g = h - LAG_T
                        if 0 <= g < NH:
                            pe.wait_ge(norm_ready.sem, norm_ready.at(NH * b + g + 1))
                            pe.wait_ge(at_ready.sem, at_ready.at(NH * b + g - 1))
                            for t in range(NKT):
                                ins = pe.transpose(ps[4 + g % 2][0:KT, t * S:(t + 1) * S],
                                                   A[g % 4][:, t * KT:(t + 1) * KT], core.ident[0:S, 0:S])
                            ins.then_inc(at_psum.sem, 1)
                        g = h - LAG_V
                        if 0 <= g < NH and g % 2:
                            m = g // 2
                            pe.wait_ge(at_ready.sem, at_ready.at(NH * b + g + 1))
                            pe.wait_ge(v_ready.sem, v_ready.at(6 * b + 6))
                            pe.wait_ge(ot_ready.sem, ot_ready.at(16 * b + 2 * m - 2))
                            if m == 0:
                                pe.wait_ge(o_used.sem, o_used.at(b))
                            for t in range(NKT):
                                ins = pe.matmul(ps[6 + m % 2][:, 0:2 * S], V[:, t, m * P:(m + 1) * P],
                                                AT[m % 2][:, t, :, :].rearrange("p c s -> p (c s)"), start=t == 0,
                                                stop=t == NKT - 1)
                            ins.then_inc(av_psum.sem, 1)
                        if more and h == NH:
                            query(b + 1, 0)
                            query(b + 1, 1)
                        if more and NH < h <= NH + 4:
                            key(b + 1, 1 - j, i + j, 2 * (h - NH) - 2)
                            key(b + 1, 1 - j, i + j, 2 * (h - NH) - 1)
                    pe.wait_ge(ot_ready.sem, ot_ready.at(16 * b + 16))
                    for t in range(8):
                        ins = pe.matmul(ps[6][0:S, 0:D], OT[:, t, :], w["Wo"][:, t, :], start=t == 0, stop=t == 7)
                    ins.then_inc(o_psum.sem, 1)

                query(0, 0)
                query(0, 1)
                for t in range(8):
                    key(0, 0, 0, t)
                batches(pe, run)

            @block.vector
            def _(dve):
                chain = Chain(dve, own)
                dve.wait_ge(core.loaded["head64"], core.loads["head64"])
                dve.wait_ge(zeroed.sem, 6)
                chain.step(dve.tensor_scalar(bq8[:, :], w["bq"][:, :], 0.125, None, ALU.mult))

                def query(b):
                    for u in range(2):
                        dve.wait_ge(q_psum.sem, q_psum.at(2 * b + u + 1))
                        if u == 0:
                            dve.wait_ge(s_psum.sem, s_psum.at(NH * b))
                        for c in range(2):
                            half = slice(64 * c, 64 * c + 64)
                            dve.scalar_tensor_tensor(
                                QH[c][half, 4 * u:4 * u + 4, :],
                                ps[u][half, 0:4 * S].rearrange("p (q s) -> p q s", q=4), 0.125,
                                wide(bq8[half, 4 * u:4 * u + 4], S), ALU.mult, ALU.add).then_inc(q_ready.sem, 1)

                def run(b, j, i, more):
                    for t in range(6):
                        dve.wait_ge(v_psum.sem, v_psum.at(6 * b + t + 1))
                        if t == 0:
                            dve.wait_ge(av_psum.sem, av_psum.at(8 * b))
                        dve.tensor_copy(V[:, t // 2, 512 * (t % 2):512 * (t % 2) + 512],
                                        ps[(10 + t) % 4][0:KT, :]).then_inc(v_ready.sem, 1)
                    for h in range(NH + LAG_V + 2):
                        if h < NH:
                            dve.wait_ge(s_psum.sem, s_psum.at(NH * b + h + 1))
                            dve.tensor_reduce(neg_max[:, h % 4:h % 4 + 1], ps[(16 + h) % 4][0:S, 0:KV], AX.X,
                                              ALU.max, negate=True).then_inc(max_ready.sem, 1)
                        g = h - 1
                        if 0 <= g < NH:
                            dve.wait_ge(exp_ready.sem, exp_ready.at(NH * b + g + 1))
                            chain.step(dve.reciprocal(inv[:, g % 4:g % 4 + 1], total[:, g % 4:g % 4 + 1]))
                            dve.tensor_scalar(A[g % 4][:, 0:KV], A[g % 4][:, 0:KV], inv[:, g % 4:g % 4 + 1], None,
                                              ALU.mult).then_inc(norm_ready.sem, 1)
                        g = h - LAG_V - 1
                        if 0 <= g < NH and g % 2:
                            m = g // 2
                            dve.wait_ge(av_psum.sem, av_psum.at(8 * b + m + 1))
                            if m == 0:
                                dve.wait_ge(o_psum.sem, o_psum.at(b))
                            for c in range(2):
                                half = slice(64 * c, 64 * c + 64)
                                dve.tensor_scalar(OT[half, m, :], ps[6 + m % 2][half, c * S:(c + 1) * S],
                                                  w["bv"][half, m:m + 1], None, ALU.add).then_inc(ot_ready.sem, 1)
                        if more and h == NH + 1:
                            query(b + 1)
                    dve.wait_ge(o_psum.sem, o_psum.at(b + 1))
                    dve.wait_ge(rows_added.sem, 2)
                    dve.tensor_tensor(O[:, :], ps[6][0:S, 0:D], N[:, bass.ds(b, 1), :], ALU.add).then_inc(o_used.sem, 1)
                    dve.wait_ge(o_used.sem, o_used.at(b + 1))
                    chain.step(dve.bn_stats(stats[:, 0, :], O[:, :]))
                    variance(dve, chain, stats[:, :, :], mv[:, 0:1], mv[:, 2:3], mv[:, 1:2]).then_inc(var_ready.sem, 1)
                    chain.step(dve.tensor_scalar(mv[:, 0:1], mv[:, 0:1], 0.5, None, ALU.mult))
                    dve.wait_ge(rstd_ready.sem, b + 1)
                    chain.step(dve.tensor_scalar(O[:, :], O[:, :], mv[:, 0:1], rstd[:, :], ALU.subtract, ALU.mult))
                    dve.tensor_tensor(O[:, :], O[:, :], core.rows[0:S, GAMMA, :], ALU.mult).then_inc(x_ready.sem, 1)
                    dve.wait_ge(x_ready.sem, 2 * b + 1)
                    xb = X[:, bass.ds(b, 1), :]
                    dve.tensor_tensor(xb, xb, O[:, :].unsqueeze(1), ALU.add).then_inc(x_ready.sem, 1)
                    dve.wait_ge(x_ready.sem, 2 * b + 2)

                query(0)
                batches(dve, run, chain, NH + 8)

            @block.scalar
            def _(act):
                act.wait_ge(core.loaded["head64"], core.loads["head64"])

                def key(b, t):
                    act.wait_ge(k_psum.sem, k_psum.at(8 * b + t + 1))
                    if t == 0:
                        act.wait_ge(s_psum.sem, s_psum.at(NH * b))
                    act.activation(KTr[:, t, 0:KV], ps[(2 + t) % 4][:, 0:KV], ACT.Identity,
                                   bias=w["bk"][:, t:t + 1]).then_inc(k_ready.sem, 1)

                def run(b, j, i, more):
                    for h in range(NH + LAG_T + 2):
                        if h < NH:
                            act.wait_ge(max_ready.sem, max_ready.at(NH * b + h + 1))
                            act.wait_ge(at_psum.sem, at_psum.at(NH * b + h - 3))
                            act.activation(A[h % 4][:, 0:KV], ps[(16 + h) % 4][0:S, 0:KV], ACT.Exp,
                                           bias=neg_max[:, h % 4:h % 4 + 1],
                                           accum_out=total[:, h % 4:h % 4 + 1]).then_inc(exp_ready.sem, 1)
                        g = h - LAG_T
                        if 0 <= g < NH:
                            act.wait_ge(at_psum.sem, at_psum.at(NH * b + g + 1))
                            act.wait_ge(av_psum.sem, av_psum.at(8 * b + g // 2 - 1))
                            act.activation(AT[g // 2 % 2][:, :, g % 2, :],
                                           ps[4 + g % 2][0:KT, 0:NKT * S].rearrange("p (t s) -> p t s", t=NKT),
                                           ACT.Copy).then_inc(at_ready.sem, 1)
                        if more and NH < h <= NH + 4:
                            key(b + 1, 2 * (h - NH) - 2)
                            key(b + 1, 2 * (h - NH) - 1)

                for t in range(8):
                    key(0, t)
                batches(act, run)


def ternary_ffn(core, io):
    X, N, NT, ps = core.X, core.N, core.NT, core.ps
    HT = 8
    with Stage(core) as st:
        w1, w2, conv_w, conv_b = (core.weights[n] for n in ("w1", "w2", "conv_w", "conv_b"))
        w1q, w2q = st.sb("w1q", [P, KD, 1024], BF16), st.sb("w2q", [P, HT, D], BF16)
        part = st.sb("part", [P, 2])
        wmean, winv = st.sb("wmean", [P, 2]), st.sb("winv", [P, 2])
        am, scale, inv, inv2 = (st.sb(n, [S, NB]) for n in ("am", "scale", "inv", "inv2"))
        am2, scale2 = st.sb("am2", [S, 4]), st.sb("scale2", [S, 1])
        tmp = st.sb("tmp", [S, D])
        Q = [st.sb(f"Q{j}", [S, D], BF16) for j in range(2)]
        QT = [st.sb(f"QT{j}", [P, KD, S], BF16) for j in range(2)]
        inv_rows = st.sb("inv_rows", [P, T])
        HP = st.sb("HP", [P, HT, S + 2])
        C = [st.sb(f"C{j}", [P, HT, S]) for j in range(2)]
        tmp2 = st.sb("tmp2", [S, 1024])
        Q2 = st.sb("Q2", [S, 1024], BF16)
        Q2T = [st.sb(f"Q2T{j}", [P, HT, S], BF16) for j in range(2)]
        ctT = [st.sb(f"ctT{j}", [P, KD, KVP]) for j in range(2)]
        Wk, Wv, bk = (core.weights[n] for n in ("L3_Wk", "L3_Wv", "L3_bk"))
        ctx_loaded, ctx_psum, ctx_used = [st.event(), st.event()], st.event(4), st.event(1)
        own, own_pool, part_ready, mean_psum, winv_ready, pads, inv_ready = (st.event() for _ in range(7))
        w_ready = [st.event(), st.event()]
        q_ready, qt_psum, qt_ready, rows_psum, h_psum, hp_ready = (st.event(4) for _ in range(6))
        rows_ready = st.event()
        c_ready, conv_ready, silu_ready, ht_psum, q2_ready, q2t_psum, q2t_ready, y_psum, x_ready = \
            (st.event(4) for _ in range(9))
        amax_ready, q2_used, middle_ready = st.event(2), st.event(2), st.event()

        def ternary(eng, chain, wt, wq, n):
            chain.step(eng.tensor_scalar(wt[:, :, :], wt[:, :, :], winv[:, n:n + 1], MAGIC, ALU.mult, ALU.add))
            chain.step(eng.tensor_scalar(wt[:, :, :], wt[:, :, :], MAGIC - 1, MAGIC + 1, ALU.max, ALU.min))
            eng.tensor_scalar(wq[:, :, :], wt[:, :, :], MAGIC, None, ALU.subtract).then_inc(w_ready[n].sem, 1)

        with st.block() as block:
            @block.sync
            def _(sp):
                st.heads(sp)
                with sp.Fori(0, NB // 2) as i:
                    for j in range(2):
                        b = 2 * i + j
                        sp.wait_ge(ctx_psum.sem, ctx_psum.at(4 * (b - 1)))
                        sp.dma_start(ctT[j][:, :, :], io["ctT"][bass.ds(b, 1)]).then_inc(ctx_loaded[j].sem, 16)

            @block.gpsimd
            def _(pool):
                pool.memset(HP[:, :, 0:1], 0.0).then_inc(pads.sem, 1)
                pool.memset(HP[:, :, S + 1:S + 2], 0.0).then_inc(pads.sem, 1)
                chain = Chain(pool, own_pool)
                pool.wait_ge(winv_ready.sem, 1)
                ternary(pool, chain, w2, w2q, 1)

            @block.tensor
            def _(pe):
                pe.wait_ge(part_ready.sem, 2)
                pe.matmul(ps[7][:, 0:2], core.ones[:, :], part[:, :], start=True, stop=True).then_inc(mean_psum.sem, 1)
                pe.wait_ge(inv_ready.sem, 1)
                for b in range(NB):
                    ins = pe.matmul(ps[4 + b // 4][:, (b % 4) * S:(b % 4 + 1) * S],
                                    inv[:, b:b + 1].broadcast_to([S, P]), core.ident[0:S, 0:S], start=True, stop=True)
                ins.then_inc(rows_psum.sem, 1)

                def front(b, j):
                    pe.wait_ge(q_ready.sem, q_ready.at(b + 1))
                    pe.wait_ge(qt_ready.sem, qt_ready.at(b))
                    for k in range(KD):
                        ins = pe.transpose(ps[0][:, :].bitcast(BF16)[:, k * S:(k + 1) * S], Q[j][:, k * P:(k + 1) * P],
                                           core.identb[0:S, 0:S])
                    ins.then_inc(qt_psum.sem, 1)
                    pe.wait_ge(qt_ready.sem, qt_ready.at(b + 1))
                    pe.wait_ge(hp_ready.sem, hp_ready.at(2 * b))
                    for t in range(HT):
                        for k in range(KD):
                            ins = pe.matmul(ps[2 + t // 4][:, (t % 4) * S:(t % 4 + 1) * S],
                                            w1q[:, k, t * P:(t + 1) * P], QT[j][:, k, :], start=k == 0, stop=k == KD - 1)
                        if t % 4 == 3:
                            ins.then_inc(h_psum.sem, 1)

                def context(b, j, i, n):
                    if n == 0:
                        pe.wait_ge(ctx_loaded[j].sem, 16 * (i + 1))
                    pe.wait_ge(ctx_used.sem, ctx_used.at(4 * b + n))
                    if n < 2:
                        for k in range(KD):
                            ins = pe.matmul(ps[1][:, 0:KVP], Wk[:, k, n * P:(n + 1) * P], ctT[j][:, k, :],
                                            start=k == 0, stop=k == KD - 1)
                    else:
                        for t in ((0, 1), (2,))[n - 2]:
                            for k in range(KD):
                                ins = pe.matmul(ps[1][0:KT, t % 2 * D:(t % 2 + 1) * D],
                                                ctT[j][:, k, t * KT:(t + 1) * KT], Wv[:, k, :], start=k == 0,
                                                stop=k == KD - 1)
                    ins.then_inc(ctx_psum.sem, 1)

                def run(b, j, i, more):
                    pe.wait_ge(q2_used.sem, q2_used.at(2 * b))
                    for t in range(HT):
                        if t % 4 == 0:
                            pe.wait_ge(silu_ready.sem, silu_ready.at(2 * b + t // 4 + 1))
                        ins = pe.transpose(ps[4 + t // 4][0:S, (t % 4) * P:(t % 4 + 1) * P], C[j][:, t, :],
                                           core.ident[:, :])
                        if t % 4 == 3:
                            ins.then_inc(ht_psum.sem, 1)
                    if more:
                        front(b + 1, 1 - j)
                    context(b, j, i, 0)
                    pe.wait_ge(q2_ready.sem, q2_ready.at(b + 1))
                    pe.wait_ge(q2t_ready.sem, q2t_ready.at(b))
                    for t in range(HT):
                        ins = pe.transpose(ps[6][:, :].bitcast(BF16)[:, t * S:(t + 1) * S], Q2[:, t * P:(t + 1) * P],
                                           core.identb[0:S, 0:S])
                    ins.then_inc(q2t_psum.sem, 1)
                    pe.wait_ge(q2t_ready.sem, q2t_ready.at(b + 1))
                    pe.wait_ge(x_ready.sem, x_ready.at(b))
                    for t in range(HT):
                        ins = pe.matmul(ps[7][0:S, 0:D], Q2T[j][:, t, :], w2q[:, t, :], start=t == 0, stop=t == HT - 1)
                    ins.then_inc(y_psum.sem, 1)
                    for n in range(1, 4):
                        context(b, j, i, n)

                pe.wait_ge(core.loaded["context"], core.loads["context"])
                pe.wait_ge(w_ready[0].sem, 1)
                front(0, 0)
                pe.wait_ge(w_ready[1].sem, 1)
                batches(pe, run)

            @block.vector
            def _(dve):
                chain = Chain(dve, own)
                dve.wait_ge(core.loaded["ternary"], core.loads["ternary"])
                dve.tensor_reduce(part[:, 0:1], w1[:, :, :], AX.XY, ALU.add,
                                  apply_absolute_value=True).then_inc(part_ready.sem, 1)
                dve.wait_ge(mean_psum.sem, 1)
                chain.step(dve.tensor_scalar(wmean[:, :], ps[7][:, 0:2], 1.0 / (D * 1024), 1e-5, ALU.mult, ALU.max))
                dve.reciprocal(winv[:, :], wmean[:, :]).then_inc(winv_ready.sem, 1)
                dve.wait_ge(winv_ready.sem, 1)
                ternary(dve, chain, w1, w1q, 0)
                chain.step(dve.tensor_reduce(am[:, :], N[:, :, :], AX.X, ALU.max, apply_absolute_value=True))
                chain.step(dve.tensor_scalar(am[:, :], am[:, :], 1e-5, None, ALU.max))
                chain.step(dve.reciprocal(scale[:, :], am[:, :]))
                chain.step(dve.tensor_scalar(scale[:, :], scale[:, :], 127.0, None, ALU.mult))
                dve.tensor_scalar(inv[:, :], am[:, :], wmean[0:S, 0:1], 1.0 / 127, ALU.mult, ALU.mult).then_inc(inv_ready.sem, 1)
                dve.wait_ge(pads.sem, 2)

                def quantise(b, j):
                    sc = scale[:, bass.ds(b, 1)]
                    chain.step(dve.tensor_scalar(tmp[:, :].unsqueeze(1), N[:, bass.ds(b, 1), :], sc, MAGIC, ALU.mult,
                                                 ALU.add))
                    dve.wait_ge(qt_psum.sem, qt_psum.at(b - 1))
                    dve.tensor_scalar(Q[j][:, :], tmp[:, :], MAGIC, 127.0, ALU.subtract, ALU.min).then_inc(q_ready.sem, 1)

                def convolve(b, j):
                    for u in range(2):
                        dve.wait_ge(h_psum.sem, h_psum.at(2 * b + u + 1))
                        if u == 0:
                            dve.wait_ge(conv_ready.sem, conv_ready.at(8 * b))
                        dve.tensor_tensor(HP[:, 4 * u:4 * u + 4, 1:S + 1],
                                          ps[2 + u][:, 0:4 * S].rearrange("p (t s) -> p t s", t=4),
                                          pair(inv_rows[:, token(b)], 4), ALU.mult).then_inc(hp_ready.sem, 1)
                    for t in range(HT + 1):
                        if t < HT:
                            dve.wait_ge(c_ready.sem, c_ready.at(8 * b + t + 1))
                            dve.scalar_tensor_tensor(C[j][:, t, :], HP[:, t, 1:S + 1], conv_w[:, t, 1:2], C[j][:, t, :],
                                                     ALU.mult, ALU.add).then_inc(middle_ready.sem, 1)
                        if t > 0:
                            dve.wait_ge(middle_ready.sem, middle_ready.at(8 * b + t))
                            dve.scalar_tensor_tensor(C[j][:, t - 1, :], HP[:, t - 1, 2:S + 2], conv_w[:, t - 1, 2:3],
                                                     C[j][:, t - 1, :], ALU.mult, ALU.add).then_inc(conv_ready.sem, 1)

                def run(b, j, i, more):
                    if more:
                        quantise(b + 1, 1 - j)
                    for u in range(2):
                        dve.wait_ge(ht_psum.sem, ht_psum.at(2 * b + u + 1))
                        dve.tensor_reduce(am2[:, u:u + 1], ps[4 + u][0:S, :], AX.X, ALU.max,
                                          apply_absolute_value=True).then_inc(amax_ready.sem, 1)
                    dve.wait_ge(amax_ready.sem, amax_ready.at(2 * b + 2))
                    chain.step(dve.tensor_tensor(am2[:, 2:3], am2[:, 0:1], am2[:, 1:2], ALU.max))
                    chain.step(dve.tensor_scalar(am2[:, 2:3], am2[:, 2:3], 1e-5, None, ALU.max))
                    chain.step(dve.reciprocal(scale2[:, :], am2[:, 2:3]))
                    chain.step(dve.tensor_scalar(scale2[:, :], scale2[:, :], 127.0, None, ALU.mult))
                    chain.step(dve.tensor_scalar(am2[:, 3:4], am2[:, 2:3], wmean[0:S, 1:2], 1.0 / 127, ALU.mult, ALU.mult))
                    for u in range(2):
                        dve.tensor_scalar(tmp2[:, 512 * u:512 * u + 512], ps[4 + u][0:S, :], scale2[:, :], MAGIC,
                                          ALU.mult, ALU.add).then_inc(q2_used.sem, 1)
                    dve.wait_ge(q2_used.sem, q2_used.at(2 * b + 2))
                    dve.wait_ge(q2t_psum.sem, q2t_psum.at(b))
                    dve.tensor_scalar(Q2[:, :], tmp2[:, :], MAGIC, 127.0, ALU.subtract, ALU.min).then_inc(q2_ready.sem, 1)
                    if more:
                        convolve(b + 1, 1 - j)
                    dve.wait_ge(y_psum.sem, y_psum.at(b + 1))
                    xb = X[:, bass.ds(b, 1), :]
                    chain.step(dve.tensor_scalar(tmp[:, :], ps[7][0:S, 0:D], am2[:, 3:4], None, ALU.mult))
                    dve.tensor_tensor(xb, xb, tmp[:, :].unsqueeze(1), ALU.add).then_inc(x_ready.sem, 1)
                    dve.wait_ge(x_ready.sem, x_ready.at(b + 1))

                quantise(0, 0)
                dve.wait_ge(rows_ready.sem, 2)
                convolve(0, 0)
                batches(dve, run, chain, 7)

            @block.scalar
            def _(act):
                act.wait_ge(core.loaded["ternary"], core.loads["ternary"])
                act.activation(w2q[:, :, :], w2[:, :, :], ACT.Abs, accum_out=part[:, 1:2]).then_inc(part_ready.sem, 1)
                act.wait_ge(rows_psum.sem, rows_psum.at(1))
                for u in range(2):
                    act.activation(inv_rows[:, 4 * u * S:4 * (u + 1) * S], ps[4 + u][:, 0:4 * S],
                                   ACT.Copy).then_inc(rows_ready.sem, 1)

                def turn(b, j):
                    act.wait_ge(qt_psum.sem, qt_psum.at(b + 1))
                    act.wait_ge(h_psum.sem, h_psum.at(2 * b - 2))
                    act.activation(QT[j][:, :, :], ps[0][:, :].bitcast(BF16)[:, 0:KD * S].rearrange(
                        "p (k s) -> p k s", k=KD), ACT.Copy).then_inc(qt_ready.sem, 1)

                def context(b, n):
                    act.wait_ge(ctx_psum.sem, ctx_psum.at(4 * b + n + 1))
                    if n < 2:
                        ins = act.activation(core.K_all[:, bass.ds(b, 1), n * KVP:(n + 1) * KVP],
                                             ps[1][:, 0:KVP].unsqueeze(1), ACT.Identity, bias=bk[:, n:n + 1])
                    else:
                        cols = slice(0, 2 * D) if n == 2 else slice(2 * D, 3 * D)
                        ins = act.activation(core.V_all[:, bass.ds(b, 1), cols],
                                             ps[1][0:KT, 0:cols.stop - cols.start].unsqueeze(1), ACT.Copy)
                    ins.then_inc(ctx_used.sem, 1)

                def run(b, j, i, more):
                    if more:
                        turn(b + 1, 1 - j)
                    context(b, 0)
                    act.wait_ge(q2t_psum.sem, q2t_psum.at(b + 1))
                    act.wait_ge(y_psum.sem, y_psum.at(b - 1))
                    act.activation(Q2T[j][:, :, :], ps[6][:, :].bitcast(BF16)[:, 0:HT * S].rearrange(
                        "p (t s) -> p t s", t=HT), ACT.Copy).then_inc(q2t_ready.sem, 1)
                    for u in range(2):
                        if more:
                            first_tap(b + 1, 1 - j, u)
                        context(b, 1 + u)
                    if more:
                        silu(b + 1, 1 - j)
                    context(b, 3)

                def first_tap(b, j, u):
                    act.wait_ge(hp_ready.sem, hp_ready.at(2 * b + u + 1))
                    if u == 0:
                        act.wait_ge(ht_psum.sem, ht_psum.at(2 * b - 2))
                    for t in range(4 * u, 4 * u + 4):
                        act.activation(C[j][:, t, :], HP[:, t, 0:S], ACT.Identity, scale=conv_w[:, t, 0:1],
                                       bias=conv_b[:, t:t + 1]).then_inc(c_ready.sem, 1)

                def silu(b, j):
                    for u in range(2):
                        act.wait_ge(conv_ready.sem, conv_ready.at(8 * b + 4 * u + 4))
                        act.activation(C[j][:, 4 * u:4 * u + 4, :], C[j][:, 4 * u:4 * u + 4, :],
                                       ACT.Silu).then_inc(silu_ready.sem, 1)

                act.wait_ge(core.loaded["context"], core.loads["context"])
                turn(0, 0)
                first_tap(0, 0, 0)
                first_tap(0, 0, 1)
                silu(0, 0)
                batches(act, run)


def heads16(core, io, layer):
    X, N, NT, ps = core.X, core.N, core.NT, core.ps
    soft = layer == 2
    NHT = 8
    with Stage(core) as st:
        ctT = [st.sb(f"ctT{j}", [P, KD, KVP]) for j in range(2)] if soft else None
        Kt = st.sb("Kt", [P, KD, KVP])
        Qz = st.sb("Qz", [P, KD, NHT, S])
        Vz = st.sb("Vz", [KT, NKT * KD * NHT * P + P])
        OT = [st.sb(f"OT{j}", [P, KD, S]) for j in range(2)]

        def v_blocks(t, k):
            at = (t * KD + k) * NHT * P
            return Vz[:, at:at + NHT * (P + 16)].rearrange("p (h e) -> p h e", e=P + 16)[:, :, 0:16]

        def v_head(t, h, rows=KT):
            at = (t * NH + h) * P
            return Vz[0:rows, at:at + P]

        ctx_loaded, mask_loaded = [st.event(), st.event()], [st.event(), st.event()]
        zeroed, bias_added, inv_ready = st.event(), st.event(), st.event()
        q_psum, q_ready, k_psum, k_ready, v_psum, v_ready = (st.event(8) for _ in range(6))
        s_psum, max_ready, exp_ready, norm_ready, at_psum, at_ready = (st.event(4) for _ in range(6))
        masked, mask_ready = st.event(4), st.event(4)
        av_psum, ot_ready, o_psum, x_ready = (st.event(4) for _ in range(4))
        if soft:
            mask_i = [st.sb(f"mask_i{j}", [S, KV], I32) for j in range(2)]
            mask = [st.sb(f"mask{j}", [S, KV]) for j in range(2)]
            A = [st.sb(f"A{c}", [S, KVP]) for c in range(4)]
            AT = [st.sb(f"AT{c}", [KT, NKT, 2, S]) for c in range(2)]
            neg_max, total, inv = st.sb("neg_max", [S, 4]), st.sb("total", [S, 4]), st.sb("inv", [S, 4])
            wh, wo = core.weights["W_heads"], core.weights["W_o"]
        else:
            AS = st.sb("AS", [KT, NKT, NH, S])
            wq, wo, bq = (core.weights[n] for n in ("L3_Wq", "L3_Wo", "L3_bq"))

        with st.block() as block:
            @block.sync
            def _(sp):
                st.heads(sp)
                if not soft:
                    return
                with sp.Fori(0, NB // 2) as i:
                    for j in range(2):
                        b = 2 * i + j
                        sp.wait_ge(v_psum.sem, v_psum.at(4 * b - 4))
                        sp.dma_start(ctT[j][:, :, :], io["ctT"][bass.ds(b, 1)]).then_inc(ctx_loaded[j].sem, 16)
                        sp.wait_ge(mask_ready.sem, mask_ready.at(b - 1))
                        sp.dma_start(mask_i[j][:, :], io["mask"][bass.ds(b, 1)]).then_inc(mask_loaded[j].sem, 16)

            @block.gpsimd
            def _(pool):
                pool.memset(Vz[:, :], 0.0).then_inc(zeroed.sem, 1)
                pool.wait_ge(zeroed.sem, 1)
                if not soft:
                    pool.tensor_tensor(X[:, :, :], X[:, :, :], pair(core.rows[0:S, L3_BO, :], NB),
                                       ALU.add).then_inc(bias_added.sem, 1)
                else:
                    for c in range(4):
                        pool.memset(A[c][:, KV:KVP], 0.0).then_inc(zeroed.sem, 1)
                    with pool.Fori(0, NB) as b:
                        for h in range(NH):
                            pool.wait_ge(inv_ready.sem, inv_ready.at(NH * b + h + 1))
                            pool.tensor_tensor(A[h % 4][:, 0:KV], A[h % 4][:, 0:KV],
                                               inv[:, h % 4:h % 4 + 1].broadcast_to([S, KV]),
                                               ALU.mult).then_inc(norm_ready.sem, 1)

            heads_zeroed = 5 if soft else 1

            def bank_free(eng, b, u):
                n = NH if soft else 12
                if u < 4:
                    eng.wait_ge(exp_ready.sem, exp_ready.at(n * b + u - 3))
                elif not soft:
                    if u < 10:
                        eng.wait_ge(q_ready.sem, q_ready.at(2 * b + u - 7))
                    else:
                        eng.wait_ge(exp_ready.sem, exp_ready.at(n * b + u - 11))
                elif u < 6:
                    eng.wait_ge(q_ready.sem, q_ready.at(2 * b + u - 3))
                elif u < 8:
                    eng.wait_ge(k_ready.sem, k_ready.at(2 * b + u - 5))
                elif u < 12:
                    eng.wait_ge(v_ready.sem, v_ready.at(4 * b + u - 7))
                else:
                    eng.wait_ge(exp_ready.sem, exp_ready.at(n * b + u - 11))

            V_USES = [[(0, 0), (0, 1)], [(0, 2)], [(1, 0), (1, 1)], [(1, 2)]]

            @block.tensor
            def _(pe):
                pe.wait_ge(core.loaded["heads16"], core.loads["heads16"])

                def queries_and_keys(b, j, i):
                    if soft:
                        pe.wait_ge(ctx_loaded[j].sem, 16 * (i + 1))
                    for m in range(KD):
                        bank_free(pe, b, m)
                        if soft:
                            ins = pe.matmul(ps[m][:, 0:S], wh[:, :], NT[:, m, token(b)], start=True, stop=True)
                        else:
                            for k in range(KD):
                                ins = pe.matmul(ps[m][:, 0:S], wq[:, k, m * P:(m + 1) * P], NT[:, k, token(b)],
                                                start=k == 0, stop=k == KD - 1)
                        ins.then_inc(q_psum.sem, 1)
                    for m in range(KD if soft else 0):
                        bank_free(pe, b, 2 + m)
                        pe.matmul(ps[2 + m][:, 0:KVP], wh[:, :], ctT[j][:, m, :], start=True,
                                  stop=True).then_inc(k_psum.sem, 1)

                def run(b, j, i, more):
                    for c, tiles in enumerate(V_USES if soft else []):
                        bank_free(pe, b, 4 + c)
                        for n, (m, t) in enumerate(tiles):
                            out = ps[c][0:KT, n * P:(n + 1) * P]
                            rows = slice(t * KT, (t + 1) * KT)
                            ins = pe.matmul(out, ctT[j][:, m, rows], wh[:, :], start=True, stop=True)
                        ins.then_inc(v_psum.sem, 1)
                    if soft:
                        for h in range(NH + LAG_V + 1):
                            if h < NH:
                                u = 8 + h
                                bank_free(pe, b, u)
                                pe.wait_ge(q_ready.sem, q_ready.at(2 * b + h // 8 + 1))
                                pe.wait_ge(k_ready.sem, k_ready.at(2 * b + h // 8 + 1))
                                pe.matmul(ps[u % 4][0:S, 0:KV], Qz[:, h // 8, h % 8, :], Kt[:, h // 8, 0:KV],
                                          start=True, stop=True).then_inc(s_psum.sem, 1)
                            g = h - LAG_T
                            if 0 <= g < NH:
                                pe.wait_ge(norm_ready.sem, norm_ready.at(NH * b + g + 1))
                                pe.wait_ge(at_ready.sem, at_ready.at(NH * b + g - 1))
                                for t in range(NKT):
                                    ins = pe.transpose(ps[4 + g % 2][0:KT, t * S:(t + 1) * S],
                                                       A[g % 4][:, t * KT:(t + 1) * KT], core.ident[0:S, 0:S])
                                ins.then_inc(at_psum.sem, 1)
                            g = h - LAG_V
                            if 0 <= g < NH:
                                pe.wait_ge(at_ready.sem, at_ready.at(NH * b + g + 1))
                                pe.wait_ge(v_ready.sem, v_ready.at(4 * b + 4))
                                if g == 0:
                                    pe.wait_ge(x_ready.sem, x_ready.at(b))
                                for t in range(NKT):
                                    ins = pe.matmul(ps[6 + g // 8][:, 0:S], v_head(t, g), AT[g // 2 % 2][:, t, g % 2, :],
                                                    start=g % 8 == 0 and t == 0, stop=g % 8 == 7 and t == NKT - 1)
                                ins.then_inc(av_psum.sem, 1)
                            if more and h == NH:
                                queries_and_keys(b + 1, 1 - j, i + j)
                    else:
                        pe.wait_ge(q_ready.sem, q_ready.at(2 * b + 2))
                        pe.wait_ge(k_ready.sem, k_ready.at(2 * b + 2))
                        for u in range(12):
                            m, t, half = u // 6, u // 2 % 3, u % 2
                            bank_free(pe, b, 8 + u)
                            rows = KT if t < NKT - 1 else KV - (NKT - 1) * KT
                            pe.matmul(ps[u % 4][0:rows, 0:4 * S], Kt[:, m, t * KT:t * KT + rows],
                                      Qz[:, m, 4 * half:4 * half + 4, :].rearrange("p h s -> p (h s)"), start=True,
                                      stop=True).then_inc(s_psum.sem, 1)
                        if more:
                            queries_and_keys(b + 1, 1 - j, i + j)
                        for m in range(KD):
                            pe.wait_ge(v_ready.sem, v_ready.at(4 * b + 4))
                            pe.wait_ge(exp_ready.sem, exp_ready.at(12 * b + 6 * m + 6))
                            if m == 0:
                                pe.wait_ge(x_ready.sem, x_ready.at(b))
                            for g in range(NHT):
                                for t in range(NKT):
                                    rows = KT if t < NKT - 1 else KV - (NKT - 1) * KT
                                    ins = pe.matmul(ps[6 + m][:, 0:S], v_head(t, NHT * m + g, rows),
                                                    AS[0:rows, t, NHT * m + g, :], start=g == 0 and t == 0,
                                                    stop=g == NHT - 1 and t == NKT - 1)
                            ins.then_inc(av_psum.sem, 1)
                    pe.wait_ge(ot_ready.sem, ot_ready.at(2 * b + 2))
                    for k in range(KD):
                        ins = pe.matmul(ps[6][0:S, 0:D], OT[j][:, k, :], wo[:, k, :], start=k == 0, stop=k == KD - 1)
                    ins.then_inc(o_psum.sem, 1)

                queries_and_keys(0, 0, 0)
                pe.wait_ge(zeroed.sem, heads_zeroed)
                batches(pe, run)

            @block.vector
            def _(dve):
                dve.wait_ge(core.loaded["heads16"], core.loads["heads16"])
                av_events = NH if soft else 2

                def queries(b):
                    for m in range(KD):
                        dve.wait_ge(q_psum.sem, q_psum.at(2 * b + m + 1))
                        if m == 0:
                            dve.wait_ge(s_psum.sem, s_psum.at((NH if soft else 12) * b))
                        dve.scalar_tensor_tensor(Qz[:, m, :, :], pair(ps[m][:, 0:S], NHT),
                                                 1.0 / 16 if soft else bq[:, m:m + 1], wide(core.head_mask[:, :], S),
                                                 ALU.mult if soft else ALU.add, ALU.mult).then_inc(q_ready.sem, 1)

                def run(b, j, i, more):
                    for c, tiles in enumerate(V_USES):
                        if soft:
                            dve.wait_ge(v_psum.sem, v_psum.at(4 * b + c + 1))
                        if c == 0:
                            dve.wait_ge(av_psum.sem, av_psum.at(av_events * b))
                        for n, (m, t) in enumerate(tiles):
                            src = ps[c][0:KT, n * P:(n + 1) * P].rearrange("p (h e) -> p h e", e=16)
                            if soft:
                                ins = dve.tensor_copy(v_blocks(t, m), src)
                            else:
                                src = core.V_all[:, bass.ds(b, 1), t * D + m * P:t * D + (m + 1) * P].rearrange(
                                    "p o (h e) -> p (o h) e", e=16)
                                ins = dve.tensor_tensor(v_blocks(t, m), src, core.rows[
                                    0:KT, L3_BV, m * P:(m + 1) * P].rearrange("p (h e) -> p h e", e=16), ALU.add)
                        ins.then_inc(v_ready.sem, 1)
                    if soft:
                        dve.wait_ge(mask_loaded[j].sem, 16 * (i + 1))
                        dve.tensor_scalar(mask[j][:, :], mask_i[j][:, :], 0.0, None,
                                          ALU.not_equal).then_inc(mask_ready.sem, 1)
                        dve.wait_ge(mask_ready.sem, mask_ready.at(b + 1))
                        for h in range(NH + LAG_V + 2):
                            if h < NH:
                                bank = ps[(8 + h) % 4][0:S, 0:KV]
                                dve.wait_ge(s_psum.sem, s_psum.at(NH * b + h + 1))
                                dve.scalar_tensor_tensor(bank, bank, 1e-20 / 16, mask[j][:, :], ALU.add,
                                                         ALU.mult).then_inc(masked.sem, 1)
                                dve.wait_ge(masked.sem, masked.at(NH * b + h + 1))
                                dve.tensor_reduce(neg_max[:, h % 4:h % 4 + 1], bank, AX.X, ALU.max,
                                                  negate=True).then_inc(max_ready.sem, 1)
                            g = h - 1
                            if 0 <= g < NH:
                                dve.wait_ge(exp_ready.sem, exp_ready.at(NH * b + g + 1))
                                dve.wait_ge(norm_ready.sem, norm_ready.at(NH * b + g - 3))
                                dve.reciprocal(inv[:, g % 4:g % 4 + 1],
                                               total[:, g % 4:g % 4 + 1]).then_inc(inv_ready.sem, 1)
                            if more and h == NH + 1:
                                queries(b + 1)
                            g = h - LAG_V - 1
                            if 0 <= g < NH and g % 8 == 7:
                                if g == 7:
                                    dve.wait_ge(o_psum.sem, o_psum.at(b - 1))
                                dve.wait_ge(av_psum.sem, av_psum.at(NH * b + g + 1))
                                dve.tensor_copy(OT[j][:, g // 8, :], ps[6 + g // 8][:, 0:S]).then_inc(ot_ready.sem, 1)
                    else:
                        if more:
                            queries(b + 1)
                        for m in range(KD):
                            if m == 0:
                                dve.wait_ge(o_psum.sem, o_psum.at(b - 1))
                            dve.wait_ge(av_psum.sem, av_psum.at(2 * b + m + 1))
                            dve.tensor_copy(OT[j][:, m, :], ps[6 + m][:, 0:S]).then_inc(ot_ready.sem, 1)
                    dve.wait_ge(o_psum.sem, o_psum.at(b + 1))
                    xb = X[:, bass.ds(b, 1), :]
                    dve.tensor_tensor(xb, xb, ps[6][0:S, 0:D].unsqueeze(1), ALU.add).then_inc(x_ready.sem, 1)

                queries(0)
                dve.wait_ge(zeroed.sem, heads_zeroed)
                if not soft:
                    dve.wait_ge(bias_added.sem, 1)
                batches(dve, run)

            @block.scalar
            def _(act):
                act.wait_ge(core.loaded["heads16"], core.loads["heads16"])

                def keys(b):
                    for m in range(KD):
                        if soft:
                            act.wait_ge(k_psum.sem, k_psum.at(2 * b + m + 1))
                        if m == 0:
                            act.wait_ge(s_psum.sem, s_psum.at((NH if soft else 12) * b))
                        if soft:
                            ins = act.activation(Kt[:, m, :], ps[2 + m][:, 0:KVP], ACT.Copy)
                        else:
                            ins = act.activation(Kt[:, m, :].unsqueeze(1),
                                                 core.K_all[:, bass.ds(b, 1), m * KVP:(m + 1) * KVP], ACT.Copy)
                        ins.then_inc(k_ready.sem, 1)

                def run(b, j, i, more):
                    if soft:
                        for h in range(NH + LAG_T):
                            if h < NH:
                                act.wait_ge(max_ready.sem, max_ready.at(NH * b + h + 1))
                                act.wait_ge(at_psum.sem, at_psum.at(NH * b + h - 3))
                                act.activation(A[h % 4][:, 0:KV], ps[(8 + h) % 4][0:S, 0:KV], ACT.Exp,
                                               bias=neg_max[:, h % 4:h % 4 + 1],
                                               accum_out=total[:, h % 4:h % 4 + 1]).then_inc(exp_ready.sem, 1)
                            g = h - LAG_T
                            if 0 <= g < NH:
                                act.wait_ge(at_psum.sem, at_psum.at(NH * b + g + 1))
                                act.wait_ge(av_psum.sem, av_psum.at(NH * b + 2 * (g // 2) - 2))
                                act.activation(AT[g // 2 % 2][:, :, g % 2, :],
                                               ps[4 + g % 2][0:KT, 0:NKT * S].rearrange("p (t s) -> p t s", t=NKT),
                                               ACT.Copy).then_inc(at_ready.sem, 1)
                            if more and h == NH + 1:
                                keys(b + 1)
                    else:
                        act.wait_ge(av_psum.sem, av_psum.at(2 * b))
                        for u in range(12):
                            m, t, half = u // 6, u // 2 % 3, u % 2
                            rows = KT if t < NKT - 1 else KV - (NKT - 1) * KT
                            act.wait_ge(s_psum.sem, s_psum.at(12 * b + u + 1))
                            h0 = NHT * m + 4 * half
                            act.activation(AS[0:rows, t, h0:h0 + 4, :],
                                           ps[u % 4][0:rows, 0:4 * S].rearrange("p (h s) -> p h s", h=4), ACT.Sigmoid,
                                           scale=0.25).then_inc(exp_ready.sem, 1)
                        if more:
                            keys(b + 1)

                keys(0)
                batches(act, run)


def head16_softmax(core, io):
    heads16(core, io, 2)


def head16_sigmoid(core, io):
    heads16(core, io, 3)


def tiles(eng, n, body):
    body(0, 0, 0, True, n == 1)
    turns = (n - 2) // 2
    with eng.Fori(0, turns) as i:
        body(2 * i + 1, 1, i, False, False)
        body(2 * i + 2, 0, i + 1, False, False)
    for t in range(2 * turns + 1, n):
        body(t, t % 2, t // 2, False, t == n - 1)


def tile_count(E, top):
    return (top * T + E * (TS - 1)) // TS


def tile_of(slots, t):
    return slots.rearrange("(t c s) d -> t s c d", c=TS // S, s=S)[bass.ds(t, 1)]


def routed_ffn(core, io, E, top, router, gu_name, down_name, slots_in, slots_out, soft):
    X, N, NT, ps = core.X, core.N, core.NT, core.ps
    TN = tile_count(E, top)
    PER = T // TS
    LAG = 2
    CH = TS // S
    with Stage(core) as st:
        Wr = core.weights[router]
        L, CW, masked = st.sb("L", [S, NB, E]), st.sb("CW", [S, NB, E]), st.sb("masked", [S, NB, E])
        small = st.sb("small", [S, 3, NB])
        above, same = st.sb("above", [S, NB, E, E]), st.sb("same", [S, NB, E, E])
        rank = st.sb("rank", [S, NB, E])
        upto = [st.sb(f"upto{k}", [S, NB, E], BF16) for k in range(top)]
        batch_picks = st.sb("batch_picks", [S, E])
        per_expert, first = st.sb("per_expert", [S, E]), st.sb("first", [S, E])
        full, more_than = st.sb("full", [S, PER]), st.sb("more_than", [S, E, PER])
        earlier, later = st.sb("earlier", [S, E, E]), st.sb("later", [S, MAX_TILES, E])
        slot_f = st.sb("slot_f", [S, top, NB])
        slot = st.sb("slot", [S, top, NB], I32)
        weight = st.sb("weight", [S, top, NB])
        expert_f, expert = st.sb("expert_f", [S, MAX_TILES]), st.sb("expert", [S, MAX_TILES], I32)
        gu = [st.sb(f"gu{j}", [P, 2, KD, IP]) for j in range(2)]
        wd = [st.sb(f"wd{j}", [HU, NI, D]) for j in range(2)]
        rows_in = [st.sb(f"rows_in{j}", [S, CH, D]) for j in range(2)]
        XT = [st.sb(f"XT{j}", [P, KD, TS]) for j in range(2)]
        G = [st.sb(f"G{j}", [HU, TS]) for j in range(2)]
        Hh = [st.sb(f"Hh{j}", [HU, TS]) for j in range(4)]
        YT = st.sb("YT", [P, KD, TS])
        Y = [st.sb(f"Y{j}", [S, CH, D]) for j in range(2)]
        picked = st.sb("picked", [S, top * NB, D])
        own = st.event()
        gu_loaded, wd_loaded, rows_loaded = ([st.event(), st.event()] for _ in range(3))
        l_psum, e_in, e_ready, picks_ready, place_psum, slot_ready, expert_ready = (st.event() for _ in range(7))
        y_free = st.event(2)
        scattered, stored, gathered = soft[0], soft[1], soft[2:]
        xt_psum, xt_ready, gate_psum, up_psum, g_ready, h_ready, down_done = \
            st.event(2), st.event(1), st.event(4 * NI), st.event(4 * NI), st.event(2), st.event(2), st.event(4 * NI)
        yt_ready, y_psum, y_ready, x_ready = st.event(2), st.event(1), st.event(1), st.event()
        with st.block() as block:
            @block.sync
            def _(sp):
                st.heads(sp)
                sp.wait_ge(expert_ready.sem, 1)

                def load(t, j, i, first, last):
                    e = sp.value_load(expert[0:1, bass.ds(t, 1)], min_val=0, max_val=E - 1)
                    sp.wait_ge(up_psum.sem, up_psum.at(NI * (t - 1)))
                    sp.dma_start(gu[j][:, :, :, :], io[gu_name][bass.ds(e, 1)]).then_inc(gu_loaded[j].sem, 16)
                    sp.wait_ge(scattered.sem, 16 * NB * top)
                    sp.wait_ge(xt_psum.sem, xt_psum.at(t - 1))
                    sp.dma_start(rows_in[j][:, :, :], tile_of(slots_in, t)).then_inc(rows_loaded[j].sem, 16)
                    sp.wait_ge(down_done.sem, down_done.at(NI * (t - 1)))
                    sp.dma_start(wd[j][:, :, :], io[down_name][bass.ds(e, 1)]).then_inc(wd_loaded[j].sem, 16)
                tiles(sp, TN, load)

            @block.gpsimd
            def _(pool):
                pool.wait_ge(slot_ready.sem, 1)
                for k in range(top):
                    for b in range(NB):
                        pool.indirect_dma_start(slots_in[:, :], bass.IndirectOffsetOnAxis(ap=slot[:, k, b:b + 1], axis=0),
                                                N[:, b, :], None).then_inc(scattered.sem, 16)

                def store(t, j, i, first, last):
                    pool.wait_ge(y_ready.sem, y_ready.at(t + 1))
                    pool.dma_start(tile_of(slots_out, t), Y[j][:, :, :]).then_inc(stored.sem, 16)
                    pool.wait_ge(stored.sem, 16 * (t + 1))
                    pool.sem_inc(y_free.sem, 1)
                tiles(pool, TN, store)
                for b in range(NB):
                    for k in range(top):
                        pool.indirect_dma_start(picked[:, k * NB + b, :], None, slots_out[:, :],
                                                bass.IndirectOffsetOnAxis(ap=slot[:, k, b:b + 1], axis=0)
                                                ).then_inc(gathered[b // 2].sem, 16)

            @block.tensor
            def _(pe):
                pe.wait_ge(core.loaded["routers"], core.loads["routers"])
                for b in range(NB):
                    for k in range(KD):
                        ins = pe.matmul(ps[0][0:S, 16 * b:16 * b + E], NT[:, k, b * S:(b + 1) * S], Wr[:, k, :],
                                        start=k == 0, stop=k == KD - 1)
                ins.then_inc(l_psum.sem, 1)
                pe.wait_ge(picks_ready.sem, 1)
                picks = upto[top - 1]
                pe.matmul(ps[1][0:S, 0:NB * E], core.before[:, :], picks[:, :, :], start=True, stop=False,
                          skip_group_check=True)
                for b in range(NB - 1):
                    left = NB - 1 - b
                    ins = pe.matmul(ps[1][0:S, (b + 1) * E:NB * E], core.ones_b[:, :],
                                    picks[:, b:b + 1, :].broadcast_to([S, left, E]), start=False, stop=b == NB - 2,
                                    skip_group_check=True)
                pe.wait_ge(picks_ready.sem, 2)
                pe.matmul(ps[2][0:S, 0:E], core.ones[0:S, 0:S], batch_picks[:, :], start=True,
                          stop=True).then_inc(place_psum.sem, 1)

                def turn(t, j, i):
                    pe.wait_ge(rows_loaded[j].sem, 16 * (i + 1))
                    pe.wait_ge(xt_ready.sem, xt_ready.at(t))
                    for c in range(CH):
                        for k in range(KD):
                            ins = pe.transpose(ps[6][:, k * TS + c * S:k * TS + (c + 1) * S],
                                               rows_in[j][:, c, k * P:(k + 1) * P], core.ident[0:S, 0:S])
                    ins.then_inc(xt_psum.sem, 1)

                def turn_back(t):
                    pe.wait_ge(yt_ready.sem, yt_ready.at(KD * (t + 1)))
                    pe.wait_ge(y_ready.sem, y_ready.at(t))
                    for c in range(CH):
                        for m in range(KD):
                            ins = pe.transpose(ps[7][0:S, c * D + m * P:c * D + (m + 1) * P],
                                               YT[:, m, c * S:(c + 1) * S], core.ident[:, :])
                    ins.then_inc(y_psum.sem, 1)
                turn(0, 0, 0)

                def run(t, j, i, first, last):
                    pe.wait_ge(xt_ready.sem, xt_ready.at(t + 1))
                    pe.wait_ge(gu_loaded[j].sem, 16 * (i + 1))
                    for u in range(NI + LAG):
                        n = NI * t + u
                        if u < NI:
                            units = slice(u * HU, (u + 1) * HU)
                            pe.wait_ge(g_ready.sem, g_ready.at(n - 1))
                            for k in range(KD):
                                ins = pe.matmul(ps[2 * (u % 2)][0:HU, 0:TS], gu[j][:, 0, k, units], XT[j][:, k, :],
                                                start=k == 0, stop=k == KD - 1)
                            ins.then_inc(gate_psum.sem, 1)
                            pe.wait_ge(h_ready.sem, h_ready.at(n - 1))
                            for k in range(KD):
                                ins = pe.matmul(ps[2 * (u % 2) + 1][0:HU, 0:TS], gu[j][:, 1, k, units], XT[j][:, k, :],
                                                start=k == 0, stop=k == KD - 1)
                            ins.then_inc(up_psum.sem, 1)
                        if u == 1 and not first:
                            turn_back(t - 1)
                        if u == NI and not last:
                            turn(t + 1, 1 - j, i + j)
                        g = u - LAG
                        if g >= 0:
                            pe.wait_ge(h_ready.sem, h_ready.at(NI * t + g + 1))
                            if g == 0:
                                pe.wait_ge(wd_loaded[j].sem, 16 * (i + 1))
                                pe.wait_ge(yt_ready.sem, yt_ready.at(KD * t))
                            for m in range(KD):
                                ins = pe.matmul(ps[4 + m][:, 0:TS], wd[j][:, g, m * P:(m + 1) * P], Hh[g % 4][:, :],
                                                start=g == 0, stop=g == NI - 1)
                            ins.then_inc(down_done.sem, 1)
                tiles(pe, TN, run)
                turn_back(TN - 1)

            @block.vector
            def _(dve):
                chain = Chain(dve, own)
                dve.wait_ge(l_psum.sem, 1)
                logits = ps[0][0:S, 0:16 * NB].rearrange("s (b e) -> s b e", e=16)[:, :, 0:E]
                chain.step(dve.tensor_copy(L[:, :, :], logits))
                if top == 2:
                    chain.step(dve.tensor_reduce(small[:, 0, :], L[:, :, :], AX.X, ALU.max))
                    dve.tensor_tensor(L[:, :, :], L[:, :, :], wide(small[:, 0, :], E), ALU.subtract).then_inc(e_in.sem, 1)
                    dve.wait_ge(e_ready.sem, 1)
                    chain.step(dve.tensor_reduce(small[:, 1, :], CW[:, :, :], AX.X, ALU.add))
                    chain.step(dve.reciprocal(small[:, 2, :], small[:, 1, :]))
                    chain.step(dve.tensor_tensor(L[:, :, :], CW[:, :, :], wide(small[:, 2, :], E), ALU.mult))
                top_mask(dve, chain, L[:, :, :], NB, E, range(1, top + 1), above[:, :, :, :], same[:, :, :, :],
                         rank[:, :, :], [m[:, :, :] for m in upto], core.below[:, 0:E, 0:E])
                picks = upto[top - 1]
                dve.tensor_scalar(full[:, :], core.counts[:, 0:PER], float(TS), None, ALU.mult).then_inc(picks_ready.sem, 1)
                dve.tensor_reduce(batch_picks[:, :], picks[:, :, :].rearrange("s b e -> s e b"), AX.X,
                                  ALU.add).then_inc(picks_ready.sem, 1)
                if top == 2:
                    chain.step(dve.tensor_tensor(CW[:, :, :], L[:, :, :], picks[:, :, :], ALU.mult))
                    chain.step(dve.tensor_reduce(small[:, 1, :], CW[:, :, :], AX.X, ALU.add))
                    chain.step(dve.reciprocal(small[:, 2, :], small[:, 1, :]))
                    chain.step(dve.tensor_tensor(CW[:, :, :], CW[:, :, :], wide(small[:, 2, :], E), ALU.mult))
                dve.wait_ge(place_psum.sem, 1)
                dve.wait_ge(picks_ready.sem, 1)
                chain.step(dve.tensor_tensor(more_than[:, :, :], wide(ps[2][0:S, 0:E], PER), pair(full[:, :], E), ALU.is_gt))
                chain.step(dve.tensor_reduce(per_expert[:, :], more_than[:, :, :], AX.X, ALU.add))
                chain.step(dve.tensor_tensor(earlier[:, :, :], pair(per_expert[:, :], E), core.below[:, 0:E, 0:E], ALU.mult))
                chain.step(dve.tensor_reduce(first[:, :], earlier[:, :, :], AX.X, ALU.add))
                chain.step(dve.tensor_tensor(later[:, 0:TN, 0:E - 1], wide(core.counts[:, 0:TN], E - 1),
                                             pair(first[:, 1:E], TN), ALU.is_ge))
                chain.step(dve.tensor_reduce(expert_f[:, 0:TN], later[:, 0:TN, 0:E - 1], AX.X, ALU.add))
                dve.tensor_copy(expert[:, 0:TN], expert_f[:, 0:TN]).then_inc(expert_ready.sem, 1)
                chain.step(dve.scalar_tensor_tensor(L[:, :, :], pair(first[:, :], NB), float(TS),
                                                    ps[1][0:S, 0:NB * E].rearrange("s (b e) -> s b e", e=E), ALU.mult,
                                                    ALU.add))
                if top == 2:
                    chain.step(dve.tensor_tensor(upto[1][:, :, :], upto[1][:, :, :], upto[0][:, :, :], ALU.subtract))
                for k in range(top):
                    chain.step(dve.tensor_tensor(masked[:, :, :], L[:, :, :], upto[k][:, :, :], ALU.mult))
                    chain.step(dve.tensor_reduce(slot_f[:, k, :], masked[:, :, :], AX.X, ALU.add))
                dve.tensor_copy(slot[:, :, :], slot_f[:, :, :]).then_inc(slot_ready.sem, 1)
                if top == 2:
                    for k in range(top):
                        chain.step(dve.tensor_tensor(masked[:, :, :], CW[:, :, :], upto[k][:, :, :], ALU.mult))
                        chain.step(dve.tensor_reduce(weight[:, k, :], masked[:, :, :], AX.X, ALU.add))

                def store(t, j):
                    dve.wait_ge(y_psum.sem, y_psum.at(t + 1))
                    dve.wait_ge(y_free.sem, y_free.at(t - 1))
                    dve.tensor_copy(Y[j][:, :, :], ps[7][0:S, 0:CH * D].rearrange("s (c d) -> s c d", c=CH)
                                    ).then_inc(y_ready.sem, 1)

                def run(t, j, i, first, last):
                    for u in range(NI):
                        n = NI * t + u
                        dve.wait_ge(g_ready.sem, g_ready.at(n + 1))
                        dve.wait_ge(up_psum.sem, up_psum.at(n + 1))
                        dve.wait_ge(down_done.sem, down_done.at(n - 3))
                        dve.tensor_tensor(Hh[u % 4][:, :], G[u % 2][:, :], ps[2 * (u % 2) + 1][0:HU, 0:TS],
                                          ALU.mult).then_inc(h_ready.sem, 1)
                        if u == 2 and not first:
                            store(t - 1, 1 - j)
                    dve.wait_ge(down_done.sem, down_done.at(NI * (t + 1)))
                    dve.wait_ge(y_psum.sem, y_psum.at(t))
                    for m in range(KD):
                        dve.tensor_copy(YT[:, m, :], ps[4 + m][:, 0:TS]).then_inc(yt_ready.sem, 1)
                tiles(dve, TN, run)
                store(TN - 1, (TN - 1) % 2)
                for b in range(NB):
                    dve.wait_ge(gathered[b // 2].sem, 16 * 2 * top)
                    for k in range(top):
                        if top == 2:
                            ins = dve.scalar_tensor_tensor(X[:, b, :], picked[:, k * NB + b, :], weight[:, k, b:b + 1],
                                                           X[:, b, :], ALU.mult, ALU.add)
                        else:
                            ins = dve.tensor_tensor(X[:, b, :], X[:, b, :], picked[:, b, :], ALU.add)
                        ins.then_inc(x_ready.sem, 1)
                        if k < top - 1:
                            dve.wait_ge(x_ready.sem, top * b + k + 1)

            @block.scalar
            def _(act):
                if top == 2:
                    act.wait_ge(e_in.sem, 1)
                    act.activation(CW[:, :, :], L[:, :, :], ACT.Exp).then_inc(e_ready.sem, 1)
                act.wait_ge(xt_psum.sem, xt_psum.at(1))
                act.activation(XT[0][:, :, :], ps[6][:, 0:KD * TS].rearrange("p (k s) -> p k s", k=KD),
                               ACT.Copy).then_inc(xt_ready.sem, 1)

                def run(t, j, i, first, last):
                    for u in range(NI):
                        n = NI * t + u
                        act.wait_ge(gate_psum.sem, gate_psum.at(n + 1))
                        act.wait_ge(h_ready.sem, h_ready.at(n - 1))
                        act.activation(G[u % 2][:, :], ps[2 * (u % 2)][0:HU, 0:TS], ACT.Silu).then_inc(g_ready.sem, 1)
                    if not last:
                        act.wait_ge(xt_psum.sem, xt_psum.at(t + 2))
                        act.wait_ge(up_psum.sem, up_psum.at(NI * t))
                        act.activation(XT[1 - j][:, :, :], ps[6][:, 0:KD * TS].rearrange("p (k s) -> p k s", k=KD),
                                       ACT.Copy).then_inc(xt_ready.sem, 1)
                tiles(act, TN, run)


def routed_ffn_2(core, io):
    routed_ffn(core, io, 9, 2, "Wr2", "gu2", "down2", core.slots_in[0], core.slots_out[0],
               core.soft_events[0])


def routed_ffn_3(core, io):
    routed_ffn(core, io, 8, 1, "Wr3", "gu3", "down3", core.slots_in[1], core.slots_out[1],
               core.soft_events[1])


ROWS = ["w1_sim", "b_qv", "bp", "L1_bo", "gamma", "beta", "L3_bv", "L3_bo"]
W1_SIM, B_QV, B_P, L1_BO, GAMMA, BETA, L3_BV, L3_BO = range(8)

WEIGHTS = {
    "sim": {"w_sim": [P, 2 * KD], "b_sim": [P, 1], "W_qv": [P, 8, D]},
    "gated": {"Vg": [P, KD, 512], "VgT": [P, 4, 512], "We": [P, KD, 8 * D], "Wp": [P, KD, D], "be": [8, D]},
    "head64": {"Wq": [P, KD, 1024], "Wk": [P, KD, 1024], "Wv": [P, KD, 1024], "Wo": [P, 8, D], "bq": [P, 8],
               "bk": [P, 8], "bv": [P, 8]},
    "ternary": {"w1": [P, KD, 1024], "w2": [P, 8, D], "conv_w": [P, 8, 3], "conv_b": [P, 8]},
    "routers": {"Wr2": [P, KD, 9], "Wr3": [P, KD, 8]},
    "heads16": {"W_heads": [P, P], "W_o": [P, KD, D], "L3_Wq": [P, KD, D], "L3_Wo": [P, KD, D], "L3_bq": [P, KD]},
    "context": {"L3_Wk": [P, KD, D], "L3_Wv": [P, KD, D], "L3_bk": [P, KD]},
}

EARLY = ("sim", "gated", "head64")


def program(nc, io, out):
    with ExitStack() as ctx:
        core = Core(nc, ctx)
        core.weights, core.loaded, core.loads = {}, {}, {}
        early = ExitStack()
        for stage, tensors in sorted(WEIGHTS.items(), key=lambda item: item[0] in EARLY):
            scope = early if stage in EARLY else ctx
            core.loaded[stage] = core.sem(f"loaded_{stage}")
            core.loads[stage] = 16 * len(tensors)
            for name, shape in tensors.items():
                core.weights[name] = scope.enter_context(nc.sbuf_tensor(name, shape, F32))

        def load(eng, stage, io):
            for name, shape in WEIGHTS[stage].items():
                eng.dma_start(core.weights[name][:], io[name]).then_inc(core.loaded[stage], 16)
        core.load = load
        core.slots_in, core.slots_out = ([nc.dram_tensor(f"slots_{way}{n}", (tile_count(*picks) * TS, D), F32,
                                                         kind="Internal").ap()
                                          for n, picks in enumerate(((9, 2), (8, 1)))] for way in ("in", "out"))
        stages = [sim_attention, gated_experts, head64_attention, ternary_ffn, head16_softmax, routed_ffn_2, head16_sigmoid, routed_ffn_3]
        setup(core, io)
        for stage in stages:
            layer_norm(core)
            stage(core, io)
            if stage is head64_attention:
                early.close()
                core.K_all = ctx.enter_context(nc.sbuf_tensor("K_all", [P, NB, KD * KVP], F32))
                core.V_all = ctx.enter_context(nc.sbuf_tensor("V_all", [KT, NB, NKT * D], F32))
        with Stage(core) as st:
            stored = st.event()
            with st.block() as block:
                @block.sync
                def _(sp):
                    sp.dma_start(out, core.X[:, :, :]).then_inc(stored.sem, 16)
                    for name, sem in core.loaded.items():
                        sp.wait_ge(sem, core.loads[name])
                    sp.wait_ge(stored.sem, 16)


def arrays_of(v, np):
    f = {k: np.asarray(a) for k, a in v.items()}
    a = {}

    def tiles(w):
        return w.reshape(-1, P, w.shape[1]).transpose(1, 0, 2)

    def cols(w):
        return w.reshape(-1, P).T

    a["x"] = f["x"].transpose(1, 0, 2)
    ctx = np.zeros((NB, KVP, D), np.float32)
    ctx[:, :KV] = f["ctx_1024"]
    a["ctT"] = ctx.transpose(0, 2, 1).reshape(NB, KD, P, KVP).transpose(0, 2, 1, 3)
    a["ctk"] = ctx.reshape(NB, NKT, KT, D).transpose(0, 2, 1, 3)
    a["mask"] = f["mask_Bx1xSxS2_ik1"][:, 0]
    a["head_mask"] = (np.arange(P)[:, None] // 16 == np.arange(8)[None, :]).astype(np.float32)
    a["below"] = (np.arange(9)[None, :] < np.arange(9)[:, None]).astype(np.float32)
    a["counts"] = np.arange(MAX_TILES, dtype=np.float32)
    w = f["L0_xattn_w_sim"]
    rows = np.zeros((len(ROWS), D), np.float32)
    for n, r in enumerate([w[:D], f["L0_xattn_b_qv"], f["L0_ffn_bp"], f["L1_xattn_bo"], f["L1_xattn_ln_gamma"],
                           f["L1_xattn_ln_beta"], f["L3_xattn_bv"], f["L3_xattn_bo"]]):
        rows[n] = r
    a["rows"] = rows
    a["w_sim"] = cols(w[D:])
    a["b_sim"] = np.broadcast_to(f["L0_xattn_b_sim"][None, :], (P, 1))
    a["W_qv"] = tiles(f["L0_xattn_W_qv"])
    vg = f["L0_ffn_Vg"]
    a["Vg"] = tiles(vg.transpose(1, 0, 2).reshape(D, 512))
    vgt = np.zeros((P, 4, 2, D), np.float32)
    for e in range(8):
        vgt[64 * (e % 2):64 * (e % 2) + 64, e // 2, e % 2] = vg[e].T
    a["VgT"] = vgt.reshape(P, 4, 512)
    a["We"] = tiles(f["L0_ffn_We"].transpose(2, 0, 1).reshape(D, 8 * D))
    a["Wp"] = tiles(f["L0_ffn_Wp"].T)
    a["be"] = f["L0_ffn_be"]
    for n in ("Wq", "Wk", "Wv", "Wo"):
        a[n] = tiles(f["L1_xattn_" + n])
    for n in ("bq", "bk", "bv"):
        a[n] = cols(f["L1_xattn_" + n])
    a["w1"] = tiles(f["L1_ffn_w1"].T)
    a["w2"] = tiles(f["L1_ffn_w2"].T)
    a["conv_w"] = f["L1_ffn_conv_w"][:, 0].reshape(8, P, 3).transpose(1, 0, 2)
    a["conv_b"] = cols(f["L1_ffn_conv_b"])
    blocks = np.zeros((P, P), np.float32)
    for n in range(8):
        blocks[16 * n:16 * n + 16, 16 * n:16 * n + 16] = f["L2_xattn_W_v"].T
    a["W_heads"] = blocks
    a["W_o"] = tiles(f["L2_xattn_W_o"].T)
    for n in ("Wq", "Wk", "Wv", "Wo"):
        a["L3_" + n] = tiles(f["L3_xattn_" + n])
    for n in ("bq", "bk"):
        a["L3_" + n] = cols(f["L3_xattn_" + n])
    a["Wr2"] = tiles(f["L2_ffn_Wr"])
    a["Wr3"] = tiles(f["L3_ffn_router_w"].T)

    def experts(gate, up, down):
        E, _, I = gate.shape
        gu = np.zeros((E, 2, D, IP), np.float32)
        gu[:, 0, :, :I], gu[:, 1, :, :I] = gate, up
        wd = np.zeros((E, IP, D), np.float32)
        wd[:, :I] = down
        return (gu.reshape(E, 2, KD, P, IP).transpose(0, 3, 1, 2, 4),
                wd.reshape(E, NI, HU, D).transpose(0, 2, 1, 3))

    a["gu2"], a["down2"] = experts(f["L2_ffn_Wg"], f["L2_ffn_Wu"], f["L2_ffn_Wd"])
    a["gu3"], a["down3"] = experts(f["L3_ffn_gate_w"].transpose(0, 2, 1), f["L3_ffn_up_w"].transpose(0, 2, 1),
                                   f["L3_ffn_down_w"].transpose(0, 2, 1))
    return {k: np.ascontiguousarray(x) for k, x in a.items()}


def kernel(**inputs):
    import numpy as np
    import concourse.bacc as bacc
    from concourse.bass_utils import run_bass_kernel_spmd

    nc = bacc.Bacc("TRN2", target_bir_lowering=False, num_devices=1)
    arrays = arrays_of(inputs, np)
    io = {k: nc.dram_tensor(f"in_{k}", a.shape, mybir.dt.from_np(a.dtype), kind="ExternalInput").ap()
          for k, a in arrays.items()}
    out = nc.dram_tensor("out_x", (S, NB, D), F32, kind="ExternalOutput").ap()
    program(nc, io, out)
    got = run_bass_kernel_spmd(nc, [{f"in_{k}": a for k, a in arrays.items()}], core_ids=[0])
    return np.ascontiguousarray(got.results[0]["out_x"].transpose(1, 0, 2))
```
